# Optimizing a Trainium2 kernel written in Bass

```python
import numpy as np
import jax
import jax.numpy as jnp

def _softmax(x, axis=-1):
    return jax.nn.softmax(x, axis=axis)

def _gelu(x):
    return jax.nn.gelu(x, approximate=True)

def _silu(x):
    return jax.nn.silu(x)

def _sigmoid(x):
    return jax.nn.sigmoid(x)

def _layernorm(x, axis=-1, eps=1e-05):
    m = jnp.mean(x, axis=axis, keepdims=True)
    v = jnp.var(x, axis=axis, keepdims=True)
    return (x - m) / jnp.sqrt(v + eps)

def _scatter_add(tgt, idx, src, axis=0):
    return tgt.at[idx].add(src)

def _segment_sum(src, seg, n):
    return jax.ops.segment_sum(src, seg, n)
kernel_name = 'mk_vit_tower_d1_tok_img512_r4_2026e4'

def setup_inputs(seed: int=0):
    np.random.seed(seed)
    _w = jnp.asarray

    def _rec_inputs():
        import jax
        import jax.numpy as jnp
        _rk = jax.random.key(seed)
        x = -0.000356955 + 1 * jax.random.normal(jax.random.fold_in(_rk, 1), (64, 3, 224, 224), jnp.float32)
        return x
    x = _rec_inputs()

    def _L0_tok_setup():
        import jax, jax.numpy as jnp
        import numpy as np
        key = jax.random.key(seed)
        k1, k2, k3 = jax.random.split(key, 3)
        B, C, H, W = (128, 3, 224, 224)
        E, p = (128, 16)
        K = C * p * p
        img = jax.random.normal(k1, (B, C, H, W), dtype=jnp.float32)
        w = jax.random.normal(k2, (E, K), dtype=jnp.float32) * (1.0 / np.sqrt(K))
        b = jax.random.normal(k3, (E,), dtype=jnp.float32)
        return {'img': img, 'w': w, 'b': b, 'patch_size': p}
    _L0_tok_all = _L0_tok_setup()
    _L0_tok_in = {k: v for k, v in _L0_tok_all.items() if k in ('w', 'b')}
    del _L0_tok_all

    def _L0_attn_setup():
        import jax, jax.numpy as jnp
        import numpy as np
        B, N, D, H, E = (4, 512, 128, 8, 8192)
        HD = D // H

        def _edge_col_bias(edge_index, edge_attr, eb_w, eb_b, n):
            eb = edge_attr @ eb_w.T + eb_b
            src, tgt = (edge_index[0], edge_index[1])
            valid = (src >= 0) & (src < n) & (tgt >= 0) & (tgt < n)
            order = jnp.where(valid, jnp.arange(edge_index.shape[1]), -1)
            tgt_safe = jnp.where(valid, tgt, 0)
            last = jnp.full((n,), -1, dtype=order.dtype).at[tgt_safe].max(order)
            hit = last >= 0
            gathered = eb[jnp.maximum(last, 0)]
            col_bias = jnp.where(hit[:, None], gathered, 0.0)
            return col_bias
        key = jax.random.key(seed)
        ks = jax.random.split(key, 12)
        s = 0.02
        inp = {'x': jax.random.normal(ks[0], (B, N, D), dtype=jnp.float32), 'edge_index': jax.random.randint(ks[1], (2, E), 0, N, dtype=jnp.int64), 'edge_attr': jax.random.normal(ks[2], (E, 3), dtype=jnp.float32), 'q_w': jax.random.normal(ks[3], (D, D), dtype=jnp.float32) * s, 'q_b': jnp.zeros((D,), jnp.float32), 'k_w': jax.random.normal(ks[4], (D, D), dtype=jnp.float32) * s, 'k_b': jnp.zeros((D,), jnp.float32), 'v_w': jax.random.normal(ks[5], (D, D), dtype=jnp.float32) * s, 'v_b': jnp.zeros((D,), jnp.float32), 'o_w': jax.random.normal(ks[6], (D, D), dtype=jnp.float32) * s, 'o_b': jnp.zeros((D,), jnp.float32), 'eb_w': jax.random.normal(ks[7], (H, 3), dtype=jnp.float32) * s, 'eb_b': jnp.zeros((H,), jnp.float32)}
        return inp
    _L0_attn_all = _L0_attn_setup()
    _L0_attn_in = {k: v for k, v in _L0_attn_all.items() if k in ('edge_index', 'edge_attr', 'q_w', 'q_b', 'k_w', 'k_b', 'v_w', 'v_b', 'o_w', 'o_b', 'eb_w', 'eb_b')}
    del _L0_attn_all

    def _L0_ffn_setup():
        import jax, jax.numpy as jnp
        import numpy as np
        E = 8
        TOP_K = 2
        D = 128
        H = 256
        B, S = (16, 1024)
        key = jax.random.key(seed)
        ks = jax.random.split(key, 10)
        sd = lambda fan_in: 1.0 / np.sqrt(fan_in)
        x = jax.random.normal(ks[0], (B, S, D), dtype=jnp.float32)
        gw1 = jax.random.uniform(ks[1], (D, D // 2), jnp.float32, -sd(D), sd(D))
        gb1 = jnp.zeros((D // 2,), jnp.float32)
        gw2 = jax.random.uniform(ks[2], (D // 2, E), jnp.float32, -sd(D // 2), sd(D // 2))
        gb2 = jnp.zeros((E,), jnp.float32)
        we1 = jax.random.uniform(ks[3], (E, D, H), jnp.float32, -sd(D), sd(D))
        be1 = jnp.zeros((E, H), jnp.float32)
        we2 = jax.random.uniform(ks[4], (E, H, D), jnp.float32, -sd(H), sd(H))
        be2 = jnp.zeros((E, D), jnp.float32)
        return {'x': x, 'gw1': gw1, 'gb1': gb1, 'gw2': gw2, 'gb2': gb2, 'we1': we1, 'be1': be1, 'we2': we2, 'be2': be2}
    _L0_ffn_all = _L0_ffn_setup()
    _L0_ffn_in = {k: v for k, v in _L0_ffn_all.items() if k in ('gw1', 'gb1', 'gw2', 'gb2', 'we1', 'be1', 'we2', 'be2')}
    del _L0_ffn_all
    return {'x': x, 'L0_tok_w': _L0_tok_in['w'], 'L0_tok_b': _L0_tok_in['b'], 'L0_attn_edge_index': _L0_attn_in['edge_index'], 'L0_attn_edge_attr': _L0_attn_in['edge_attr'], 'L0_attn_q_w': _L0_attn_in['q_w'], 'L0_attn_q_b': _L0_attn_in['q_b'], 'L0_attn_k_w': _L0_attn_in['k_w'], 'L0_attn_k_b': _L0_attn_in['k_b'], 'L0_attn_v_w': _L0_attn_in['v_w'], 'L0_attn_v_b': _L0_attn_in['v_b'], 'L0_attn_o_w': _L0_attn_in['o_w'], 'L0_attn_o_b': _L0_attn_in['o_b'], 'L0_attn_eb_w': _L0_attn_in['eb_w'], 'L0_attn_eb_b': _L0_attn_in['eb_b'], 'L0_ffn_gw1': _L0_ffn_in['gw1'], 'L0_ffn_gb1': _L0_ffn_in['gb1'], 'L0_ffn_gw2': _L0_ffn_in['gw2'], 'L0_ffn_gb2': _L0_ffn_in['gb2'], 'L0_ffn_we1': _L0_ffn_in['we1'], 'L0_ffn_be1': _L0_ffn_in['be1'], 'L0_ffn_we2': _L0_ffn_in['we2'], 'L0_ffn_be2': _L0_ffn_in['be2']}

def reference(x, L0_tok_w, L0_tok_b, L0_attn_edge_index, L0_attn_edge_attr, L0_attn_q_w, L0_attn_q_b, L0_attn_k_w, L0_attn_k_b, L0_attn_v_w, L0_attn_v_b, L0_attn_o_w, L0_attn_o_b, L0_attn_eb_w, L0_attn_eb_b, L0_ffn_gw1, L0_ffn_gb1, L0_ffn_gw2, L0_ffn_gb2, L0_ffn_we1, L0_ffn_be1, L0_ffn_we2, L0_ffn_be2):
    import jax
    import jax.numpy as jnp

    def _L0_tok_ref(img, w, b, patch_size):
        import jax, jax.numpy as jnp
        import numpy as np
        B, C, H, W = img.shape
        p = patch_size
        Hp, Wp = (H // p, W // p)
        S = Hp * Wp
        patches = img.reshape(B, C, Hp, p, Wp, p)
        patches = patches.transpose(0, 2, 4, 1, 3, 5).reshape(B, S, C * p * p)
        out = jnp.einsum('bsk,ek->bse', patches, w) + b
        return out

    def _L0_attn_ref(x, edge_index, edge_attr, q_w, q_b, k_w, k_b, v_w, v_b, o_w, o_b, eb_w, eb_b):
        import jax, jax.numpy as jnp
        import numpy as np
        B, N, D, H, E = (4, 512, 128, 8, 8192)
        HD = D // H

        def _edge_col_bias(edge_index, edge_attr, eb_w, eb_b, n):
            eb = edge_attr @ eb_w.T + eb_b
            src, tgt = (edge_index[0], edge_index[1])
            valid = (src >= 0) & (src < n) & (tgt >= 0) & (tgt < n)
            order = jnp.where(valid, jnp.arange(edge_index.shape[1]), -1)
            tgt_safe = jnp.where(valid, tgt, 0)
            last = jnp.full((n,), -1, dtype=order.dtype).at[tgt_safe].max(order)
            hit = last >= 0
            gathered = eb[jnp.maximum(last, 0)]
            col_bias = jnp.where(hit[:, None], gathered, 0.0)
            return col_bias
        b, n, d = x.shape
        q = (x @ q_w.T + q_b).reshape(b, n, H, HD)
        k = (x @ k_w.T + k_b).reshape(b, n, H, HD)
        v = (x @ v_w.T + v_b).reshape(b, n, H, HD)
        scores = jnp.einsum('bnhd,bmhd->bhnm', q, k) / jnp.sqrt(jnp.float32(HD))
        col_bias = _edge_col_bias(edge_index, edge_attr, eb_w, eb_b, n)
        scores = scores + col_bias.T[None, :, None, :]
        attn = jax.nn.softmax(scores, axis=-1)
        out = jnp.einsum('bhnm,bmhd->bnhd', attn, v).reshape(b, n, d)
        return out @ o_w.T + o_b

    def _L0_ffn_ref(x, gw1, gb1, gw2, gb2, we1, be1, we2, be2):
        import jax, jax.numpy as jnp
        import numpy as np
        E = 8
        TOP_K = 2
        D = 128
        H = 256
        B, S = (16, 1024)
        b, s, d = x.shape
        xf = x.reshape(-1, d)
        T = xf.shape[0]
        gate_logits = jax.nn.relu(xf @ gw1 + gb1) @ gw2 + gb2
        gate_weights = jax.nn.softmax(gate_logits, axis=-1)
        top_w, top_idx = jax.lax.top_k(gate_weights, TOP_K)
        top_w = jax.nn.softmax(top_w, axis=-1)
        combine = jnp.zeros((T, E), dtype=xf.dtype)
        combine = combine.at[jnp.arange(T)[:, None], top_idx].add(top_w)
        out = jnp.zeros_like(xf)
        for e in range(E):
            h = jax.nn.gelu(xf @ we1[e] + be1[e], approximate=False)
            y = h @ we2[e] + be2[e]
            out = out + combine[:, e:e + 1] * y
        return out.reshape(b, s, d)
    h = _L0_tok_ref(x, L0_tok_w, L0_tok_b, 16)
    h = h + _L0_attn_ref(_layernorm(h, axis=-1), L0_attn_edge_index, L0_attn_edge_attr, L0_attn_q_w, L0_attn_q_b, L0_attn_k_w, L0_attn_k_b, L0_attn_v_w, L0_attn_v_b, L0_attn_o_w, L0_attn_o_b, L0_attn_eb_w, L0_attn_eb_b)
    h = h + _L0_ffn_ref(_layernorm(h, axis=-1), L0_ffn_gw1, L0_ffn_gb1, L0_ffn_gw2, L0_ffn_gb2, L0_ffn_we1, L0_ffn_be1, L0_ffn_we2, L0_ffn_be2)
    return h

_drawn_inputs = setup_inputs


def setup_inputs(seed=0):
    import zlib

    import numpy as np

    out = dict(_drawn_inputs(seed))
    spreads = {'L0_attn_q_b': (0.0, 2.0),
     'L0_attn_k_b': (0.0, 2.0),
     'L0_attn_v_b': (0.0, 0.375),
     'L0_attn_o_b': (0.0, 0.1),
     'L0_attn_eb_b': (0.0, 2.0),
     'L0_ffn_gb1': (0.0, 0.1),
     'L0_ffn_gb2': (0.0, 0.1),
     'L0_ffn_be1': (0.0, 0.467),
     'L0_ffn_be2': (0.0, 0.1)}
    factors = {'L0_attn_edge_attr': 25.835,
     'L0_attn_q_w': 23.983,
     'L0_attn_k_w': 22.424,
     'L0_attn_eb_w': 31.931}
    for name, (base, spread) in spreads.items():
        noise = np.random.default_rng([zlib.crc32(name.encode()), seed]).standard_normal(out[name].shape)
        drawn = base * np.exp(spread * noise) if base else spread * noise
        out[name] = jnp.asarray(drawn.astype(out[name].dtype))
    for name, factor in factors.items():
        out[name] = (out[name] * factor).astype(out[name].dtype)
    return out
```

```python
from contextlib import ExitStack

import concourse.bass as bass
from concourse import mybir

ALU = mybir.AluOpType
ACT = mybir.ActivationFunctionType
F32 = mybir.dt.float32
F32R = mybir.dt.float32r
BF16 = mybir.dt.bfloat16
U32 = mybir.dt.uint32
I32 = mybir.dt.int32
AX_X = mybir.AxisListType.X

P = 128
PATCH = 16
N = 196
HALF = N // 2
D = 128
H = 8
HD = D // H
NE = 8
HID = 256
EPS = 1e-5
RING = 3
FRONT = 9
LAST_LAG = 5
CH = 256
XW = 132
BR = 6
OG = 8
JUNK_ROW = float(1 << 20)
ROW_BIAS, ROW_MAX, ROW_END = 4 * HD, 4 * HD + 2, 4 * HD + 4
ROWS, PROJ, SMALL, S1A, S2, PVA = 0, 1, 2, 3, 5, 6
HBANKS, YBANKS = (3, 4, 5), (6, 7, 1)


class Image:

    def __init__(self, slot, it, lag, count):
        c = slot - lag
        self.ring = c % RING
        self.turn = it + c // RING
        self.n = RING * it + c
        self.live = not isinstance(self.n, int) or 0 <= self.n < count


def wait(eng, sem, value):
    if not isinstance(value, int) or value > 0:
        eng.wait_ge(sem, value)


def vit_block(nc, x, wtok, wqkv, wo, gw1, gw2, wexp, be2, cols, rows, edges, attr, ebw, consts, tri,
              tokens, out):
    NB = x.shape[0]
    NK = x.shape[2]
    NT = NB * N
    TILES = 2 * NB
    REGION = NT + CH
    NCH = -(-((2 * NT + NE * (CH - 1)) // CH) // 3) * 3
    TURNS = (NB - 1 - FRONT) // RING
    EJ = edges.shape[2]
    assert (NB - 1 - FRONT) % RING == 0 and TILES % (2 * OG) == 0

    with ExitStack() as ctx:
        def sb(name, shape, dt=F32):
            return ctx.enter_context(nc.sbuf_tensor(name, shape, dt))

        def sem(name):
            return ctx.enter_context(nc.semaphore(name))

        ps = ctx.enter_context(nc.psum_tensor("ps", [P, 8, 512], F32))

        parts_dram = nc.dram_tensor("parts_dram", (RING, 2, 2, P, N), F32, kind="Internal").ap()
        xsort = nc.dram_tensor("xsort", (NE * REGION + CH, XW), F32, kind="Internal").ap()
        ysort = nc.dram_tensor("ysort", (2 * NT, D), F32, kind="Internal").ap()

        wtok_s = sb("wtok_s", [P, NK, D])
        wqkv_s = sb("wqkv_s", [P, 3, D])
        wo_s = sb("wo_s", [P, D])
        gw1_s = sb("gw1_s", [P, D])
        gw2_s = sb("gw2_s", [P, NE])
        cols_s = sb("cols_s", [P, 4])
        vb_s = sb("vb_s", [HALF, 2, D])
        gb2_s = sb("gb2_s", [HALF, 2, NE])
        ob_s = sb("ob_s", [HALF, 2, D])
        power = sb("power", [HALF, 2])
        ebw_s = sb("ebw_s", [HALF, 4, H])
        ident = sb("ident", [P, P])
        expert_no = sb("expert_no", [HALF, NE])
        region_row = sb("region_row", [HALF, NE])
        lower = sb("lower", [HALF, 2, HALF], BF16)

        WW = 2 * HID + 2
        room1 = sb("room1", [P, BR * WW])
        edge_i = room1[:, 0:2 * EJ].bitcast(I32).rearrange("p (a j) -> p a j", a=2)
        edge_f = room1[:, 2 * EJ:4 * EJ].rearrange("p (a j) -> p a j", a=2)
        edge_ok = room1[:, 4 * EJ:8 * EJ].rearrange("p (a j) -> p a j", a=4)
        edge_key = room1[:, 8 * EJ:9 * EJ]
        tok_no = sb("tok_no", [P, N + 1])
        tok_no16 = sb("tok_no16", [P, N], BF16)
        edge_hit = sb("edge_hit", [P, 2, N], BF16)
        edge_last16 = sb("edge_last16", [P, 2, N], BF16)
        edge_last = sb("edge_last", [P, N])
        last = sb("last", [HALF, 3, 2])
        last_i = sb("last_i", [HALF, 2], U32)
        attr_s = sb("attr_s", [HALF, 2, 4])
        eb = sb("eb", [HALF, 2, H])
        bias_part = sb("bias_part", [H, 2, N], F32R)

        tokens_s = sb("tokens_s", [HALF, 4 * RING], U32)

        patches = sb("patches", [P, RING, NK, N])
        hcols = sb("hcols", [P, N])
        h_all = sb("h_all", [HALF, TILES, D])
        stats = sb("stats", [HALF, 2, 6])
        mv = sb("mv", [HALF, 2, 2])
        var = sb("var", [HALF, 2])
        rstd = sb("rstd", [HALF, 2])
        xn = sb("xn", [HALF, 2, D])
        sizes = [RING * N, RING * 2 * H * 2 * HD, 4 * 2 * N, 2 * N]
        o = [sum(sizes[:i]) for i in range(5)]
        room2 = sb("room2", [P, max(o[4], 4 * OG * D)])
        xncols = room2[:, o[0]:o[1]].rearrange("p (r n) -> p r n", r=RING)
        vaug = room2[0:HALF, o[1]:o[2]].rearrange("p (r c h f) -> p r c h f", r=RING, c=2, h=H)
        probs = room2[0:HALF, o[2]:o[3]].rearrange("p (r c n) -> p r c n", r=4, c=2)
        sums = room2[:, o[3]:o[4]].rearrange("p (g n) -> p g n", g=2)
        parts = sb("parts", [P, RING, 2, 2, N], F32R)
        qside = sb("qside", [P, RING, H, N], F32R)
        kside = sb("kside", [P, RING, H, N], F32R)
        rowmax = sb("rowmax", [HALF, RING, 2 * H])
        negmax = sb("negmax", [2 * H, RING, 2, HALF], F32R)
        rden = sb("rden", [HALF, 2, H])
        att = sb("att", [HALF, 2, H, HD])
        att_cols = sb("att_cols", [P, N])
        stats2 = sb("stats2", [HALF, 2, 6])
        mv2 = sb("mv2", [HALF, 2, 2])
        var2 = sb("var2", [HALF, 2])
        rstd2 = sb("rstd2", [HALF, 2])
        xs = sb("xs", [HALF, RING, 2, 2, XW])
        xs_cols = sb("xs_cols", [P, N])
        gate_h = sb("gate_h", [P, N])
        logits = sb("logits", [HALF, RING, 2, NE])
        top = sb("top", [HALF, RING, 2, NE])
        top_i = sb("top_i", [HALF, 2, NE], U32)
        top_f = sb("top_f", [HALF, 2, 2])
        first_hot = sb("first_hot", [HALF, 2, NE])
        hot = sb("hot", [HALF, 2, NE], BF16)
        base = sb("base", [HALF, RING, 2, NE])
        place = sb("place", [HALF, 2, NE])
        place_one = sb("place_one", [HALF, 4, NE])
        pos = sb("pos", [HALF, 4])
        pos_i = sb("pos_i", [HALF, RING, 4], U32)
        logits_all = sb("logits_all", [HALF, TILES, NE])
        top_all = sb("top_all", [HALF, TILES, 2])
        plan = sb("plan", [1, 6, NE])
        chunk_row = sb("chunk_row", [1, NCH])
        plan_c = sb("plan_c", [1, 5, NCH])
        plan_i = sb("plan_i", [1, 2, NCH], I32)
        fill_i = sb("fill_i", [1, NE], I32)
        count_i = sb("count_i", [1, NE], I32)
        filler = sb("filler", [P, 2, XW])
        xg_cols = sb("xg_cols", [P, 3, CH])
        xg = sb("xg", [P, BR, 2, XW])
        wring = room1[:].rearrange("p (r w) -> p r w", r=BR)
        b2ring = sb("b2ring", [P, BR, D])
        x_room = patches[:].rearrange("p r k n -> p (r k n)")
        hid = x_room[:, 0:6 * CH].rearrange("p (r j n) -> p r j n", r=3, j=2)
        ys = x_room[:, 6 * CH:6 * CH + BR * 2 * D].rearrange("p (r s d) -> p r s d", r=BR, s=2)
        wt = sb("wt", [HALF, TILES, 2])
        psum2 = sb("psum2", [HALF, 3, TILES])
        yin = room2[0:HALF, 0:4 * OG * D].rearrange("p (r k j d) -> p r k j d", r=2, k=2, j=OG)
        res = room1[0:HALF, 0:2 * OG * D].rearrange("p (r j d) -> p r j d", r=2, j=OG)

        c_embed, c_qkv, c_edge, c_misc = sem("c_embed"), sem("c_qkv"), sem("c_edge"), sem("c_misc")
        x_loaded = [sem(f"x_loaded{r}") for r in range(RING)]
        parts_out = [sem(f"parts_out{r}") for r in range(RING)]
        sides_in = [sem(f"sides_in{r}") for r in range(RING)]
        max_in = [sem(f"max_in{r}") for r in range(RING)]
        rows_sent = [sem(f"rows_sent{r}") for r in range(RING)]
        memsets, gone_on = sem("memsets"), sem("gone_on")
        edge_step, edge_max, attr_in = sem("edge_step"), sem("edge_max"), sem("attr_in")
        edge_T, bias_T, bias_done, bias_in = sem("edge_T"), sem("bias_T"), sem("bias_done"), sem("bias_in")
        embed_done, hrows_done, xncols_done = sem("embed_done"), sem("hrows_done"), sem("xncols_done")
        qk_done, v_done, s1_done, s2_done, pv_done = (sem(x) for x in ("qk_done", "v_done", "s1_done", "s2_done", "pv_done"))
        max_T, sums_T, att_T, o_done, xs_T, gate1_done, gate2_done, rank_done = (
            sem(x) for x in ("max_T", "sums_T", "att_T", "o_done", "xs_T", "gate1_done", "gate2_done", "rank_done"))
        hcols_ready, h_ready, xncols_ready, high_ready, probs_ready = (
            sem(x) for x in ("hcols_ready", "h_ready", "xncols_ready", "high_ready", "probs_ready"))
        max_high, sums_ready, att_cols_ready, xs_cols_ready, gate_h_ready = (
            sem(x) for x in ("max_high", "sums_ready", "att_cols_ready", "xs_cols_ready", "gate_h_ready"))
        max_ready, max_low, low_ready, v_ready, rden_ready, att_ready = (
            sem(x) for x in ("max_ready", "max_low", "low_ready", "v_ready", "rden_ready", "att_ready"))
        stats_ready, mv_ready, rstd_ready, xn_ready = (sem(x) for x in ("stats_ready", "mv_ready", "rstd_ready", "xn_ready"))
        h2_ready, stats2_ready, mv2_ready, rstd2_ready, xs_ready = (
            sem(x) for x in ("h2_ready", "stats2_ready", "mv2_ready", "rstd2_ready", "xs_ready"))
        logits_ready, top_ready, top_i_ready, top_f_ready, first_ready, hot_ready = (
            sem(x) for x in ("logits_ready", "top_ready", "top_i_ready", "top_f_ready", "first_ready", "hot_ready"))
        place_ready, base_mid, base_ready, pos_f_ready, pos_ready = (
            sem(x) for x in ("place_ready", "base_mid", "base_ready", "pos_f_ready", "pos_ready"))
        var_ready, var2_ready, ob_added = sem("var_ready"), sem("var2_ready"), sem("ob_added")
        xs2_ready, dest_in, dest_ready, kept = sem("xs2_ready"), sem("dest_in"), sem("dest_ready"), sem("kept")
        plan_step, plan_ready, filled = sem("plan_step"), sem("plan_ready"), sem("filled")
        xg_loaded = [sem(f"xg_loaded{r}") for r in range(BR)]
        w_loaded = [sem(f"w_loaded{r}") for r in range(BR)]
        y_sent = [sem(f"y_sent{r}") for r in range(BR)]
        xg_T, xg_ready, hid_done, hid_ready, y_done, y_ready = (
            sem(x) for x in ("xg_T", "xg_ready", "hid_done", "hid_ready", "y_done", "y_ready"))
        wt_step, wt_exp = sem("wt_step"), sem("wt_exp")
        yin_loaded = [sem(f"yin_loaded{r}") for r in range(2)]
        out_stored = [sem(f"out_stored{r}") for r in range(2)]
        res_mid, res_ready = sem("res_mid"), sem("res_ready")

        block = ctx.enter_context(nc.Block())

        def apart(eng, it):
            if not isinstance(it, int):
                eng.sem_inc(gone_on, 1)

        def slots(eng, slot):
            for t in range(FRONT):
                slot(t, 0)
            if TURNS == 1:
                for u in range(RING):
                    slot(FRONT + u, 0)
            else:
                with eng.Fori(0, TURNS) as it:
                    for u in range(RING):
                        slot(FRONT + u, it)
            for t in range(NB - 1, NB + LAST_LAG):
                slot(t, 0)

        def chunks(eng, ahead, one):
            turns = (NCH - BR - ahead) // BR
            for c in range(BR):
                one(c, 0)
            with eng.Fori(0, turns) as it:
                for u in range(BR):
                    one(BR + u, it)
            for c in range(BR + turns * BR, NCH):
                one(c, 0)

        def tile_rows(n):
            return h_all[:, bass.ds(2 * n, 2), :]

        @block.sync
        def _(sp):
            sp.dma_start(wtok_s[:], wtok).then_inc(c_embed, 16)
            sp.dma_start(cols_s[:], cols).then_inc(c_embed, 16)
            sp.dma_start(patches[:, 0], x[0]).then_inc(x_loaded[0], 16)
            sp.dma_start(ident[:], consts[:, 0:P]).then_inc(c_embed, 16)
            sp.dma_start(wqkv_s[:], wqkv).then_inc(c_qkv, 16)
            sp.dma_start(vb_s[:], rows[0:1, 0:2 * D].to_broadcast([HALF, 2 * D]).rearrange(
                "p (c d) -> p c d", c=2)).then_inc(c_qkv, 16)
            sp.dma_start(wo_s[:], wo).then_inc(c_misc, 16)
            sp.dma_start(gw1_s[:], gw1).then_inc(c_misc, 16)
            sp.dma_start(gw2_s[:], gw2).then_inc(c_misc, 16)
            sp.dma_start(gb2_s[:], rows[0:1, 2 * D:2 * D + 2 * NE].to_broadcast([HALF, 2 * NE]).rearrange(
                "p (c e) -> p c e", c=2)).then_inc(c_misc, 16)
            sp.dma_start(ob_s[:], rows[0:1, 2 * D + 2 * NE:].to_broadcast([HALF, 2 * D]).rearrange(
                "p (c d) -> p c d", c=2)).then_inc(c_misc, 16)
            sp.dma_start(expert_no[:], consts[0:HALF, P:P + NE]).then_inc(c_misc, 16)
            sp.dma_start(region_row[:], consts[0:HALF, P + NE:P + 2 * NE]).then_inc(c_misc, 16)
            sp.dma_start(lower[:], tri).then_inc(c_misc, 16)
            sp.dma_start(chunk_row[:], consts[0:1, P + 2 * NE + N + 1:P + 2 * NE + N + 1 + NCH]).then_inc(c_misc, 16)
            sp.dma_start(tokens_s[:], tokens).then_inc(dest_in, 16)
            sp.wait_ge(memsets, 5)
            sp.dma_start(xsort[NE * REGION:NE * REGION + CH, :].rearrange("(p s) w -> p s w", s=2),
                         filler[:]).then_inc(filled, 16)

            def slot(t, it):
                a, b, c, d = (Image(t, it, lag, NB) for lag in (-1, 1, 3, 0))
                if a.live:
                    wait(sp, embed_done, a.n - 2)
                    apart(sp, it)
                    sp.dma_start(patches[:, a.ring], x[bass.ds(a.n, 1)].rearrange("o p k n -> p (o k) n")).then_inc(
                        x_loaded[a.ring], 16)
                if c.live:
                    sp.wait_ge(max_low, c.n + 1)
                    wait(sp, s2_done, H * (c.n - 2))
                    for j in range(2):
                        sp.dma_start(
                            qside[ROW_MAX + j:ROW_MAX + j + 1, c.ring].bitcast(F32).rearrange(
                                "o h (c n) -> o (h c) n", c=2),
                            negmax[:, c.ring, j].bitcast(F32).rearrange("p (o n) -> p o n", o=1)).then_inc(
                                max_in[c.ring], 16)
                if b.live:
                    sp.wait_ge(low_ready, 2 * (b.n + 1))
                    apart(sp, it)
                    wait(sp, sides_in[b.ring], 96 * b.turn)
                    sp.dma_start(parts_dram[b.ring].rearrange("a j p n -> p (a j) n"),
                                 parts[:, b.ring].bitcast(F32).rearrange("p a j n -> p (a j) n")).then_inc(
                                     parts_out[b.ring], 16)
                    sp.wait_ge(parts_out[b.ring], 16 * (b.turn + 1))
                    apart(sp, it)
                    wait(sp, s2_done, H * (b.n - 2))
                    apart(sp, it)
                    for j in range(4):
                        sp.dma_start(qside[HD * j:HD * (j + 1), b.ring].bitcast(F32).rearrange("d h n -> d (h n)"),
                                     parts_dram[b.ring, 0, j // 2].rearrange("(d h) n -> d (h n)", h=H)).then_inc(
                                         sides_in[b.ring], 16)
                    for j in range(2):
                        sp.dma_start(
                            kside[2 * HD * j:2 * HD * (j + 1), b.ring].bitcast(F32).rearrange("d h n -> d (h n)"),
                            parts_dram[b.ring, 1].rearrange("j (d h) n -> (j d) (h n)", h=H)).then_inc(
                                sides_in[b.ring], 16)

            slots(sp, slot)

            sp.wait_ge(plan_ready, 1)
            for e in range(NE):
                row = sp.value_load(fill_i[0:1, e:e + 1], min_val=0, max_val=NE * REGION - CH)
                sp.dma_start(xsort[bass.ds(row, CH), :].rearrange("(p s) w -> p s w", s=2), filler[:]).then_inc(
                    filled, 16)
            sp.wait_ge(filled, 16 * (NE + 1))
            for r in range(RING):
                sp.wait_ge(rows_sent[r], 64 * len(range(r, NB, RING)))

            def load(c0, it):
                c, ring, turn = BR * it + c0, c0 % BR, it + c0 // BR
                row = sp.value_load(plan_i[0:1, 0, bass.ds(c, 1)], min_val=0, max_val=NE * REGION)
                e = sp.value_load(plan_i[0:1, 1, bass.ds(c, 1)], min_val=0, max_val=NE - 1)
                wait(sp, y_sent[ring], 32 * turn)
                sp.dma_start(xg[:, ring], xsort[bass.ds(row, CH), :].rearrange("(p s) w -> p s w", s=2)).then_inc(
                    xg_loaded[ring], 16)
                sp.dma_start(wring[:, ring], wexp[bass.ds(e, 1)].rearrange("o p w -> p (o w)")).then_inc(
                    w_loaded[ring], 16)
                sp.dma_start(b2ring[:, ring], be2[bass.ds(e, 1), :].to_broadcast([P, D])).then_inc(w_loaded[ring], 16)

            chunks(sp, 0, load)

            for r in range(BR):
                sp.wait_ge(y_sent[r], 32 * len(range(r, NCH, BR)))
            ytiles = ysort.rearrange("(k t p) d -> k p t d", k=2, p=HALF)

            def group(g, r, turn):
                wait(sp, res_ready, g - 1)
                for k in range(2):
                    sp.dma_start(yin[:, r, k], ytiles[k][:, bass.ds(OG * g, OG), :]).then_inc(yin_loaded[r], 16)

            group(0, 0, 0)
            group(1, 1, 0)
            with sp.Fori(1, TILES // OG // 2) as it:
                for r in range(2):
                    group(2 * it + r, r, it)

        @block.gpsimd
        def _(pool):
            nc.gpsimd.memset(qside[4 * HD:P].bitcast(F32), 1.0).then_inc(memsets, 1)
            nc.gpsimd.memset(kside[4 * HD:P].bitcast(F32), 1.0).then_inc(memsets, 1)
            pool.wait_ge(memsets, 2)
            nc.gpsimd.memset(xs[:, :, :, :, D:XW], 0.0).then_inc(memsets, 1)
            nc.gpsimd.memset(filler[:, :, 0:D], 0.0).then_inc(memsets, 1)
            nc.gpsimd.memset(filler[:, :, D:XW].bitcast(U32), int(JUNK_ROW)).then_inc(memsets, 1)
            nc.gpsimd.memset(vaug[:, :, :, :, HD:2 * HD], 1.0).then_inc(memsets, 1)
            pool.wait_ge(dest_in, 16)
            pool.wait_ge(memsets, 3)
            nc.gpsimd.tensor_copy(xs[:, :, :, :, D].bitcast(U32).rearrange("p r c k -> p (r c k)"),
                                  tokens_s[:]).then_inc(dest_ready, 1)
            pool.wait_ge(dest_ready, 1)

            nc.gpsimd.memset(power[:], -0.5).then_inc(memsets, 1)
            pool.wait_ge(memsets, 7)
            pool.wait_ge(c_misc, 144)

            def edge_attributes():
                pool.wait_ge(edge_max, 4)
                for c in range(2):
                    pool.indirect_dma_start(attr_s[:, c, :], None, attr, bass.IndirectOffsetOnAxis(
                        ap=last_i[:, c:c + 1], axis=0)).then_inc(attr_in, 16)

            def rsqrt(out_, mv_, var_, ready, n, it):
                nc.gpsimd.tensor_scalar(var_, mv_[:, :, 1], EPS, None, ALU.add).then_inc(ready[0], 1)
                pool.wait_ge(ready[0], n + 1)
                apart(pool, it)
                nc.gpsimd.tensor_tensor(out_, var_, power[:], ALU.pow).then_inc(ready[1], 1)

            def slot(t, it):
                i0, i1, i4, i5 = (Image(t, it, lag, NB) for lag in (0, 1, 4, 5))
                if t == 1:
                    edge_attributes()
                if i5.live:
                    pool.wait_ge(xs_ready, 2 * (i5.n + 1))
                    wait(pool, rows_sent[i5.ring], 64 * i5.turn)
                    apart(pool, it)
                    nc.gpsimd.tensor_copy(xs[:, i5.ring, :, 1, 0:D], xs[:, i5.ring, :, 0, 0:D]).then_inc(xs2_ready, 1)
                    step = 0.0 if isinstance(i5.n, int) and i5.n < RING else float(RING * N)
                    dest = xs[:, i5.ring, :, :, D].bitcast(U32)
                    nc.gpsimd.tensor_scalar(dest, dest, step, None, ALU.add).then_inc(xs2_ready, 1)
                if i1.live:
                    pool.wait_ge(xn_ready, 2 * (i1.n + 1))
                    apart(pool, it)
                    nc.gpsimd.tensor_tensor(tile_rows(i1.n), tile_rows(i1.n), ob_s[:], ALU.add).then_inc(ob_added, 1)
                if i5.live:
                    pool.wait_ge(top_ready, 2 * (i5.n + 1))
                    apart(pool, it)
                    nc.gpsimd.tensor_copy(logits_all[:, bass.ds(2 * i5.n, 2), :], logits[:, i5.ring]).then_inc(kept, 1)
                    nc.gpsimd.tensor_copy(top_all[:, bass.ds(2 * i5.n, 2), :], top[:, i5.ring, :, 0:2]).then_inc(
                        kept, 1)
                if i0.live:
                    pool.wait_ge(mv_ready, 2 * (i0.n + 1))
                    wait(pool, xn_ready, 2 * i0.n)
                    apart(pool, it)
                    rsqrt(rstd[:], mv, var[:], (var_ready, rstd_ready), i0.n, it)
                if i4.live:
                    pool.wait_ge(mv2_ready, 2 * (i4.n + 1))
                    wait(pool, xs_ready, 2 * i4.n)
                    apart(pool, it)
                    rsqrt(rstd2[:], mv2, var2[:], (var2_ready, rstd2_ready), i4.n, it)
                if i5.live:
                    pool.wait_ge(pos_ready, i5.n + 1)
                    pool.wait_ge(xs2_ready, 2 * i5.n + 2)
                    apart(pool, it)
                    for c in range(2):
                        for k in range(2):
                            j = 2 * c + k
                            pool.indirect_dma_start(
                                xsort, bass.IndirectOffsetOnAxis(ap=pos_i[:, i5.ring, j:j + 1], axis=0),
                                xs[:, i5.ring, c, k, :], None).then_inc(rows_sent[i5.ring], 16)

            slots(pool, slot)

            def send(c0, it):
                c, ring = BR * it + c0, c0 % BR
                pool.wait_ge(y_ready, c + 1)
                apart(pool, it)
                for s in range(2):
                    pool.indirect_dma_start(
                        ysort, bass.IndirectOffsetOnAxis(ap=xg[:, ring, s, D:D + 1].bitcast(U32), axis=0),
                        ys[:, ring, s, :], None, bounds_check=2 * NT - 1, oob_is_err=False).then_inc(y_sent[ring], 16)

            chunks(pool, 0, send)

        @block.scalar
        def _(act):
            act.dma_start(edge_i, edges).then_inc(c_edge, 16)
            act.dma_start(tok_no[:], consts[:, P + 2 * NE:P + 2 * NE + N + 1]).then_inc(c_edge, 16)
            act.dma_start(ebw_s[:], ebw[0:1, :].to_broadcast([HALF, 4 * H]).rearrange(
                "p (j h) -> p j h", j=4)).then_inc(c_edge, 16)
            act.wait_ge(c_embed, 48)

            def bias_rows():
                act.wait_ge(bias_T, 1)
                nc.scalar.activation(bias_part[:, 0], ps[0:H, SMALL, 0:N], ACT.Copy).then_inc(bias_done, 1)
                act.wait_ge(bias_done, 2)
                act.wait_ge(memsets, 6)
                for r in range(RING):
                    for j in range(2):
                        act.dma_start(kside[ROW_BIAS + j:ROW_BIAS + j + 1, r].bitcast(F32),
                                      bias_part[:, j].bitcast(F32).rearrange("p (o n) -> p o n", o=1)
                                      ).then_inc(bias_in, 16)

            def slot(t, it):
                i0, i1, i3, i4, i5 = (Image(t, it, lag, NB) for lag in (0, 1, 3, 4, 5))
                if t == 1:
                    bias_rows()
                for s in range(H):
                    img, h = (i4, s + 4) if s < 4 else (i3, s - 4)
                    if s == 0 and i3.live:
                        act.wait_ge(max_T, i3.n + 1)
                        wait(act, max_in[i3.ring], 32 * i3.turn)
                        nc.scalar.activation(negmax[:, i3.ring, 0], ps[0:2 * H, SMALL, 0:HALF], ACT.Copy,
                                             scale=-1.0).then_inc(max_high, 1)
                    if img.live:
                        act.wait_ge(s2_done, H * img.n + h + 1)
                        wait(act, pv_done, H * img.n + h - 3)
                        nc.scalar.activation(probs[:, h % 4], ps[0:HALF, S2, 0:2 * N], ACT.Exp,
                                             scale=float(HD) ** -0.5).then_inc(probs_ready, 1)
                    if s == 0 and i4.live or s == 4 and i4.live:
                        g = s // 4
                        act.wait_ge(pv_done, H * i4.n + 4 * g + 4)
                        wait(act, sums_T, i4.n)
                        nc.scalar.activation(sums[:, g], ps[:, PVA + g, 0:N], ACT.Copy).then_inc(sums_ready, 1)
                    if s == 6 and i4.live:
                        act.wait_ge(att_T, i4.n + 1)
                        wait(act, o_done, i4.n)
                        nc.scalar.activation(att_cols[:], ps[:, PROJ, 0:N], ACT.Copy).then_inc(att_cols_ready, 1)
                    if s == 1 and i5.live:
                        act.wait_ge(xs_T, i5.n + 1)
                        wait(act, gate1_done, i5.n)
                        nc.scalar.activation(xs_cols[:], ps[:, PROJ, 0:N], ACT.Copy).then_inc(xs_cols_ready, 1)
                    if s == 1 and i0.live:
                        act.wait_ge(embed_done, i0.n + 1)
                        wait(act, hrows_done, i0.n)
                        nc.scalar.activation(hcols[:], ps[:, ROWS, 0:N], ACT.Identity, bias=cols_s[:, 0:1]).then_inc(
                            hcols_ready, 1)
                    if s == 2 and i1.live:
                        act.wait_ge(qk_done, i1.n + 1)
                        wait(act, parts_out[i1.ring], 16 * i1.turn)
                        for a in range(2):
                            nc.scalar.activation(parts[:, i1.ring, a, 0], ps[:, PROJ, a * N:(a + 1) * N],
                                                 ACT.Identity, bias=cols_s[:, 1 + a:2 + a]).then_inc(high_ready, 1)
                    if s == 3 and i5.live:
                        act.wait_ge(gate1_done, i5.n + 1)
                        wait(act, gate2_done, i5.n)
                        nc.scalar.activation(gate_h[:], ps[:, SMALL, 0:N], ACT.Relu, bias=cols_s[:, 3:4]).then_inc(
                            gate_h_ready, 1)
                    if s == 3 and i0.live:
                        act.wait_ge(hrows_done, i0.n + 1)
                        nc.scalar.activation(tile_rows(i0.n), ps[0:HALF, ROWS, 0:2 * D].rearrange(
                            "p (c d) -> p c d", c=2), ACT.Copy).then_inc(h_ready, 1)
                    if s == 6 and i0.live:
                        act.wait_ge(xncols_done, i0.n + 1)
                        wait(act, v_done, i0.n - 2)
                        nc.scalar.activation(xncols[:, i0.ring], ps[:, ROWS, 0:N], ACT.Copy).then_inc(xncols_ready, 1)

            slots(act, slot)

            act.wait_ge(wt_step, 2)
            nc.scalar.activation(logits_all[:], logits_all[:], ACT.Exp).then_inc(wt_exp, 1)
            nc.scalar.activation(psum2[:, 0], psum2[:, 0], ACT.Exp).then_inc(wt_exp, 1)
            act.wait_ge(wt_step, 6)
            nc.scalar.activation(psum2[:, 1], psum2[:, 1], ACT.Exp).then_inc(wt_exp, 1)

            def gelu(c0, it):
                c, r3, ring = BR * it + c0, c0 % 3, c0 % BR
                act.wait_ge(hid_done, c + 1)
                wait(act, y_done, c - 2)
                for j in range(2):
                    nc.scalar.activation(hid[:, r3, j], ps[:, HBANKS[r3], j * CH:(j + 1) * CH], ACT.Gelu,
                                         bias=wring[:, ring, 2 * HID + j:2 * HID + j + 1]).then_inc(hid_ready, 1)

            chunks(act, 0, gelu)

            otiles = out.rearrange("b (c p) d -> p (b c) d", p=HALF)

            def store(g, r):
                act.wait_ge(res_ready, g + 1)
                act.dma_start(otiles[:, bass.ds(OG * g, OG), :], res[:, r]).then_inc(out_stored[r], 16)

            with act.Fori(0, TILES // OG // 2) as it:
                for r in range(2):
                    store(2 * it + r, r)
            for r in range(2):
                act.wait_ge(out_stored[r], 16 * (TILES // OG // 2))

        @block.vector
        def _(dve):
            v = nc.vector
            dve.wait_ge(c_edge, 48)
            v.tensor_copy(edge_f, edge_i).then_inc(edge_step, 1)
            v.tensor_copy(tok_no16[:], tok_no[:, 0:N]).then_inc(edge_step, 1)
            v.memset(edge_last16[:], 0.0).then_inc(edge_step, 1)
            dve.wait_ge(edge_step, 3)
            for j in range(2):
                v.tensor_scalar(edge_ok[:, j], edge_f[:, j], 0.0, None, ALU.is_ge).then_inc(edge_step, 1)
            dve.wait_ge(edge_step, 5)
            for j in range(2):
                v.scalar_tensor_tensor(edge_ok[:, 2 + j], edge_f[:, j], float(N), edge_ok[:, j],
                                       ALU.is_lt, ALU.mult).then_inc(edge_step, 1)
            dve.wait_ge(edge_step, 7)
            v.tensor_tensor(edge_ok[:, 0], edge_ok[:, 2], edge_ok[:, 3], ALU.mult).then_inc(edge_step, 1)
            dve.wait_ge(edge_step, 8)
            v.tensor_tensor(edge_key, edge_ok[:, 0], tok_no[:, 1:EJ + 1], ALU.mult).then_inc(edge_step, 1)
            dve.wait_ge(edge_step, 9)
            for j in range(EJ):
                if j:
                    dve.wait_ge(edge_step, 8 + 2 * j)
                v.tensor_scalar(edge_hit[:, j % 2], tok_no16[:], edge_f[:, 1, j:j + 1], edge_key[:, j:j + 1],
                                ALU.is_equal, ALU.mult).then_inc(edge_step, 1)
                dve.wait_ge(edge_step, 10 + 2 * j)
                v.tensor_tensor(edge_last16[:, (j + 1) % 2], edge_last16[:, j % 2], edge_hit[:, j % 2],
                                ALU.max).then_inc(edge_step, 1)
            es = 9 + 2 * EJ
            dve.wait_ge(edge_step, es)
            v.tensor_scalar(edge_last[:], edge_last16[:, EJ % 2], 0.0, tok_no[:, N:N + 1], ALU.is_gt, ALU.mult).then_inc(
                edge_step, 1)
            dve.wait_ge(edge_step, es + 1)
            v.tensor_tensor(edge_last[:], edge_last[:], edge_last16[:, EJ % 2], ALU.add).then_inc(edge_T, 1)
            dve.wait_ge(c_misc, 144)
            v.tensor_copy(base[:, 0, 0], region_row[:]).then_inc(base_ready, 1)

            def attend(img):
                dve.wait_ge(sums_T, img.n + 1)
                wait(dve, att_T, img.n)
                four = ps[0:HALF, PROJ, :].rearrange("p (c h f) -> p c h f", c=2, h=H)
                v.reciprocal(rden[:], four[:, :, :, HD]).then_inc(rden_ready, 1)
                dve.wait_ge(rden_ready, img.n + 1)
                for c in range(2):
                    v.tensor_tensor(att[:, c], four[:, c, :, 0:HD],
                                    rden[:, c].rearrange("p (h o) -> p h o", o=1).to_broadcast([HALF, H, HD]),
                                    ALU.mult).then_inc(att_ready, 1)

            def norm_stats(img, it, sems, s_, m_):
                apart(dve, it)
                for c in range(2):
                    v.bn_stats(s_[:, c], h_all[:, bass.ds(2 * img.n + c, 1), :].rearrange("p o d -> p (o d)")).then_inc(
                        sems[0], 1)
                dve.wait_ge(sems[0], 2 * (img.n + 1))
                apart(dve, it)
                for c in range(2):
                    v.bn_aggr(m_[:, c], s_[:, c]).then_inc(sems[1], 1)

            def normed(img, out_, m_, r_, c):
                return v.tensor_scalar(out_, h_all[:, bass.ds(2 * img.n + c, 1), :].rearrange("p o d -> p (o d)"),
                                       m_[:, c, 0:1], r_[:, c:c + 1], ALU.subtract, ALU.mult)

            def column_bias():
                dve.wait_ge(edge_T, 2)
                v.tensor_reduce(last[:, 0], ps[0:HALF, SMALL, 0:2 * P].rearrange("p (c e) -> p c e", c=2),
                                AX_X, ALU.max).then_inc(edge_max, 1)
                dve.wait_ge(edge_max, 1)
                v.tensor_scalar(last[:, 1], last[:, 0], 1.0, 4.0, ALU.is_ge, ALU.mult).then_inc(edge_max, 1)
                v.tensor_scalar(last[:, 2], last[:, 0], -1.0, 0.0, ALU.add, ALU.max).then_inc(edge_max, 1)
                dve.wait_ge(edge_max, 3)
                v.tensor_copy(last_i[:], last[:, 2]).then_inc(edge_max, 1)
                dve.wait_ge(attr_in, 32)
                for c in range(2):
                    for j in range(3):
                        v.scalar_tensor_tensor(eb[:, c], ebw_s[:, j], attr_s[:, c, j:j + 1],
                                               ebw_s[:, 3] if j == 0 else eb[:, c], ALU.mult, ALU.add).then_inc(
                                                   edge_max, 1)
                        dve.wait_ge(edge_max, 5 + 4 * c + j)
                    v.tensor_scalar(eb[:, c], eb[:, c], last[:, 1, c:c + 1], None, ALU.mult).then_inc(edge_max, 1)
                dve.wait_ge(bias_done, 1)
                v.tensor_tensor(bias_part[:, 1], ps[0:H, SMALL, 0:N], bias_part[:, 0].bitcast(F32),
                                ALU.subtract).then_inc(bias_done, 1)

            def slot(t, it):
                i0, i1, i2, i3, i4, i5 = (Image(t, it, lag, NB) for lag in range(6))
                if t == 1:
                    column_bias()
                for s in range(H):
                    if s == 0 and i3.live:
                        dve.wait_ge(max_high, i3.n + 1)
                        v.scalar_tensor_tensor(negmax[:, i3.ring, 1], ps[0:2 * H, SMALL, 0:HALF], -1.0,
                                               negmax[:, i3.ring, 0].bitcast(F32), ALU.mult, ALU.subtract).then_inc(
                                                   max_low, 1)
                    if i2.live:
                        dve.wait_ge(s1_done, H * i2.n + s + 1)
                        v.tensor_reduce(rowmax[:, i2.ring, 2 * s:2 * s + 2],
                                        ps[0:HALF, S1A + s % 2, 0:2 * N].rearrange("p (c n) -> p c n", c=2),
                                        AX_X, ALU.max).then_inc(max_ready, 1)
                    if s == 0 and i5.live:
                        dve.wait_ge(rstd2_ready, i5.n + 1)
                        wait(dve, rows_sent[i5.ring], 64 * i5.turn)
                        for c in range(2):
                            normed(i5, xs[:, i5.ring, c, 0, 0:D], mv2, rstd2, c).then_inc(xs_ready, 1)
                    if s == 2 and i1.live:
                        dve.wait_ge(high_ready, 2 * (i1.n + 1))
                        for a in range(2):
                            v.scalar_tensor_tensor(parts[:, i1.ring, a, 1], ps[:, PROJ, a * N:(a + 1) * N],
                                                   cols_s[:, 1 + a:2 + a], parts[:, i1.ring, a, 0].bitcast(F32),
                                                   ALU.add, ALU.subtract).then_inc(low_ready, 1)
                    if s == 4 and i5.live:
                        dve.wait_ge(gate2_done, i5.n + 1)
                        wait(dve, kept, 2 * (i5.n - 2))
                        v.tensor_tensor(logits[:, i5.ring], ps[0:HALF, SMALL, 0:2 * NE].rearrange(
                            "p (c e) -> p c e", c=2), gb2_s[:], ALU.add).then_inc(logits_ready, 1)
                        dve.wait_ge(logits_ready, i5.n + 1)
                        apart(dve, it)
                        for c in range(2):
                            v.max(top[:, i5.ring, c], logits[:, i5.ring, c]).then_inc(top_ready, 1)
                        dve.wait_ge(top_ready, 2 * (i5.n + 1))
                        apart(dve, it)
                        for c in range(2):
                            v.max_index(top_i[:, c], top[:, i5.ring, c], logits[:, i5.ring, c]).then_inc(top_i_ready, 1)
                        dve.wait_ge(top_i_ready, 2 * (i5.n + 1))
                        v.tensor_copy(top_f[:], top_i[:, :, 0:2]).then_inc(top_f_ready, 1)
                        dve.wait_ge(top_f_ready, i5.n + 1)
                        for c in range(2):
                            v.tensor_scalar(first_hot[:, c], expert_no[:], top_f[:, c, 0:1], None,
                                            ALU.is_equal).then_inc(first_ready, 1)
                        for c in range(2):
                            dve.wait_ge(first_ready, 2 * i5.n + 1 + c)
                            v.scalar_tensor_tensor(hot[:, c], expert_no[:], top_f[:, c, 1:2], first_hot[:, c],
                                                   ALU.is_equal, ALU.add).then_inc(hot_ready, 1)
                    if s == 5 and i1.live:
                        dve.wait_ge(v_done, i1.n + 1)
                        wait(dve, pv_done, H * (i1.n - 2))
                        v.tensor_tensor(vaug[:, i1.ring, :, :, 0:HD], ps[0:HALF, SMALL, 0:2 * D].rearrange(
                            "p (c h d) -> p c h d", c=2, h=H), vb_s[:].rearrange("p c (h d) -> p c h d", h=H),
                            ALU.add).then_inc(v_ready, 1)
                    if s == 4 and i0.live:
                        dve.wait_ge(h_ready, i0.n + 1)
                        wait(dve, var_ready, i0.n)
                        norm_stats(i0, it, (stats_ready, mv_ready), stats, mv)
                    if s == 5 and i4.live:
                        attend(i4)
                    if s == 5 and i0.live:
                        dve.wait_ge(rstd_ready, i0.n + 1)
                        wait(dve, xncols_done, i0.n)
                        for c in range(2):
                            normed(i0, xn[:, c], mv, rstd, c).then_inc(xn_ready, 1)
                    if s == 7 and i4.live:
                        dve.wait_ge(o_done, i4.n + 1)
                        dve.wait_ge(ob_added, i4.n + 1)
                        v.tensor_tensor(tile_rows(i4.n), ps[0:HALF, PROJ, 0:2 * D].rearrange("p (c d) -> p c d", c=2),
                                        tile_rows(i4.n), ALU.add).then_inc(h2_ready, 1)
                        dve.wait_ge(h2_ready, i4.n + 1)
                        wait(dve, var2_ready, i4.n)
                        norm_stats(i4, it, (stats2_ready, mv2_ready), stats2, mv2)
                    if s == 7 and i5.live:
                        n, r = i5.n, i5.ring
                        dve.wait_ge(rank_done, n + 1)
                        dve.wait_ge(base_ready, n + 1)
                        v.tensor_tensor(place[:, 0], ps[0:HALF, SMALL, 0:NE], base[:, r, 0], ALU.add).then_inc(
                            place_ready, 1)
                        v.tensor_tensor(base[:, r, 1], ps[0:HALF, SMALL, 2 * NE:3 * NE], base[:, r, 0],
                                        ALU.add).then_inc(base_mid, 1)
                        dve.wait_ge(base_mid, n + 1)
                        v.tensor_tensor(place[:, 1], ps[0:HALF, SMALL, NE:2 * NE], base[:, r, 1], ALU.add).then_inc(
                            place_ready, 1)
                        v.tensor_tensor(base[:, (r + 1) % RING, 0], ps[0:HALF, SMALL, 3 * NE:4 * NE], base[:, r, 1],
                                        ALU.add).then_inc(base_ready, 1)
                        for c in range(2):
                            dve.wait_ge(place_ready, 2 * n + 1 + c)
                            for k in range(2):
                                j = 2 * c + k
                                v.scalar_tensor_tensor(place_one[:, j], expert_no[:], top_f[:, c, k:k + 1], place[:, c],
                                                       ALU.is_equal, ALU.mult, accum_out=pos[:, j:j + 1]).then_inc(
                                                           pos_f_ready, 1)
                        dve.wait_ge(pos_f_ready, 4 * (n + 1))
                        wait(dve, rows_sent[r], 64 * i5.turn)
                        v.tensor_copy(pos_i[:, r], pos[:]).then_inc(pos_ready, 1)

            slots(dve, slot)

            steps = [0]

            def step(ins):
                steps[0] += 1
                ins.then_inc(plan_step, 1)
                dve.wait_ge(plan_step, steps[0])

            fin = base[0:1, NB % RING, 0]
            dve.wait_ge(base_ready, NB + 1)
            count, rounded, ends, ones = (plan[:, i] for i in range(4))
            step(v.tensor_tensor(count, fin, region_row[0:1], ALU.subtract))
            step(v.tensor_scalar(count, count, float(CH - 1), None, ALU.add))
            step(v.tensor_copy(count_i[:], count))
            step(v.tensor_scalar(count_i[:], count_i[:], 8, 8, ALU.logical_shift_right, ALU.logical_shift_left))
            step(v.tensor_copy(rounded, count_i[:]))
            step(v.memset(ones, 1.0))
            step(v.tensor_tensor_scan(ends, ones, rounded, 0.0, ALU.mult, ALU.add))
            expert, start, passed, row, live_ = (plan_c[:, i] for i in range(5))
            step(v.memset(plan_c[:], 0.0))
            for e in range(NE):
                step(v.scalar_tensor_tensor(expert, chunk_row[:], ends[:, e:e + 1], expert, ALU.is_ge, ALU.add))
                step(v.tensor_scalar(passed, chunk_row[:], ends[:, e:e + 1], rounded[:, e:e + 1], ALU.is_ge, ALU.mult))
                step(v.tensor_tensor(start, start, passed, ALU.add))
            step(v.tensor_scalar(live_, expert, float(NE), None, ALU.is_lt))
            step(v.tensor_tensor(row, chunk_row[:], start, ALU.subtract))
            step(v.tensor_tensor(row, row, live_, ALU.mult))
            step(v.scalar_tensor_tensor(row, expert, float(REGION), row, ALU.mult, ALU.add))
            step(v.tensor_scalar(expert, expert, float(NE - 1), None, ALU.min))
            step(v.tensor_copy(plan_i[:, 0], row))
            step(v.tensor_copy(plan_i[:, 1], expert))
            v.tensor_copy(fill_i[:], fin).then_inc(plan_ready, 1)

            dve.wait_ge(kept, 2 * NB)
            best = top_all[:, :, 0:1]
            v.tensor_tensor(logits_all[:], logits_all[:], best.to_broadcast([HALF, TILES, NE]),
                            ALU.subtract).then_inc(wt_step, 1)
            v.tensor_tensor(psum2[:, 0], top_all[:, :, 1], top_all[:, :, 0], ALU.subtract).then_inc(wt_step, 1)
            dve.wait_ge(wt_exp, 2)
            v.tensor_reduce(psum2[:, 2], logits_all[:], AX_X, ALU.add).then_inc(wt_step, 1)
            dve.wait_ge(wt_step, 3)
            v.reciprocal(psum2[:, 1], psum2[:, 2]).then_inc(wt_step, 1)
            dve.wait_ge(wt_step, 4)
            v.tensor_tensor(psum2[:, 0], psum2[:, 0], psum2[:, 1], ALU.mult).then_inc(wt_step, 1)
            dve.wait_ge(wt_step, 5)
            v.tensor_tensor(psum2[:, 1], psum2[:, 0], psum2[:, 1], ALU.subtract).then_inc(wt_step, 1)
            dve.wait_ge(wt_exp, 3)
            v.tensor_scalar(psum2[:, 2], psum2[:, 1], 1.0, None, ALU.add).then_inc(wt_step, 1)
            dve.wait_ge(wt_step, 7)
            v.reciprocal(wt[:, :, 0], psum2[:, 2]).then_inc(wt_step, 1)
            dve.wait_ge(wt_step, 8)
            v.tensor_tensor(wt[:, :, 1], psum2[:, 1], wt[:, :, 0], ALU.mult).then_inc(wt_step, 1)

            def turned(c0, it):
                c = BR * it + c0
                dve.wait_ge(xg_T, c + 1)
                wait(dve, hid_done, c - 2)
                v.tensor_copy(xg_cols[:, c0 % 3], ps[:, ROWS, 0:CH]).then_inc(xg_ready, 1)

            def biased(c0, it):
                c, r3, ring, turn = BR * it + c0, c0 % 3, c0 % BR, it + c0 // BR
                dve.wait_ge(y_done, c + 1)
                wait(dve, y_sent[ring], 32 * turn)
                b2 = b2ring[:, ring:ring + 1, :].to_broadcast([P, 2, D])
                v.tensor_tensor(ys[:, ring], ps[:, YBANKS[r3], 0:2 * D].rearrange("p (s d) -> p s d", s=2), b2,
                                ALU.add).then_inc(y_ready, 1)

            def both(c0, it):
                if not isinstance(it, int) or c0 + 2 < NCH:
                    turned(c0 + 2, it)
                biased(c0, it)

            turned(0, 0)
            turned(1, 0)
            chunks(dve, 2, both)

            def group(g, r, turn):
                dve.wait_ge(yin_loaded[r], 32 * (turn + 1))
                wait(dve, out_stored[r], 16 * turn)
                for k in range(2):
                    for j in range(OG):
                        i = OG * g + j
                        if k == 1:
                            dve.wait_ge(res_mid, OG * g + j + 1)
                        old = h_all[:, bass.ds(i, 1), :].rearrange("p o d -> p (o d)") if k == 0 else res[:, r, j]
                        ins = v.scalar_tensor_tensor(res[:, r, j], yin[:, r, k, j],
                                                     wt[:, bass.ds(i, 1), k:k + 1].rearrange("p o k -> p (o k)"), old,
                                                     ALU.mult, ALU.add)
                        if k == 0:
                            ins.then_inc(res_mid, 1)
                        elif j == OG - 1:
                            ins.then_inc(res_ready, 1)

            dve.wait_ge(wt_step, 9)
            group(0, 0, 0)
            group(1, 1, 0)
            with dve.Fori(1, TILES // OG // 2) as it:
                for r in range(2):
                    group(2 * it + r, r, it)

        @block.tensor
        def _(pe):
            mm, tr = nc.tensor.matmul, nc.tensor.transpose

            def edge_turn():
                pe.wait_ge(c_embed, 48)
                pe.wait_ge(edge_T, 1)
                for c in range(2):
                    last_ = tr(ps[0:HALF, SMALL, c * P:(c + 1) * P], edge_last[:, c * HALF:(c + 1) * HALF], ident[:])
                last_.then_inc(edge_T, 1)
                pe.wait_ge(edge_max, 12)
                for c in range(2):
                    last_ = tr(ps[0:H, SMALL, c * HALF:(c + 1) * HALF], eb[:, c], ident[0:HALF, 0:HALF])
                last_.then_inc(bias_T, 1)

            def slot(t, it):
                i0, i1, i2, i3, i4, i5, i6 = (Image(t, it, lag, NB) for lag in range(7))
                if t == 0:
                    pe.wait_ge(c_embed, 48)
                if t == 1:
                    edge_turn()
                    pe.wait_ge(c_qkv, 32)
                if t == 2:
                    pe.wait_ge(bias_in, 16 * 2 * RING)
                if t == 4:
                    pe.wait_ge(c_misc, 144)
                for s in range(H):
                    if s == 0 and i3.live:
                        pe.wait_ge(max_ready, H * (i3.n + 1))
                        if i6.live:
                            pe.wait_ge(pos_f_ready, 4 * (i6.n + 1))
                            pe.wait_ge(base_ready, i6.n + 2)
                        tr(ps[0:2 * H, SMALL, 0:HALF], rowmax[:, i3.ring], ident[0:HALF, 0:HALF]).then_inc(max_T, 1)
                    if i2.live:
                        if s == 0:
                            pe.wait_ge(sides_in[i2.ring], 96 * (i2.turn + 1))
                        wait(pe, max_ready, H * i2.n + s - 1)
                        for c in range(2):
                            last_ = mm(ps[0:HALF, S1A + s % 2, c * N:(c + 1) * N],
                                       qside[0:ROW_MAX, i2.ring, s, c * HALF:(c + 1) * HALF],
                                       kside[0:ROW_MAX, i2.ring, s, :], start=True, stop=True)
                        last_.then_inc(s1_done, 1)
                    img, h = (i4, s + 4) if s < 4 else (i3, s - 4)
                    if img.live:
                        if s == 4:
                            pe.wait_ge(max_in[img.ring], 32 * (img.turn + 1))
                        wait(pe, probs_ready, H * img.n + h)
                        for c in range(2):
                            last_ = mm(ps[0:HALF, S2, c * N:(c + 1) * N],
                                       kside[0:ROW_END, img.ring, h, c * HALF:(c + 1) * HALF],
                                       qside[0:ROW_END, img.ring, h, :], start=True, stop=True)
                        last_.then_inc(s2_done, 1)
                    if s == 1 and i5.live:
                        pe.wait_ge(xs_ready, 2 * (i5.n + 1))
                        for c in range(2):
                            last_ = tr(ps[:, PROJ, c * HALF:(c + 1) * HALF], xs[:, i5.ring, c, 0, 0:D],
                                       ident[0:HALF, 0:HALF])
                        last_.then_inc(xs_T, 1)
                    if s in (0, 1) and i0.live:
                        if s == 0:
                            pe.wait_ge(x_loaded[i0.ring], 16 * (i0.turn + 1))
                            wait(pe, xncols_ready, i0.n)
                        for k in range(s * NK // 2, (s + 1) * NK // 2):
                            last_ = mm(ps[:, ROWS, 0:N], wtok_s[:, k], patches[:, i0.ring, k], start=(k == 0),
                                       stop=(k == NK - 1))
                        if s == 1:
                            last_.then_inc(embed_done, 1)
                    if s == 2 and i1.live:
                        pe.wait_ge(xncols_ready, i1.n + 1)
                        if i5.live:
                            pe.wait_ge(xs_cols_ready, i5.n + 1)
                        for a in range(2):
                            last_ = mm(ps[:, PROJ, a * N:(a + 1) * N], wqkv_s[:, a], xncols[:, i1.ring], start=True,
                                       stop=True)
                        last_.then_inc(qk_done, 1)
                    if s == 3 and i5.live:
                        pe.wait_ge(xs_cols_ready, i5.n + 1)
                        if i3.live:
                            pe.wait_ge(max_low, i3.n + 1)
                        mm(ps[:, SMALL, 0:N], gw1_s[:], xs_cols[:], start=True, stop=True).then_inc(gate1_done, 1)
                    if s == 3 and i0.live:
                        pe.wait_ge(hcols_ready, i0.n + 1)
                        for c in range(2):
                            last_ = tr(ps[0:HALF, ROWS, c * D:(c + 1) * D], hcols[:, c * HALF:(c + 1) * HALF], ident[:])
                        last_.then_inc(hrows_done, 1)
                    if s == 4 and i5.live:
                        pe.wait_ge(gate_h_ready, i5.n + 1)
                        for c in range(2):
                            last_ = mm(ps[0:HALF, SMALL, c * NE:(c + 1) * NE], gate_h[:, c * HALF:(c + 1) * HALF],
                                       gw2_s[:], start=True, stop=True)
                        last_.then_inc(gate2_done, 1)
                    if s == 5 and i1.live:
                        if i5.live:
                            pe.wait_ge(logits_ready, i5.n + 1)
                        elif i3.live:
                            pe.wait_ge(max_low, i3.n + 1)
                        for c in range(2):
                            last_ = mm(ps[0:HALF, SMALL, c * D:(c + 1) * D],
                                       xncols[:, i1.ring, c * HALF:(c + 1) * HALF], wqkv_s[:, 2], start=True, stop=True)
                        last_.then_inc(v_done, 1)
                    if s == 5 and i4.live:
                        pe.wait_ge(sums_ready, 2 * (i4.n + 1))
                        if i1.live:
                            pe.wait_ge(low_ready, 2 * (i1.n + 1))
                        elif i5.live:
                            pe.wait_ge(xs_cols_ready, i5.n + 1)
                        for c in range(2):
                            for g in range(2):
                                last_ = tr(ps[0:HALF, PROJ, (2 * c + g) * P:(2 * c + g + 1) * P],
                                           sums[:, g, c * HALF:(c + 1) * HALF], ident[:])
                        last_.then_inc(sums_T, 1)
                    if s == 6 and i4.live:
                        pe.wait_ge(att_ready, 2 * (i4.n + 1))
                        for c in range(2):
                            last_ = tr(ps[:, PROJ, c * HALF:(c + 1) * HALF], att[:, c].rearrange("p h d -> p (h d)"),
                                       ident[0:HALF, 0:HALF])
                        last_.then_inc(att_T, 1)
                    if s == 7 and i4.live:
                        pe.wait_ge(att_cols_ready, i4.n + 1)
                        for c in range(2):
                            last_ = mm(ps[0:HALF, PROJ, c * D:(c + 1) * D], att_cols[:, c * HALF:(c + 1) * HALF],
                                       wo_s[:], start=True, stop=True)
                        last_.then_inc(o_done, 1)
                    if s == 6 and i5.live:
                        pe.wait_ge(hot_ready, 2 * (i5.n + 1))
                        if i1.live:
                            pe.wait_ge(v_ready, i1.n + 1)
                        for a in range(2):
                            last_ = mm(ps[0:HALF, SMALL, 2 * NE * a:2 * NE * (a + 1)], lower[:, a],
                                       hot[:].rearrange("p c e -> p (c e)"), start=True, stop=True)
                        last_.then_inc(rank_done, 1)
                    if s == 6 and i0.live:
                        pe.wait_ge(xn_ready, 2 * (i0.n + 1))
                        for c in range(2):
                            last_ = tr(ps[:, ROWS, c * HALF:(c + 1) * HALF], xn[:, c], ident[0:HALF, 0:HALF])
                        last_.then_inc(xncols_done, 1)
                    if img.live:
                        g, j = h // 4, h % 4
                        pe.wait_ge(probs_ready, H * img.n + h + 1)
                        if h == 0:
                            pe.wait_ge(v_ready, img.n + 1)
                        if j == 0:
                            wait(pe, sums_ready, 2 * img.n + g - 1)
                        for c in range(2):
                            last_ = mm(ps[2 * HD * j:2 * HD * (j + 1), PVA + g, 0:N], vaug[:, img.ring, c, h],
                                       probs[:, h % 4, c], start=(c == 0), stop=(c == 1))
                        last_.then_inc(pv_done, 1)

            slots(pe, slot)

            def turn_x(c0, it):
                c, ring, turn = BR * it + c0, c0 % BR, it + c0 // BR
                pe.wait_ge(xg_loaded[ring], 16 * (turn + 1))
                wait(pe, xg_ready, c)
                for s in range(2):
                    last_ = tr(ps[:, ROWS, s * P:(s + 1) * P], xg[:, ring, s, 0:D], ident[:])
                last_.then_inc(xg_T, 1)

            def hidden(c0, it):
                c, r3, ring, turn = BR * it + c0, c0 % 3, c0 % BR, it + c0 // BR
                pe.wait_ge(xg_ready, c + 1)
                pe.wait_ge(w_loaded[ring], 32 * (turn + 1))
                wait(pe, hid_ready, 2 * (c - 2))
                for j in range(2):
                    last_ = mm(ps[:, HBANKS[r3], j * CH:(j + 1) * CH], wring[:, ring, j * P:(j + 1) * P],
                               xg_cols[:, r3], start=True, stop=True)
                last_.then_inc(hid_done, 1)

            def outputs(c0, it):
                c, r3, ring = BR * it + c0, c0 % 3, c0 % BR
                pe.wait_ge(hid_ready, 2 * (c + 1))
                wait(pe, y_ready, c - 2)
                for s in range(2):
                    for j in range(2):
                        last_ = mm(ps[:, YBANKS[r3], s * D:(s + 1) * D], hid[:, r3, j, s * P:(s + 1) * P],
                                   wring[:, ring, HID + j * D:HID + (j + 1) * D], start=(j == 0), stop=(j == 1))
                last_.then_inc(y_done, 1)

            def all_three(c0, it):
                if not isinstance(it, int) or c0 + 2 < NCH:
                    turn_x(c0 + 2, it)
                if not isinstance(it, int) or c0 + 1 < NCH:
                    hidden(c0 + 1, it)
                outputs(c0, it)

            turn_x(0, 0)
            turn_x(1, 0)
            hidden(0, 0)
            chunks(pe, 2, all_three)


def kernel(**inputs):
    import numpy as np
    import concourse.bacc as bacc
    from concourse.bass_utils import run_bass_kernel_spmd as run

    a = {k: np.asarray(v) for k, v in inputs.items()}
    nb, ch, hh, ww = a["x"].shape
    hp, wp = hh // PATCH, ww // PATCH
    k = ch * PATCH * PATCH
    nk = k // P
    f32 = np.float32

    x = a["x"].reshape(nb, ch, hp, PATCH, wp, PATCH).transpose(0, 1, 3, 5, 2, 4).reshape(nb, nk, P, hp * wp)
    x = x.transpose(0, 2, 1, 3)
    wtok = a["L0_tok_w"].T.reshape(nk, P, D).transpose(1, 0, 2)
    by_feature = lambda w: np.moveaxis(w.reshape((H, HD) + w.shape[1:]), 0, 1).reshape(w.shape)
    wqkv = np.stack([by_feature(a["L0_attn_q_w"]).T, by_feature(a["L0_attn_k_w"]).T, a["L0_attn_v_w"].T], axis=1)
    gh = a["L0_ffn_gw1"].shape[1]
    gw1 = np.zeros((D, P), f32)
    gw1[:, 0:gh] = a["L0_ffn_gw1"]
    gw2 = np.zeros((P, NE), f32)
    gw2[0:gh] = a["L0_ffn_gw2"]
    gb1 = np.zeros(P, f32)
    gb1[0:gh] = a["L0_ffn_gb1"]
    wexp = np.concatenate(
        [a["L0_ffn_we1"], a["L0_ffn_we2"].reshape(NE, 2, P, D).transpose(0, 2, 1, 3).reshape(NE, P, 2 * D),
         a["L0_ffn_be1"].reshape(NE, 2, P).transpose(0, 2, 1)], axis=2)
    cols = np.stack([a["L0_tok_b"], by_feature(a["L0_attn_q_b"]), by_feature(a["L0_attn_k_b"]), gb1], axis=1)
    rows = np.concatenate([a["L0_attn_v_b"]] * 2 + [a["L0_ffn_gb2"]] * 2 + [a["L0_attn_o_b"]] * 2)[None]
    ne = a["L0_attn_edge_index"].shape[1]
    edges = a["L0_attn_edge_index"].reshape(2, P, ne // P).transpose(1, 0, 2)
    attr = np.zeros((ne, 4), f32)
    attr[:, 0:3] = a["L0_attn_edge_attr"]
    ebw = np.concatenate([a["L0_attn_eb_w"].T.reshape(-1), a["L0_attn_eb_b"]])[None]
    nt = nb * N
    region = nt + CH
    nch = -(-((2 * nt + NE * (CH - 1)) // CH) // 3) * 3
    every = lambda r: np.broadcast_to(np.asarray(r, f32)[None], (P, len(r)))
    consts = np.concatenate(
        [np.eye(P, dtype=f32), every(range(NE)), every([e * region for e in range(NE)]), every(range(N)),
         (np.arange(P, dtype=f32) * (ne // P))[:, None], every([CH * c for c in range(nch)])], axis=1)
    import ml_dtypes
    earlier = np.triu(np.ones((HALF, HALF)), 1)
    tri = np.stack([earlier, np.ones((HALF, HALF))], axis=1).astype(ml_dtypes.bfloat16)
    tokens = np.array([[i * N + c * HALF + p + kk * nt for i in range(RING) for c in range(2) for kk in range(2)]
                       for p in range(HALF)], np.uint32)

    nc = bacc.Bacc("TRN2", target_bir_lowering=False, num_devices=1)
    arrays, args = {}, []
    for name, v in (("x", x), ("wtok", wtok), ("wqkv", wqkv), ("wo", a["L0_attn_o_w"].T), ("gw1", gw1), ("gw2", gw2),
                    ("wexp", wexp), ("be2", a["L0_ffn_be2"]), ("cols", cols), ("rows", rows), ("edges", edges),
                    ("attr", attr), ("ebw", ebw), ("consts", consts), ("tri", tri), ("tokens", tokens)):
        v = np.ascontiguousarray(v)
        arrays[name + "_in"] = v
        args.append(nc.dram_tensor(name + "_in", v.shape, mybir.dt.from_np(v.dtype), kind="ExternalInput").ap())
    out = nc.dram_tensor("h_out", (nb, N, D), F32, kind="ExternalOutput").ap()
    vit_block(nc, *args, out)
    r = run(nc, [arrays], core_ids=[0])
    return r.results[0]["h_out"]
```

```python
from contextlib import ExitStack

import concourse.bass as bass
from concourse import mybir

ALU = mybir.AluOpType
ACT = mybir.ActivationFunctionType
F32 = mybir.dt.float32
F32R = mybir.dt.float32r
BF16 = mybir.dt.bfloat16
U32 = mybir.dt.uint32
I32 = mybir.dt.int32
AX_X = mybir.AxisListType.X

P = 128
PATCH = 16
N = 196
HALF = N // 2
D = 128
H = 8
HD = D // H
NE = 8
HID = 256
EPS = 1e-5
RING = 4
FRONT = 15
LAST_LAG = 8
CH = 256
XW = 132
BR = 6
OG = 8
JUNK_ROW = float(1 << 20)
ROW_BIAS, ROW_MAX, ROW_END = 4 * HD, 4 * HD + 2, 4 * HD + 4
ROWS, PROJ, TURNED, S1, S2, PV = 0, 1, 2, 3, 5, 7
HBANKS, YBANKS = (3, 4, 5), (6, 7, 1)


class Image:

    def __init__(self, slot, it, lag, count):
        c = slot - lag
        self.ring = c % RING
        self.turn = it + c // RING
        self.ring2, self.turn2 = c % 2, RING // 2 * it + c // 2
        self.n = RING * it + c
        self.live = not isinstance(self.n, int) or 0 <= self.n < count


def wait(eng, sem, value):
    if not isinstance(value, int) or value > 0:
        eng.wait_ge(sem, value)


def freed(eng, *users):
    for img, sem, value in users:
        if img.live:
            wait(eng, sem, value)
            return


def vit_block(nc, x, wtok, wqkv, wo, gw1, gw2, wexp, be2, cols, rows, edges, attr, ebw, consts, tri,
              tokens, out):
    NB = x.shape[0]
    NK = x.shape[2]
    NT = NB * N
    TILES = 2 * NB
    REGION = NT + CH
    NCH = -(-((2 * NT + NE * (CH - 1)) // CH) // 3) * 3
    TURNS = (NB - 1 - FRONT) // RING
    EJ = edges.shape[2]
    assert (NB - 1 - FRONT) % RING == 0 and TILES % (2 * OG) == 0

    with ExitStack() as ctx:
        def sb(name, shape, dt=F32):
            return ctx.enter_context(nc.sbuf_tensor(name, shape, dt))

        def sem(name):
            return ctx.enter_context(nc.semaphore(name))

        ps = ctx.enter_context(nc.psum_tensor("ps", [P, 8, 512], F32))

        xsort = nc.dram_tensor("xsort", (NE * REGION + CH, XW), F32, kind="Internal").ap()
        ysort = nc.dram_tensor("ysort", (2 * NT, D), F32, kind="Internal").ap()

        wtok_s = sb("wtok_s", [P, NK, D])
        wqkv_s = sb("wqkv_s", [P, 3, D])
        wo_s = sb("wo_s", [P, D])
        gw1_s = sb("gw1_s", [P, D])
        gw2_s = sb("gw2_s", [P, NE])
        cols_s = sb("cols_s", [P, 4])
        vb_s = sb("vb_s", [HALF, 2, D])
        gb2_s = sb("gb2_s", [HALF, 2, NE])
        ob_s = sb("ob_s", [HALF, 2, D])
        power = sb("power", [HALF, 2])
        ebw_s = sb("ebw_s", [HALF, 4, H])
        ident = sb("ident", [P, P])
        expert_no = sb("expert_no", [HALF, NE])
        region_row = sb("region_row", [HALF, NE])
        lower = sb("lower", [HALF, 2, HALF], BF16)

        WW = 2 * HID + 2
        room1 = sb("room1", [P, BR * WW])
        edge_i = room1[:, 0:2 * EJ].bitcast(I32).rearrange("p (a j) -> p a j", a=2)
        edge_f = room1[:, 2 * EJ:4 * EJ].rearrange("p (a j) -> p a j", a=2)
        edge_ok = room1[:, 4 * EJ:8 * EJ].rearrange("p (a j) -> p a j", a=4)
        edge_key = room1[:, 8 * EJ:9 * EJ]
        tok_no = room1[:, 9 * EJ:9 * EJ + N + 1]
        edge_last = room1[:, 10 * EJ + N:10 * EJ + 2 * N]
        halves = room1[:, 10 * EJ + 2 * N:10 * EJ + 2 * N + 5 * N // 2].bitcast(BF16)
        tok_no16 = halves[:, 0:N]
        edge_hit = halves[:, N:3 * N].rearrange("p (a n) -> p a n", a=2)
        edge_last16 = halves[:, 3 * N:5 * N].rearrange("p (a n) -> p a n", a=2)
        last = sb("last", [HALF, 3, 2])
        last_i = sb("last_i", [HALF, 2], U32)
        attr_s = sb("attr_s", [HALF, 2, 4])
        eb = sb("eb", [HALF, 2, H])
        bias_part = sb("bias_part", [H, 2, N], F32R)

        tokens_s = sb("tokens_s", [HALF, 4 * RING], U32)

        patches = sb("patches", [P, 2, NK, N])
        hcols = sb("hcols", [P, N])
        h_all = sb("h_all", [HALF, TILES, D])
        stats = sb("stats", [HALF, 2, 6])
        mv = sb("mv", [HALF, 2, 2])
        var = sb("var", [HALF, 2])
        rstd = sb("rstd", [HALF, 2])
        shift = sb("shift", [HALF, 2])
        xn = sb("xn", [HALF, 2, D])
        sizes = [2 * N, RING * 2 * H * 2 * HD, 4 * 2 * N, 2 * N]
        o = [sum(sizes[:i]) for i in range(5)]
        room2 = sb("room2", [P, max(o[4], 4 * OG * D)])
        xncols = room2[:, o[0]:o[1]].rearrange("p (r n) -> p r n", r=2)
        vaug = room2[0:HALF, o[1]:o[2]].rearrange("p (r c h f) -> p r c h f", r=RING, c=2, h=H)
        probs = room2[0:HALF, o[2]:o[3]].rearrange("p (r c n) -> p r c n", r=4, c=2)
        sums = room2[:, o[3]:o[4]].rearrange("p (g n) -> p g n", g=2)
        parts = sb("parts", [P, 2, 2, 2, N], F32R)
        qside = sb("qside", [P, RING, H, N], F32R)
        kside = sb("kside", [P, RING, H, N], F32R)
        rowmax = sb("rowmax", [HALF, RING, 2 * H])
        negmax = sb("negmax", [2 * H, RING, 2, HALF], F32R)
        rden = sb("rden", [HALF, 2, H])
        att = sb("att", [HALF, 2, H, HD])
        att_cols = sb("att_cols", [P, N])
        stats2 = sb("stats2", [HALF, 2, 6])
        mv2 = sb("mv2", [HALF, 2, 2])
        var2 = sb("var2", [HALF, 2])
        rstd2 = sb("rstd2", [HALF, 2])
        shift2 = sb("shift2", [HALF, 2])
        room3 = sb("room3", [P, max(RING * 4, BR * 2) * XW])
        xs = room3[0:HALF, 0:RING * 4 * XW].rearrange("p (r c k w) -> p r c k w", r=RING, c=2, k=2)
        xs_cols = sb("xs_cols", [P, N])
        gate_h = sb("gate_h", [P, N])
        logits = sb("logits", [HALF, RING, 2, NE])
        top = sb("top", [HALF, RING, 2, NE])
        top_i = sb("top_i", [HALF, 2, NE], U32)
        top_f = sb("top_f", [HALF, 2, 2])
        first_hot = sb("first_hot", [HALF, 2, NE])
        hot = sb("hot", [HALF, 2, NE], BF16)
        base = sb("base", [HALF, RING, 2, NE])
        place = sb("place", [HALF, 2, NE])
        place_one = sb("place_one", [HALF, 4, NE])
        pos = sb("pos", [HALF, 4])
        pos_i = sb("pos_i", [HALF, RING, 4], U32)
        logits_all = sb("logits_all", [HALF, TILES, NE])
        top_all = sb("top_all", [HALF, TILES, 2])
        plan = sb("plan", [1, 6, NE])
        chunk_row = sb("chunk_row", [1, NCH])
        plan_c = sb("plan_c", [1, 5, NCH])
        plan_i = sb("plan_i", [1, 2, NCH], I32)
        fill_i = sb("fill_i", [1, NE], I32)
        count_i = sb("count_i", [1, NE], I32)
        filler = sb("filler", [P, 2, XW])
        xg = room3[:, 0:BR * 2 * XW].rearrange("p (r s w) -> p r s w", r=BR, s=2)
        dest = sb("dest", [P, BR, 2], U32)
        wring = room1[:].rearrange("p (r w) -> p r w", r=BR)
        b2ring = room2[:, 0:BR * D].rearrange("p (r d) -> p r d", r=BR)
        xg_cols = room2[:, BR * D:BR * D + 3 * CH].rearrange("p (r n) -> p r n", r=3)
        hid = room2[:, BR * D + 3 * CH:BR * D + 9 * CH].rearrange("p (r j n) -> p r j n", r=3, j=2)
        ys = patches[:].rearrange("p r k n -> p (r k n)")[:, 0:BR * 2 * D].rearrange(
            "p (r s d) -> p r s d", r=BR, s=2)
        wt = sb("wt", [HALF, TILES, 2])
        psum2 = sb("psum2", [HALF, 3, TILES])
        yin = room2[0:HALF, 0:4 * OG * D].rearrange("p (r k j d) -> p r k j d", r=2, k=2, j=OG)
        res = room1[0:HALF, 0:2 * OG * D].rearrange("p (r j d) -> p r j d", r=2, j=OG)

        c_embed, c_qkv, c_edge, c_misc = sem("c_embed"), sem("c_qkv"), sem("c_edge"), sem("c_misc")
        x_loaded = [sem(f"x_loaded{r}") for r in range(2)]
        sides_in = [sem(f"sides_in{r}") for r in range(RING)]
        max_in = [sem(f"max_in{r}") for r in range(RING)]
        rows_sent = [sem(f"rows_sent{r}") for r in range(RING)]
        memsets, gone_on = sem("memsets"), sem("gone_on")
        edge_step, edge_max, attr_in = sem("edge_step"), sem("edge_max"), sem("attr_in")
        edge_T, bias_T, bias_done, bias_in = sem("edge_T"), sem("bias_T"), sem("bias_done"), sem("bias_in")
        embed_done, hrows_done, xncols_done = sem("embed_done"), sem("hrows_done"), sem("xncols_done")
        qk_done, v_done, s1_done, s2_done, pv_done = (sem(x) for x in ("qk_done", "v_done", "s1_done", "s2_done", "pv_done"))
        max_T, sums_T, att_T, o_done, xs_T, gate1_done, gate2_done, rank_done = (
            sem(x) for x in ("max_T", "sums_T", "att_T", "o_done", "xs_T", "gate1_done", "gate2_done", "rank_done"))
        hcols_ready, h_ready, xncols_ready, high_ready, probs_ready = (
            sem(x) for x in ("hcols_ready", "h_ready", "xncols_ready", "high_ready", "probs_ready"))
        max_high, sums_ready, att_cols_ready, xs_cols_ready, gate_h_ready = (
            sem(x) for x in ("max_high", "sums_ready", "att_cols_ready", "xs_cols_ready", "gate_h_ready"))
        max_ready, max_low, low_ready, v_ready, rden_ready, att_ready = (
            sem(x) for x in ("max_ready", "max_low", "low_ready", "v_ready", "rden_ready", "att_ready"))
        stats_ready, mv_ready, rstd_ready, xn_ready = (sem(x) for x in ("stats_ready", "mv_ready", "rstd_ready", "xn_ready"))
        h2_ready, stats2_ready, mv2_ready, rstd2_ready, xs_ready = (
            sem(x) for x in ("h2_ready", "stats2_ready", "mv2_ready", "rstd2_ready", "xs_ready"))
        logits_ready, top_ready, top_i_ready, top_f_ready, first_ready, hot_ready = (
            sem(x) for x in ("logits_ready", "top_ready", "top_i_ready", "top_f_ready", "first_ready", "hot_ready"))
        place_ready, base_mid, base_ready, pos_f_ready, pos_ready = (
            sem(x) for x in ("place_ready", "base_mid", "base_ready", "pos_f_ready", "pos_ready"))
        var_ready, var2_ready, ob_added = sem("var_ready"), sem("var2_ready"), sem("ob_added")
        shift_ready, shift2_ready = sem("shift_ready"), sem("shift2_ready")
        xs2_ready, dest_in, dest_ready, kept = sem("xs2_ready"), sem("dest_in"), sem("dest_ready"), sem("kept")
        plan_step, plan_ready, filled = sem("plan_step"), sem("plan_ready"), sem("filled")
        xg_loaded = [sem(f"xg_loaded{r}") for r in range(BR)]
        w_loaded = [sem(f"w_loaded{r}") for r in range(BR)]
        y_sent = [sem(f"y_sent{r}") for r in range(BR)]
        dest_kept = sem("dest_kept")
        xg_T, xg_ready, hid_done, hid_ready, y_done, y_ready = (
            sem(x) for x in ("xg_T", "xg_ready", "hid_done", "hid_ready", "y_done", "y_ready"))
        wt_step, wt_exp = sem("wt_step"), sem("wt_exp")
        yin_loaded = [sem(f"yin_loaded{r}") for r in range(2)]
        out_stored = [sem(f"out_stored{r}") for r in range(2)]
        yin_scaled, res_mid, res_ready = sem("yin_scaled"), sem("res_mid"), sem("res_ready")

        block = ctx.enter_context(nc.Block())

        def apart(eng, it):
            if not isinstance(it, int):
                eng.sem_inc(gone_on, 1)

        def slots(eng, slot):
            for t in range(FRONT):
                slot(t, 0)
            if TURNS == 1:
                for u in range(RING):
                    slot(FRONT + u, 0)
            else:
                with eng.Fori(0, TURNS) as it:
                    for u in range(RING):
                        slot(FRONT + u, it)
            for t in range(NB - 1, NB + LAST_LAG):
                slot(t, 0)

        def chunks(eng, ahead, one):
            turns = (NCH - BR - ahead) // BR
            for c in range(BR):
                one(c, 0)
            with eng.Fori(0, turns) as it:
                for u in range(BR):
                    one(BR + u, it)
            for c in range(BR + turns * BR, NCH):
                one(c, 0)

        def tile_rows(n):
            return h_all[:, bass.ds(2 * n, 2), :]

        @block.sync
        def _(sp):
            sp.dma_start(wtok_s[:], wtok).then_inc(c_embed, 16)
            sp.dma_start(cols_s[:], cols).then_inc(c_embed, 16)
            sp.dma_start(patches[:, 0], x[0]).then_inc(x_loaded[0], 16)
            sp.dma_start(ident[:], consts[:, 0:P]).then_inc(c_embed, 16)
            sp.dma_start(wqkv_s[:], wqkv).then_inc(c_qkv, 16)
            sp.dma_start(vb_s[:], rows[0:1, 0:2 * D].to_broadcast([HALF, 2 * D]).rearrange(
                "p (c d) -> p c d", c=2)).then_inc(c_qkv, 16)
            sp.dma_start(wo_s[:], wo).then_inc(c_misc, 16)
            sp.dma_start(gw1_s[:], gw1).then_inc(c_misc, 16)
            sp.dma_start(gw2_s[:], gw2).then_inc(c_misc, 16)
            sp.dma_start(gb2_s[:], rows[0:1, 2 * D:2 * D + 2 * NE].to_broadcast([HALF, 2 * NE]).rearrange(
                "p (c e) -> p c e", c=2)).then_inc(c_misc, 16)
            sp.dma_start(ob_s[:], rows[0:1, 2 * D + 2 * NE:].to_broadcast([HALF, 2 * D]).rearrange(
                "p (c d) -> p c d", c=2)).then_inc(c_misc, 16)
            sp.dma_start(expert_no[:], consts[0:HALF, P:P + NE]).then_inc(c_misc, 16)
            sp.dma_start(region_row[:], consts[0:HALF, P + NE:P + 2 * NE]).then_inc(c_misc, 16)
            sp.dma_start(lower[:], tri).then_inc(c_misc, 16)
            sp.dma_start(chunk_row[:], consts[0:1, P + 2 * NE + N + 1:P + 2 * NE + N + 1 + NCH]).then_inc(c_misc, 16)
            sp.dma_start(tokens_s[:], tokens).then_inc(dest_in, 16)
            sp.wait_ge(memsets, 5)
            sp.dma_start(xsort[NE * REGION:NE * REGION + CH, :].rearrange("(p s) w -> p s w", s=2),
                         filler[:]).then_inc(filled, 16)

            def slot(t, it):
                a, b, c, d = (Image(t, it, lag, NB) for lag in (-1, 1, 3, 0))
                if a.live:
                    wait(sp, embed_done, a.n - 1)
                    apart(sp, it)
                    sp.dma_start(patches[:, a.ring2], x[bass.ds(a.n, 1)].rearrange("o p k n -> p (o k) n")).then_inc(
                        x_loaded[a.ring2], 16)
                if c.live:
                    sp.wait_ge(max_low, c.n + 1)
                    wait(sp, s2_done, H * (c.n - 3))
                    apart(sp, it)
                    for j in range(2):
                        sp.dma_start(
                            qside[ROW_MAX + j:ROW_MAX + j + 1, c.ring].bitcast(F32).rearrange(
                                "o h (c n) -> o (h c) n", c=2),
                            negmax[:, c.ring, j].bitcast(F32).rearrange("p (o n) -> p o n", o=1)).then_inc(
                                max_in[c.ring], 16)
                if b.live:
                    wait(sp, s2_done, H * (b.n - 3))
                    apart(sp, it)
                    for part, ready in ((0, high_ready), (1, low_ready)):
                        sp.wait_ge(ready, 2 * (b.n + 1))
                        apart(sp, it)
                        for side, a, places in ((qside, 0, (2 * part, 2 * part + 1)), (kside, 1, (part, part + 2))):
                            for j in places:
                                sp.dma_start(side[HD * j:HD * (j + 1), b.ring].bitcast(F32),
                                             parts[:, b.ring2, a, part].bitcast(F32).rearrange("p (o n) -> p o n", o=1)
                                             ).then_inc(sides_in[b.ring], 16)

            slots(sp, slot)

            sp.wait_ge(plan_ready, 1)
            for e in range(NE):
                row = sp.value_load(fill_i[0:1, e:e + 1], min_val=0, max_val=NE * REGION - CH)
                sp.dma_start(xsort[bass.ds(row, CH), :].rearrange("(p s) w -> p s w", s=2), filler[:]).then_inc(
                    filled, 16)
            sp.wait_ge(filled, 16 * (NE + 1))
            for r in range(RING):
                sp.wait_ge(rows_sent[r], 64 * len(range(r, NB, RING)))

            def load(c0, it):
                c, ring = BR * it + c0, c0 % BR
                row = sp.value_load(plan_i[0:1, 0, bass.ds(c, 1)], min_val=0, max_val=NE * REGION)
                wait(sp, y_ready, c - BR + 1)
                sp.dma_start(xg[:, ring], xsort[bass.ds(row, CH), :].rearrange("(p s) w -> p s w", s=2)).then_inc(
                    xg_loaded[ring], 16)

            chunks(sp, 0, load)

            for r in range(BR):
                sp.wait_ge(y_sent[r], 32 * len(range(r, NCH, BR)))
            ytiles = ysort.rearrange("(k t p) d -> k p t d", k=2, p=HALF)

            def group(g, r, turn):
                wait(sp, res_ready, g - 1)
                for k in range(2):
                    sp.dma_start(yin[:, r, k], ytiles[k][:, bass.ds(OG * g, OG), :]).then_inc(yin_loaded[r], 16)

            group(0, 0, 0)
            group(1, 1, 0)
            with sp.Fori(1, TILES // OG // 2) as it:
                for r in range(2):
                    group(2 * it + r, r, it)

        @block.gpsimd
        def _(pool):
            nc.gpsimd.memset(qside[4 * HD:P].bitcast(F32), 1.0).then_inc(memsets, 1)
            nc.gpsimd.memset(kside[4 * HD:P].bitcast(F32), 1.0).then_inc(memsets, 1)
            pool.wait_ge(memsets, 2)
            nc.gpsimd.memset(xs[:, :, :, :, D:XW], 0.0).then_inc(memsets, 1)
            nc.gpsimd.memset(filler[:, :, 0:D], 0.0).then_inc(memsets, 1)
            nc.gpsimd.memset(filler[:, :, D:XW].bitcast(U32), int(JUNK_ROW)).then_inc(memsets, 1)
            nc.gpsimd.memset(vaug[:, :, :, :, HD:2 * HD], 1.0).then_inc(memsets, 1)
            pool.wait_ge(dest_in, 16)
            pool.wait_ge(memsets, 3)
            nc.gpsimd.tensor_copy(xs[:, :, :, :, D].bitcast(U32).rearrange("p r c k -> p (r c k)"),
                                  tokens_s[:]).then_inc(dest_ready, 1)
            pool.wait_ge(dest_ready, 1)

            nc.gpsimd.memset(power[:], -0.5).then_inc(memsets, 1)
            pool.wait_ge(memsets, 7)
            pool.wait_ge(c_misc, 144)

            def edge_attributes():
                pool.wait_ge(edge_max, 4)
                for c in range(2):
                    pool.indirect_dma_start(attr_s[:, c, :], None, attr, bass.IndirectOffsetOnAxis(
                        ap=last_i[:, c:c + 1], axis=0)).then_inc(attr_in, 16)

            def rsqrt(out_, shift_, mv_, var_, ready, n, it):
                nc.gpsimd.tensor_scalar(shift_, mv_[:, :, 0], -1.0, None, ALU.mult).then_inc(ready[0], 1)
                nc.gpsimd.tensor_scalar(var_, mv_[:, :, 1], EPS, None, ALU.add).then_inc(ready[0], 1)
                pool.wait_ge(ready[0], 2 * (n + 1))
                apart(pool, it)
                nc.gpsimd.tensor_tensor(out_, var_, power[:], ALU.pow).then_inc(ready[1], 1)
                pool.wait_ge(ready[1], n + 1)
                apart(pool, it)
                nc.gpsimd.tensor_tensor(shift_, shift_, out_, ALU.mult).then_inc(ready[2], 1)

            def slot(t, it):
                i0, i1, i6, i7, i8 = (Image(t, it, lag, NB) for lag in (0, 1, 6, 7, 8))
                if t == 1:
                    edge_attributes()
                if i6.live:
                    pool.wait_ge(mv2_ready, 2 * (i6.n + 1))
                    wait(pool, xs_ready, 2 * i6.n)
                    apart(pool, it)
                    rsqrt(rstd2[:], shift2[:], mv2, var2[:], (var2_ready, rstd2_ready, shift2_ready), i6.n, it)
                if i8.live:
                    pool.wait_ge(pos_ready, i8.n + 1)
                    pool.wait_ge(xs2_ready, 2 * i8.n + 2)
                    apart(pool, it)
                    for c in range(2):
                        for k in range(2):
                            j = 2 * c + k
                            pool.indirect_dma_start(
                                xsort, bass.IndirectOffsetOnAxis(ap=pos_i[:, i8.ring, j:j + 1], axis=0),
                                xs[:, i8.ring, c, k, :], None).then_inc(rows_sent[i8.ring], 16)
                if i1.live:
                    pool.wait_ge(xn_ready, 2 * (i1.n + 1))
                    apart(pool, it)
                    nc.gpsimd.tensor_tensor(tile_rows(i1.n), tile_rows(i1.n), ob_s[:], ALU.add).then_inc(ob_added, 1)
                if i6.live:
                    pool.wait_ge(xs_ready, 2 * (i6.n + 1))
                    wait(pool, rows_sent[i6.ring], 64 * i6.turn)
                    apart(pool, it)
                    nc.gpsimd.tensor_copy(xs[:, i6.ring, :, 1, 0:D], xs[:, i6.ring, :, 0, 0:D]).then_inc(xs2_ready, 1)
                    step = 0.0 if isinstance(i6.n, int) and i6.n < RING else float(RING * N)
                    dest = xs[:, i6.ring, :, :, D].bitcast(U32)
                    nc.gpsimd.tensor_scalar(dest, dest, step, None, ALU.add).then_inc(xs2_ready, 1)
                if i7.live:
                    pool.wait_ge(top_ready, 2 * (i7.n + 1))
                    apart(pool, it)
                    nc.gpsimd.tensor_copy(logits_all[:, bass.ds(2 * i7.n, 2), :], logits[:, i7.ring]).then_inc(kept, 1)
                    nc.gpsimd.tensor_copy(top_all[:, bass.ds(2 * i7.n, 2), :], top[:, i7.ring, :, 0:2]).then_inc(
                        kept, 1)
                if i0.live:
                    pool.wait_ge(mv_ready, 2 * (i0.n + 1))
                    wait(pool, xn_ready, 2 * i0.n)
                    apart(pool, it)
                    rsqrt(rstd[:], shift[:], mv, var[:], (var_ready, rstd_ready, shift_ready), i0.n, it)

            slots(pool, slot)

            def send(c0, it):
                c, ring = BR * it + c0, c0 % BR
                pool.wait_ge(y_ready, c + 1)
                pool.wait_ge(dest_kept, c + 1)
                apart(pool, it)
                for s in range(2):
                    pool.indirect_dma_start(
                        ysort, bass.IndirectOffsetOnAxis(ap=dest[:, ring, s:s + 1], axis=0),
                        ys[:, ring, s, :], None, bounds_check=2 * NT - 1, oob_is_err=False).then_inc(y_sent[ring], 16)

            chunks(pool, 0, send)

        @block.scalar
        def _(act):
            act.dma_start(edge_i, edges).then_inc(c_edge, 16)
            act.dma_start(tok_no, consts[:, P + 2 * NE:P + 2 * NE + N + 1]).then_inc(c_edge, 16)
            act.dma_start(ebw_s[:], ebw[0:1, :].to_broadcast([HALF, 4 * H]).rearrange(
                "p (j h) -> p j h", j=4)).then_inc(c_edge, 16)
            act.wait_ge(c_embed, 48)

            def bias_rows():
                act.wait_ge(bias_T, 1)
                nc.scalar.activation(bias_part[:, 0], ps[0:H, TURNED, 0:N], ACT.Copy).then_inc(bias_done, 1)
                act.wait_ge(bias_done, 2)
                act.wait_ge(memsets, 6)
                for r in range(RING):
                    for j in range(2):
                        act.dma_start(kside[ROW_BIAS + j:ROW_BIAS + j + 1, r].bitcast(F32),
                                      bias_part[:, j].bitcast(F32).rearrange("p (o n) -> p o n", o=1)
                                      ).then_inc(bias_in, 16)

            def normed(img, it, out_, rstd_, shift_, sems):
                act.wait_ge(sems[0], img.n + 1)
                apart(act, it)
                for c in range(2):
                    nc.scalar.activation(out_(c), h_all[:, bass.ds(2 * img.n + c, 1), :].rearrange("p o d -> p (o d)"),
                                         ACT.Identity, bias=shift_[:, c:c + 1], scale=rstd_[:, c:c + 1]).then_inc(
                                             sems[1], 1)

            def slot(t, it):
                i0, i1, i2, i3, i4, i5, i6 = (Image(t, it, lag, NB) for lag in range(7))
                if t == 1:
                    bias_rows()
                for s in range(H):
                    if s == 0 and i5.live:
                        act.wait_ge(pv_done, H * (i5.n + 1))
                        wait(act, sums_T, i5.n)
                        nc.scalar.activation(sums[:], ps[:, PV, 0:2 * N].rearrange("p (g n) -> p g n", g=2),
                                             ACT.Copy).then_inc(sums_ready, 1)
                    if s == 0 and i1.live:
                        wait(act, xncols_done, i1.n)
                        normed(i1, it, lambda c: xn[:, c], rstd, shift, (shift_ready, xn_ready))
                    if s == 1 and i6.live:
                        wait(act, rows_sent[i6.ring], 64 * i6.turn)
                        normed(i6, it, lambda c: xs[:, i6.ring, c, 0, 0:D], rstd2, shift2, (shift2_ready, xs_ready))
                    if s == 2 and i1.live:
                        act.wait_ge(xncols_done, i1.n + 1)
                        wait(act, v_done, i1.n - 1)
                        nc.scalar.activation(xncols[:, i1.ring2], ps[:, TURNED, 0:N], ACT.Copy).then_inc(
                            xncols_ready, 1)
                    if s == 2 and i0.live:
                        act.wait_ge(embed_done, i0.n + 1)
                        wait(act, hrows_done, i0.n)
                        nc.scalar.activation(hcols[:], ps[:, ROWS, 0:N], ACT.Identity, bias=cols_s[:, 0:1]).then_inc(
                            hcols_ready, 1)
                    if s == 3 and i6.live:
                        act.wait_ge(xs_T, i6.n + 1)
                        wait(act, gate1_done, i6.n)
                        nc.scalar.activation(xs_cols[:], ps[:, TURNED, 0:N], ACT.Copy).then_inc(xs_cols_ready, 1)
                    if s == 3 and i3.live:
                        act.wait_ge(max_T, i3.n + 1)
                        wait(act, max_in[i3.ring], 32 * i3.turn)
                        nc.scalar.activation(negmax[:, i3.ring, 0], ps[0:2 * H, ROWS, 0:HALF], ACT.Copy,
                                             scale=-1.0).then_inc(max_high, 1)
                    if s == 4 and i5.live:
                        act.wait_ge(att_T, i5.n + 1)
                        wait(act, o_done, i5.n)
                        nc.scalar.activation(att_cols[:], ps[:, TURNED, 0:N], ACT.Copy).then_inc(att_cols_ready, 1)
                    if s == 4 and i1.live:
                        act.wait_ge(qk_done, i1.n + 1)
                        if i3.live:
                            act.wait_ge(sides_in[i3.ring], 128 * (i3.turn + 1))
                        for a in range(2):
                            nc.scalar.activation(parts[:, i1.ring2, a, 0], ps[:, PROJ, a * N:(a + 1) * N],
                                                 ACT.Identity, bias=cols_s[:, 1 + a:2 + a]).then_inc(high_ready, 1)
                    if s == 5 and i0.live:
                        act.wait_ge(hrows_done, i0.n + 1)
                        apart(act, it)
                        nc.scalar.activation(tile_rows(i0.n), ps[0:HALF, ROWS, 0:2 * D].rearrange(
                            "p (c d) -> p c d", c=2), ACT.Copy).then_inc(h_ready, 1)
                    if s == 7 and i6.live:
                        act.wait_ge(gate1_done, i6.n + 1)
                        wait(act, gate2_done, i6.n)
                        nc.scalar.activation(gate_h[:], ps[:, ROWS, 0:N], ACT.Relu, bias=cols_s[:, 3:4]).then_inc(
                            gate_h_ready, 1)
                    img, h = (i3, 0) if s == 7 else (i4, s + 1)
                    if img.live:
                        act.wait_ge(s2_done, H * img.n + h + 1)
                        wait(act, pv_done, H * img.n + h - 3)
                        nc.scalar.activation(probs[:, h % 4], ps[0:HALF, S2 + h % 2, 0:2 * N], ACT.Exp,
                                             scale=float(HD) ** -0.5).then_inc(probs_ready, 1)

            slots(act, slot)

            act.wait_ge(wt_step, 2)
            nc.scalar.activation(logits_all[:], logits_all[:], ACT.Exp).then_inc(wt_exp, 1)
            nc.scalar.activation(psum2[:, 0], psum2[:, 0], ACT.Exp).then_inc(wt_exp, 1)
            act.wait_ge(wt_step, 6)
            nc.scalar.activation(psum2[:, 1], psum2[:, 1], ACT.Exp).then_inc(wt_exp, 1)

            AHEAD = 4

            def load(c0, it):
                c, ring = BR * it + c0, c0 % BR
                e = act.value_load(plan_i[0:1, 1, bass.ds(c, 1)], min_val=0, max_val=NE - 1)
                wait(act, y_ready, c - BR + 1)
                act.dma_start(wring[:, ring], wexp[bass.ds(e, 1)].rearrange("o p w -> p (o w)")).then_inc(
                    w_loaded[ring], 16)
                act.dma_start(b2ring[:, ring], be2[bass.ds(e, 1), :].to_broadcast([P, D])).then_inc(
                    w_loaded[ring], 16)

            def gelu(c0, it):
                c, r3, ring = BR * it + c0, c0 % 3, c0 % BR
                act.wait_ge(hid_done, c + 1)
                wait(act, y_done, c - 2)
                for j in range(2):
                    nc.scalar.activation(hid[:, r3, j], ps[:, HBANKS[r3], j * CH:(j + 1) * CH], ACT.Gelu,
                                         bias=wring[:, ring, 2 * HID + j:2 * HID + j + 1]).then_inc(hid_ready, 1)
                if not isinstance(it, int) or c0 + AHEAD < NCH:
                    load(c0 + AHEAD, it)

            act.wait_ge(plan_ready, 1)
            for r in range(RING):
                act.wait_ge(rows_sent[r], 64 * len(range(r, NB, RING)))
            for c in range(AHEAD):
                load(c, 0)
            chunks(act, AHEAD, gelu)

            otiles = out.rearrange("b (c p) d -> p (b c) d", p=HALF)

            GROUPS = TILES // OG

            def scale(g, r, turn):
                act.wait_ge(yin_loaded[r], 32 * (turn + 1))
                for j in range(OG):
                    nc.scalar.activation(yin[:, r, 1, j], yin[:, r, 1, j], ACT.Copy, scale=wt[:, bass.ds(
                        OG * g + j, 1), 1:2].rearrange("p o k -> p (o k)")).then_inc(yin_scaled, 1)

            def store(g, r):
                act.wait_ge(res_ready, g + 1)
                act.dma_start(otiles[:, bass.ds(OG * g, OG), :], res[:, r]).then_inc(out_stored[r], 16)

            act.wait_ge(wt_step, 9)
            scale(0, 0, 0)
            with act.Fori(0, GROUPS // 2 - 1) as it:
                for u in range(2):
                    scale(2 * it + 1 + u, 1 - u, it + u)
                    store(2 * it + u, u)
            scale(GROUPS - 1, 1, GROUPS // 2 - 1)
            store(GROUPS - 2, 0)
            store(GROUPS - 1, 1)
            for r in range(2):
                act.wait_ge(out_stored[r], 16 * (TILES // OG // 2))

        @block.vector
        def _(dve):
            v = nc.vector
            dve.wait_ge(c_edge, 48)
            v.tensor_copy(edge_f, edge_i).then_inc(edge_step, 1)
            v.tensor_copy(tok_no16, tok_no[:, 0:N]).then_inc(edge_step, 1)
            v.memset(edge_last16, 0.0).then_inc(edge_step, 1)
            dve.wait_ge(edge_step, 3)
            for j in range(2):
                v.tensor_scalar(edge_ok[:, j], edge_f[:, j], 0.0, None, ALU.is_ge).then_inc(edge_step, 1)
            dve.wait_ge(edge_step, 5)
            for j in range(2):
                v.scalar_tensor_tensor(edge_ok[:, 2 + j], edge_f[:, j], float(N), edge_ok[:, j],
                                       ALU.is_lt, ALU.mult).then_inc(edge_step, 1)
            dve.wait_ge(edge_step, 7)
            v.tensor_tensor(edge_ok[:, 0], edge_ok[:, 2], edge_ok[:, 3], ALU.mult).then_inc(edge_step, 1)
            dve.wait_ge(edge_step, 8)
            v.tensor_tensor(edge_key, edge_ok[:, 0], tok_no[:, 1:EJ + 1], ALU.mult).then_inc(edge_step, 1)
            dve.wait_ge(edge_step, 9)
            for j in range(EJ):
                if j:
                    dve.wait_ge(edge_step, 8 + 2 * j)
                v.tensor_scalar(edge_hit[:, j % 2], tok_no16, edge_f[:, 1, j:j + 1], edge_key[:, j:j + 1],
                                ALU.is_equal, ALU.mult).then_inc(edge_step, 1)
                dve.wait_ge(edge_step, 10 + 2 * j)
                v.tensor_tensor(edge_last16[:, (j + 1) % 2], edge_last16[:, j % 2], edge_hit[:, j % 2],
                                ALU.max).then_inc(edge_step, 1)
            es = 9 + 2 * EJ
            dve.wait_ge(edge_step, es)
            v.tensor_scalar(edge_last, edge_last16[:, EJ % 2], 0.0, tok_no[:, N:N + 1], ALU.is_gt, ALU.mult).then_inc(
                edge_step, 1)
            dve.wait_ge(edge_step, es + 1)
            v.tensor_tensor(edge_last, edge_last, edge_last16[:, EJ % 2], ALU.add).then_inc(edge_T, 1)
            dve.wait_ge(c_misc, 144)
            v.tensor_copy(base[:, 0, 0], region_row[:]).then_inc(base_ready, 1)

            def attend(img):
                dve.wait_ge(sums_T, img.n + 1)
                wait(dve, att_T, img.n)
                four = ps[0:HALF, PROJ, :].rearrange("p (c h f) -> p c h f", c=2, h=H)
                v.reciprocal(rden[:], four[:, :, :, HD]).then_inc(rden_ready, 1)
                dve.wait_ge(rden_ready, img.n + 1)
                for c in range(2):
                    v.tensor_tensor(att[:, c], four[:, c, :, 0:HD],
                                    rden[:, c].rearrange("p (h o) -> p h o", o=1).to_broadcast([HALF, H, HD]),
                                    ALU.mult).then_inc(att_ready, 1)

            def norm_stats(img, it, sems, s_, m_):
                apart(dve, it)
                for c in range(2):
                    v.bn_stats(s_[:, c], h_all[:, bass.ds(2 * img.n + c, 1), :].rearrange("p o d -> p (o d)")).then_inc(
                        sems[0], 1)
                dve.wait_ge(sems[0], 2 * (img.n + 1))
                apart(dve, it)
                for c in range(2):
                    v.bn_aggr(m_[:, c], s_[:, c]).then_inc(sems[1], 1)

            def column_bias():
                dve.wait_ge(edge_T, 2)
                v.tensor_reduce(last[:, 0], ps[0:HALF, TURNED, 0:2 * P].rearrange("p (c e) -> p c e", c=2),
                                AX_X, ALU.max).then_inc(edge_max, 1)
                dve.wait_ge(edge_max, 1)
                v.tensor_scalar(last[:, 1], last[:, 0], 1.0, 4.0, ALU.is_ge, ALU.mult).then_inc(edge_max, 1)
                v.tensor_scalar(last[:, 2], last[:, 0], -1.0, 0.0, ALU.add, ALU.max).then_inc(edge_max, 1)
                dve.wait_ge(edge_max, 3)
                v.tensor_copy(last_i[:], last[:, 2]).then_inc(edge_max, 1)
                dve.wait_ge(attr_in, 32)
                for c in range(2):
                    for j in range(3):
                        v.scalar_tensor_tensor(eb[:, c], ebw_s[:, j], attr_s[:, c, j:j + 1],
                                               ebw_s[:, 3] if j == 0 else eb[:, c], ALU.mult, ALU.add).then_inc(
                                                   edge_max, 1)
                        dve.wait_ge(edge_max, 5 + 4 * c + j)
                    v.tensor_scalar(eb[:, c], eb[:, c], last[:, 1, c:c + 1], None, ALU.mult).then_inc(edge_max, 1)
                dve.wait_ge(bias_done, 1)
                v.tensor_tensor(bias_part[:, 1], ps[0:H, TURNED, 0:N], bias_part[:, 0].bitcast(F32),
                                ALU.subtract).then_inc(bias_done, 1)

            def slot(t, it):
                i0, i1, i2, i3, i4, i5, i6, i7 = (Image(t, it, lag, NB) for lag in range(8))
                if t == 1:
                    column_bias()
                for s in range(H):
                    if s == 0 and i3.live:
                        dve.wait_ge(v_done, i3.n + 1)
                        wait(dve, pv_done, H * (i3.n - 3))
                        v.tensor_tensor(vaug[:, i3.ring, :, :, 0:HD], ps[0:HALF, PROJ, 0:2 * D].rearrange(
                            "p (c h d) -> p c h d", c=2, h=H), vb_s[:].rearrange("p c (h d) -> p c h d", h=H),
                            ALU.add).then_inc(v_ready, 1)
                    if s == 1 and i7.live:
                        dve.wait_ge(gate2_done, i7.n + 1)
                        wait(dve, kept, 2 * (i7.n - 3))
                        v.tensor_tensor(logits[:, i7.ring], ps[0:HALF, S1, 2 * N:2 * N + 2 * NE].rearrange(
                            "p (c e) -> p c e", c=2), gb2_s[:], ALU.add).then_inc(logits_ready, 1)
                    if s == 2 and i5.live:
                        attend(i5)
                    if s == 2 and i7.live:
                        dve.wait_ge(logits_ready, i7.n + 1)
                        apart(dve, it)
                        for c in range(2):
                            v.max(top[:, i7.ring, c], logits[:, i7.ring, c]).then_inc(top_ready, 1)
                        dve.wait_ge(top_ready, 2 * (i7.n + 1))
                        apart(dve, it)
                        for c in range(2):
                            v.max_index(top_i[:, c], top[:, i7.ring, c], logits[:, i7.ring, c]).then_inc(top_i_ready, 1)
                        dve.wait_ge(top_i_ready, 2 * (i7.n + 1))
                        v.tensor_copy(top_f[:], top_i[:, :, 0:2]).then_inc(top_f_ready, 1)
                    if s == 3 and i7.live:
                        dve.wait_ge(top_f_ready, i7.n + 1)
                        wait(dve, rank_done, i7.n)
                        for c in range(2):
                            v.tensor_scalar(first_hot[:, c], expert_no[:], top_f[:, c, 0:1], None,
                                            ALU.is_equal).then_inc(first_ready, 1)
                        for c in range(2):
                            dve.wait_ge(first_ready, 2 * i7.n + 1 + c)
                            v.scalar_tensor_tensor(hot[:, c], expert_no[:], top_f[:, c, 1:2], first_hot[:, c],
                                                   ALU.is_equal, ALU.add).then_inc(hot_ready, 1)
                    if s == 4 and i3.live:
                        dve.wait_ge(max_high, i3.n + 1)
                        v.scalar_tensor_tensor(negmax[:, i3.ring, 1], ps[0:2 * H, ROWS, 0:HALF], -1.0,
                                               negmax[:, i3.ring, 0].bitcast(F32), ALU.mult, ALU.subtract).then_inc(
                                                   max_low, 1)
                    if s == 5 and i1.live:
                        dve.wait_ge(high_ready, 2 * (i1.n + 1))
                        for a in range(2):
                            v.scalar_tensor_tensor(parts[:, i1.ring2, a, 1], ps[:, PROJ, a * N:(a + 1) * N],
                                                   cols_s[:, 1 + a:2 + a], parts[:, i1.ring2, a, 0].bitcast(F32),
                                                   ALU.add, ALU.subtract).then_inc(low_ready, 1)
                    if s == 5 and i7.live:
                        n, r = i7.n, i7.ring
                        ranks = ps[0:HALF, S1, 2 * N:2 * N + 4 * NE].rearrange("p (a e) -> p a e", a=4)
                        dve.wait_ge(rank_done, n + 1)
                        dve.wait_ge(base_ready, n + 1)
                        v.tensor_tensor(place[:, 0], ranks[:, 0], base[:, r, 0], ALU.add).then_inc(place_ready, 1)
                        v.tensor_tensor(base[:, r, 1], ranks[:, 2], base[:, r, 0], ALU.add).then_inc(base_mid, 1)
                        dve.wait_ge(base_mid, n + 1)
                        v.tensor_tensor(place[:, 1], ranks[:, 1], base[:, r, 1], ALU.add).then_inc(place_ready, 1)
                        v.tensor_tensor(base[:, (r + 1) % RING, 0], ranks[:, 3], base[:, r, 1],
                                        ALU.add).then_inc(base_ready, 1)
                    if s == 6 and i5.live:
                        dve.wait_ge(o_done, i5.n + 1)
                        dve.wait_ge(ob_added, i5.n + 1)
                        v.tensor_tensor(tile_rows(i5.n), ps[0:HALF, TURNED, 0:2 * D].rearrange(
                            "p (c d) -> p c d", c=2), tile_rows(i5.n), ALU.add).then_inc(h2_ready, 1)
                    if s == 6 and i0.live:
                        dve.wait_ge(h_ready, i0.n + 1)
                        wait(dve, shift_ready, i0.n)
                        norm_stats(i0, it, (stats_ready, mv_ready), stats, mv)
                    if s == 7 and i5.live:
                        dve.wait_ge(h2_ready, i5.n + 1)
                        wait(dve, shift2_ready, i5.n)
                        norm_stats(i5, it, (stats2_ready, mv2_ready), stats2, mv2)
                    if s == 7 and i7.live:
                        n, r = i7.n, i7.ring
                        for c in range(2):
                            dve.wait_ge(place_ready, 2 * n + 1 + c)
                            for k in range(2):
                                j = 2 * c + k
                                v.scalar_tensor_tensor(place_one[:, j], expert_no[:], top_f[:, c, k:k + 1], place[:, c],
                                                       ALU.is_equal, ALU.mult, accum_out=pos[:, j:j + 1]).then_inc(
                                                           pos_f_ready, 1)
                        dve.wait_ge(pos_f_ready, 4 * (n + 1))
                        wait(dve, rows_sent[r], 64 * i7.turn)
                        v.tensor_copy(pos_i[:, r], pos[:]).then_inc(pos_ready, 1)
                    img, h = (i2, s - 2) if s >= 2 else (i3, s + 6)
                    if img.live:
                        dve.wait_ge(s1_done, H * img.n + h + 1)
                        v.tensor_reduce(rowmax[:, img.ring, 2 * h:2 * h + 2],
                                        ps[0:HALF, S1 + s % 2, 0:2 * N].rearrange("p (c n) -> p c n", c=2),
                                        AX_X, ALU.max).then_inc(max_ready, 1)

            slots(dve, slot)

            steps = [0]

            def step(ins):
                steps[0] += 1
                ins.then_inc(plan_step, 1)
                dve.wait_ge(plan_step, steps[0])

            fin = base[0:1, NB % RING, 0]
            dve.wait_ge(base_ready, NB + 1)
            count, rounded, ends, ones = (plan[:, i] for i in range(4))
            step(v.tensor_tensor(count, fin, region_row[0:1], ALU.subtract))
            step(v.tensor_scalar(count, count, float(CH - 1), None, ALU.add))
            step(v.tensor_copy(count_i[:], count))
            step(v.tensor_scalar(count_i[:], count_i[:], 8, 8, ALU.logical_shift_right, ALU.logical_shift_left))
            step(v.tensor_copy(rounded, count_i[:]))
            step(v.memset(ones, 1.0))
            step(v.tensor_tensor_scan(ends, ones, rounded, 0.0, ALU.mult, ALU.add))
            expert, start, passed, row, live_ = (plan_c[:, i] for i in range(5))
            step(v.memset(plan_c[:], 0.0))
            for e in range(NE):
                step(v.scalar_tensor_tensor(expert, chunk_row[:], ends[:, e:e + 1], expert, ALU.is_ge, ALU.add))
                step(v.tensor_scalar(passed, chunk_row[:], ends[:, e:e + 1], rounded[:, e:e + 1], ALU.is_ge, ALU.mult))
                step(v.tensor_tensor(start, start, passed, ALU.add))
            step(v.tensor_scalar(live_, expert, float(NE), None, ALU.is_lt))
            step(v.tensor_tensor(row, chunk_row[:], start, ALU.subtract))
            step(v.tensor_tensor(row, row, live_, ALU.mult))
            step(v.scalar_tensor_tensor(row, expert, float(REGION), row, ALU.mult, ALU.add))
            step(v.tensor_scalar(expert, expert, float(NE - 1), None, ALU.min))
            step(v.tensor_copy(plan_i[:, 0], row))
            step(v.tensor_copy(plan_i[:, 1], expert))
            v.tensor_copy(fill_i[:], fin).then_inc(plan_ready, 1)

            dve.wait_ge(kept, 2 * NB)
            best = top_all[:, :, 0:1]
            v.tensor_tensor(logits_all[:], logits_all[:], best.to_broadcast([HALF, TILES, NE]),
                            ALU.subtract).then_inc(wt_step, 1)
            v.tensor_tensor(psum2[:, 0], top_all[:, :, 1], top_all[:, :, 0], ALU.subtract).then_inc(wt_step, 1)
            dve.wait_ge(wt_exp, 2)
            v.tensor_reduce(psum2[:, 2], logits_all[:], AX_X, ALU.add).then_inc(wt_step, 1)
            dve.wait_ge(wt_step, 3)
            v.reciprocal(psum2[:, 1], psum2[:, 2]).then_inc(wt_step, 1)
            dve.wait_ge(wt_step, 4)
            v.tensor_tensor(psum2[:, 0], psum2[:, 0], psum2[:, 1], ALU.mult).then_inc(wt_step, 1)
            dve.wait_ge(wt_step, 5)
            v.tensor_tensor(psum2[:, 1], psum2[:, 0], psum2[:, 1], ALU.subtract).then_inc(wt_step, 1)
            dve.wait_ge(wt_exp, 3)
            v.tensor_scalar(psum2[:, 2], psum2[:, 1], 1.0, None, ALU.add).then_inc(wt_step, 1)
            dve.wait_ge(wt_step, 7)
            v.reciprocal(wt[:, :, 0], psum2[:, 2]).then_inc(wt_step, 1)
            dve.wait_ge(wt_step, 8)
            v.tensor_tensor(wt[:, :, 1], psum2[:, 1], wt[:, :, 0], ALU.mult).then_inc(wt_step, 1)

            def turned(c0, it):
                c, ring, turn = BR * it + c0, c0 % BR, it + c0 // BR
                dve.wait_ge(xg_T, c + 1)
                wait(dve, hid_done, c - 2)
                v.tensor_copy(xg_cols[:, c0 % 3], ps[:, ROWS, 0:CH]).then_inc(xg_ready, 1)
                wait(dve, y_sent[ring], 32 * turn)
                v.tensor_copy(dest[:, ring], xg[:, ring, :, D].bitcast(U32)).then_inc(dest_kept, 1)

            def biased(c0, it):
                c, r3, ring = BR * it + c0, c0 % 3, c0 % BR
                dve.wait_ge(y_done, c + 1)
                b2 = b2ring[:, ring:ring + 1, :].to_broadcast([P, 2, D])
                v.tensor_tensor(ys[:, ring], ps[:, YBANKS[r3], 0:2 * D].rearrange("p (s d) -> p s d", s=2), b2,
                                ALU.add).then_inc(y_ready, 1)

            def both(c0, it):
                if not isinstance(it, int) or c0 + 2 < NCH:
                    turned(c0 + 2, it)
                biased(c0, it)

            turned(0, 0)
            turned(1, 0)
            chunks(dve, 2, both)

            def group(g, r, turn):
                dve.wait_ge(yin_loaded[r], 32 * (turn + 1))
                wait(dve, out_stored[r], 16 * turn)
                for j in range(OG):
                    i = OG * g + j
                    v.scalar_tensor_tensor(res[:, r, j], yin[:, r, 0, j],
                                           wt[:, bass.ds(i, 1), 0:1].rearrange("p o k -> p (o k)"),
                                           h_all[:, bass.ds(i, 1), :].rearrange("p o d -> p (o d)"),
                                           ALU.mult, ALU.add).then_inc(res_mid, 1)
                dve.wait_ge(res_mid, OG * (g + 1))
                dve.wait_ge(yin_scaled, OG * (g + 1))
                v.tensor_tensor(res[:, r], res[:, r], yin[:, r, 1], ALU.add).then_inc(res_ready, 1)

            dve.wait_ge(wt_step, 9)
            group(0, 0, 0)
            group(1, 1, 0)
            with dve.Fori(1, TILES // OG // 2) as it:
                for r in range(2):
                    group(2 * it + r, r, it)

        @block.tensor
        def _(pe):
            mm, tr = nc.tensor.matmul, nc.tensor.transpose

            def edge_turn():
                pe.wait_ge(c_embed, 48)
                pe.wait_ge(edge_T, 1)
                for c in range(2):
                    last_ = tr(ps[0:HALF, TURNED, c * P:(c + 1) * P], edge_last[:, c * HALF:(c + 1) * HALF], ident[:])
                last_.then_inc(edge_T, 1)
                pe.wait_ge(edge_max, 12)
                for c in range(2):
                    last_ = tr(ps[0:H, TURNED, c * HALF:(c + 1) * HALF], eb[:, c], ident[0:HALF, 0:HALF])
                last_.then_inc(bias_T, 1)

            def slot(t, it):
                i0, i1, i2, i3, i4, i5, i6, i7, i8 = (Image(t, it, lag, NB) for lag in range(9))
                if t == 0:
                    pe.wait_ge(c_embed, 48)
                if t == 1:
                    edge_turn()
                    pe.wait_ge(c_qkv, 32)
                if t == 2:
                    pe.wait_ge(bias_in, 16 * 2 * RING)
                if t == 5:
                    pe.wait_ge(c_misc, 144)
                for s in range(H):
                    if s == 1 and i1.live:
                        pe.wait_ge(xn_ready, 2 * (i1.n + 1))
                        freed(pe, (i6, h2_ready, i6.n + 1), (i2, xncols_ready, i2.n + 1))
                        for c in range(2):
                            last_ = tr(ps[:, TURNED, c * HALF:(c + 1) * HALF], xn[:, c], ident[0:HALF, 0:HALF])
                        last_.then_inc(xncols_done, 1)
                    if s == 1 and i5.live:
                        pe.wait_ge(sums_ready, i5.n + 1)
                        freed(pe, (i3, v_ready, i3.n + 1), (i6, att_ready, 2 * (i6.n + 1)))
                        for c in range(2):
                            for g in range(2):
                                last_ = tr(ps[0:HALF, PROJ, (2 * c + g) * P:(2 * c + g + 1) * P],
                                           sums[:, g, c * HALF:(c + 1) * HALF], ident[:])
                        last_.then_inc(sums_T, 1)
                    img, h = (i2, s - 2) if s >= 2 else (i3, s + 6)
                    if img.live:
                        wait(pe, max_ready, H * img.n + h - 1)
                        if s == 2 and i7.live:
                            pe.wait_ge(logits_ready, i7.n + 1)
                        if s == 6 and i7.live:
                            pe.wait_ge(place_ready, 2 * (i7.n + 1))
                            pe.wait_ge(base_ready, i7.n + 2)
                    elif s in (0, 4) and i7.live:
                        pe.wait_ge(max_ready, H * NB)
                    if s == 0 and i7.live:
                        pe.wait_ge(gate_h_ready, i7.n + 1)
                        if not img.live:
                            freed(pe, (i8, base_ready, i8.n + 2))
                            freed(pe, (i8, place_ready, 2 * (i8.n + 1)))
                        for c in range(2):
                            last_ = mm(ps[0:HALF, S1, 2 * N + c * NE:2 * N + (c + 1) * NE],
                                       gate_h[:, c * HALF:(c + 1) * HALF], gw2_s[:], start=True, stop=True)
                        last_.then_inc(gate2_done, 1)
                    if s == 4 and i7.live:
                        pe.wait_ge(hot_ready, 2 * (i7.n + 1))
                        for a in range(2):
                            last_ = mm(ps[0:HALF, S1, 2 * N + 2 * NE * a:2 * N + 2 * NE * (a + 1)], lower[:, a],
                                       hot[:].rearrange("p c e -> p (c e)"), start=True, stop=True)
                        last_.then_inc(rank_done, 1)
                    if img.live:
                        if h == 0:
                            pe.wait_ge(sides_in[img.ring], 128 * (img.turn + 1))
                        for c in range(2):
                            last_ = mm(ps[0:HALF, S1 + s % 2, c * N:(c + 1) * N],
                                       qside[0:ROW_MAX, img.ring, h, c * HALF:(c + 1) * HALF],
                                       kside[0:ROW_MAX, img.ring, h, :], start=True, stop=True)
                        last_.then_inc(s1_done, 1)
                    img, h = (i3, 0) if s == 7 else (i4, s + 1)
                    if img.live:
                        if h == 0:
                            pe.wait_ge(max_in[img.ring], 32 * (img.turn + 1))
                        wait(pe, probs_ready, H * img.n + h - 1)
                        for c in range(2):
                            last_ = mm(ps[0:HALF, S2 + h % 2, c * N:(c + 1) * N],
                                       kside[0:ROW_END, img.ring, h, c * HALF:(c + 1) * HALF],
                                       qside[0:ROW_END, img.ring, h, :], start=True, stop=True)
                        last_.then_inc(s2_done, 1)
                    if s in (0, 1) and i0.live:
                        if s == 0:
                            pe.wait_ge(x_loaded[i0.ring2], 16 * (i0.turn2 + 1))
                            freed(pe, (i7, gate_h_ready, i7.n + 1), (i1, h_ready, i1.n + 1))
                        for k in range(s * NK // 2, (s + 1) * NK // 2):
                            last_ = mm(ps[:, ROWS, 0:N], wtok_s[:, k], patches[:, i0.ring2, k], start=(k == 0),
                                       stop=(k == NK - 1))
                        if s == 1:
                            last_.then_inc(embed_done, 1)
                    if s == 3 and i1.live:
                        pe.wait_ge(xncols_ready, i1.n + 1)
                        freed(pe, (i5, att_ready, 2 * (i5.n + 1)), (i3, v_ready, i3.n + 1),
                              (i2, low_ready, 2 * (i2.n + 1)))
                        for a in range(2):
                            last_ = mm(ps[:, PROJ, a * N:(a + 1) * N], wqkv_s[:, a], xncols[:, i1.ring2], start=True,
                                       stop=True)
                        last_.then_inc(qk_done, 1)
                    if s == 5 and i5.live:
                        pe.wait_ge(att_cols_ready, i5.n + 1)
                        for c in range(2):
                            last_ = mm(ps[0:HALF, TURNED, c * D:(c + 1) * D], att_cols[:, c * HALF:(c + 1) * HALF],
                                       wo_s[:], start=True, stop=True)
                        last_.then_inc(o_done, 1)
                    if s == 6 and i6.live:
                        pe.wait_ge(xs_cols_ready, i6.n + 1)
                        freed(pe, (i0, h_ready, i0.n + 1), (i3, max_low, i3.n + 1), (i7, gate_h_ready, i7.n + 1))
                        mm(ps[:, ROWS, 0:N], gw1_s[:], xs_cols[:], start=True, stop=True).then_inc(gate1_done, 1)
                    if s == 7 and i2.live:
                        freed(pe, (i1, low_ready, 2 * (i1.n + 1)), (i5, att_ready, 2 * (i5.n + 1)))
                        for c in range(2):
                            last_ = mm(ps[0:HALF, PROJ, c * D:(c + 1) * D],
                                       xncols[:, i2.ring2, c * HALF:(c + 1) * HALF], wqkv_s[:, 2], start=True, stop=True)
                        last_.then_inc(v_done, 1)
                    if i4.live:
                        g, j = s // 4, s % 4
                        pe.wait_ge(probs_ready, H * i4.n + s + 1)
                        if s == 0:
                            pe.wait_ge(v_ready, i4.n + 1)
                            wait(pe, sums_ready, i4.n)
                        for c in range(2):
                            last_ = mm(ps[2 * HD * j:2 * HD * (j + 1), PV, g * N:(g + 1) * N], vaug[:, i4.ring, c, s],
                                       probs[:, s % 4, c], start=(c == 0), stop=(c == 1))
                        last_.then_inc(pv_done, 1)
                    if s == 2 and i6.live:
                        pe.wait_ge(xs_ready, 2 * (i6.n + 1))
                        freed(pe, (i1, xncols_ready, i1.n + 1))
                        for c in range(2):
                            last_ = tr(ps[:, TURNED, c * HALF:(c + 1) * HALF], xs[:, i6.ring, c, 0, 0:D],
                                       ident[0:HALF, 0:HALF])
                        last_.then_inc(xs_T, 1)
                    if s == 2 and i3.live:
                        pe.wait_ge(max_ready, H * (i3.n + 1))
                        freed(pe, (i0, hcols_ready, i0.n + 1), (i7, gate_h_ready, i7.n + 1))
                        tr(ps[0:2 * H, ROWS, 0:HALF], rowmax[:, i3.ring], ident[0:HALF, 0:HALF]).then_inc(max_T, 1)
                    if s == 3 and i5.live:
                        pe.wait_ge(att_ready, 2 * (i5.n + 1))
                        freed(pe, (i6, xs_cols_ready, i6.n + 1), (i1, xncols_ready, i1.n + 1))
                        for c in range(2):
                            last_ = tr(ps[:, TURNED, c * HALF:(c + 1) * HALF], att[:, c].rearrange("p h d -> p (h d)"),
                                       ident[0:HALF, 0:HALF])
                        last_.then_inc(att_T, 1)
                    if s == 4 and i0.live:
                        pe.wait_ge(hcols_ready, i0.n + 1)
                        freed(pe, (i3, max_low, i3.n + 1))
                        for c in range(2):
                            last_ = tr(ps[0:HALF, ROWS, c * D:(c + 1) * D], hcols[:, c * HALF:(c + 1) * HALF], ident[:])
                        last_.then_inc(hrows_done, 1)

            slots(pe, slot)

            def turn_x(c0, it):
                c, ring, turn = BR * it + c0, c0 % BR, it + c0 // BR
                pe.wait_ge(xg_loaded[ring], 16 * (turn + 1))
                wait(pe, xg_ready, c)
                for s in range(2):
                    last_ = tr(ps[:, ROWS, s * P:(s + 1) * P], xg[:, ring, s, 0:D], ident[:])
                last_.then_inc(xg_T, 1)

            def hidden(c0, it):
                c, r3, ring, turn = BR * it + c0, c0 % 3, c0 % BR, it + c0 // BR
                pe.wait_ge(xg_ready, c + 1)
                pe.wait_ge(w_loaded[ring], 32 * (turn + 1))
                wait(pe, hid_ready, 2 * (c - 2))
                for j in range(2):
                    last_ = mm(ps[:, HBANKS[r3], j * CH:(j + 1) * CH], wring[:, ring, j * P:(j + 1) * P],
                               xg_cols[:, r3], start=True, stop=True)
                last_.then_inc(hid_done, 1)

            def outputs(c0, it):
                c, r3, ring = BR * it + c0, c0 % 3, c0 % BR
                pe.wait_ge(hid_ready, 2 * (c + 1))
                wait(pe, y_ready, c - 2)
                for s in range(2):
                    for j in range(2):
                        last_ = mm(ps[:, YBANKS[r3], s * D:(s + 1) * D], hid[:, r3, j, s * P:(s + 1) * P],
                                   wring[:, ring, HID + j * D:HID + (j + 1) * D], start=(j == 0), stop=(j == 1))
                last_.then_inc(y_done, 1)

            def all_three(c0, it):
                if not isinstance(it, int) or c0 + 2 < NCH:
                    turn_x(c0 + 2, it)
                if not isinstance(it, int) or c0 + 1 < NCH:
                    hidden(c0 + 1, it)
                outputs(c0, it)

            turn_x(0, 0)
            turn_x(1, 0)
            hidden(0, 0)
            chunks(pe, 2, all_three)


def kernel(**inputs):
    import numpy as np
    import concourse.bacc as bacc
    from concourse.bass_utils import run_bass_kernel_spmd as run

    a = {k: np.asarray(v) for k, v in inputs.items()}
    nb, ch, hh, ww = a["x"].shape
    hp, wp = hh // PATCH, ww // PATCH
    k = ch * PATCH * PATCH
    nk = k // P
    f32 = np.float32

    x = a["x"].reshape(nb, ch, hp, PATCH, wp, PATCH).transpose(0, 1, 3, 5, 2, 4).reshape(nb, nk, P, hp * wp)
    x = x.transpose(0, 2, 1, 3)
    wtok = a["L0_tok_w"].T.reshape(nk, P, D).transpose(1, 0, 2)
    by_feature = lambda w: np.moveaxis(w.reshape((H, HD) + w.shape[1:]), 0, 1).reshape(w.shape)
    wqkv = np.stack([by_feature(a["L0_attn_q_w"]).T, by_feature(a["L0_attn_k_w"]).T, a["L0_attn_v_w"].T], axis=1)
    gh = a["L0_ffn_gw1"].shape[1]
    gw1 = np.zeros((D, P), f32)
    gw1[:, 0:gh] = a["L0_ffn_gw1"]
    gw2 = np.zeros((P, NE), f32)
    gw2[0:gh] = a["L0_ffn_gw2"]
    gb1 = np.zeros(P, f32)
    gb1[0:gh] = a["L0_ffn_gb1"]
    wexp = np.concatenate(
        [a["L0_ffn_we1"], a["L0_ffn_we2"].reshape(NE, 2, P, D).transpose(0, 2, 1, 3).reshape(NE, P, 2 * D),
         a["L0_ffn_be1"].reshape(NE, 2, P).transpose(0, 2, 1)], axis=2)
    cols = np.stack([a["L0_tok_b"], by_feature(a["L0_attn_q_b"]), by_feature(a["L0_attn_k_b"]), gb1], axis=1)
    rows = np.concatenate([a["L0_attn_v_b"]] * 2 + [a["L0_ffn_gb2"]] * 2 + [a["L0_attn_o_b"]] * 2)[None]
    ne = a["L0_attn_edge_index"].shape[1]
    edges = a["L0_attn_edge_index"].reshape(2, P, ne // P).transpose(1, 0, 2)
    attr = np.zeros((ne, 4), f32)
    attr[:, 0:3] = a["L0_attn_edge_attr"]
    ebw = np.concatenate([a["L0_attn_eb_w"].T.reshape(-1), a["L0_attn_eb_b"]])[None]
    nt = nb * N
    region = nt + CH
    nch = -(-((2 * nt + NE * (CH - 1)) // CH) // 3) * 3
    every = lambda r: np.broadcast_to(np.asarray(r, f32)[None], (P, len(r)))
    consts = np.concatenate(
        [np.eye(P, dtype=f32), every(range(NE)), every([e * region for e in range(NE)]), every(range(N)),
         (np.arange(P, dtype=f32) * (ne // P))[:, None], every([CH * c for c in range(nch)])], axis=1)
    import ml_dtypes
    earlier = np.triu(np.ones((HALF, HALF)), 1)
    tri = np.stack([earlier, np.ones((HALF, HALF))], axis=1).astype(ml_dtypes.bfloat16)
    tokens = np.array([[i * N + c * HALF + p + kk * nt for i in range(RING) for c in range(2) for kk in range(2)]
                       for p in range(HALF)], np.uint32)

    nc = bacc.Bacc("TRN2", target_bir_lowering=False, num_devices=1)
    arrays, args = {}, []
    for name, v in (("x", x), ("wtok", wtok), ("wqkv", wqkv), ("wo", a["L0_attn_o_w"].T), ("gw1", gw1), ("gw2", gw2),
                    ("wexp", wexp), ("be2", a["L0_ffn_be2"]), ("cols", cols), ("rows", rows), ("edges", edges),
                    ("attr", attr), ("ebw", ebw), ("consts", consts), ("tri", tri), ("tokens", tokens)):
        v = np.ascontiguousarray(v)
        arrays[name + "_in"] = v
        args.append(nc.dram_tensor(name + "_in", v.shape, mybir.dt.from_np(v.dtype), kind="ExternalInput").ap())
    out = nc.dram_tensor("h_out", (nb, N, D), F32, kind="ExternalOutput").ap()
    vit_block(nc, *args, out)
    r = run(nc, [arrays], core_ids=[0])
    return r.results[0]["h_out"]
```

```python
from contextlib import ExitStack

import concourse.bass as bass
from concourse import mybir

ALU = mybir.AluOpType
ACT = mybir.ActivationFunctionType
F32 = mybir.dt.float32
F32R = mybir.dt.float32r
BF16 = mybir.dt.bfloat16
U32 = mybir.dt.uint32
I32 = mybir.dt.int32
AX_X = mybir.AxisListType.X

P = 128
PATCH = 16
N = 196
HALF = N // 2
D = 128
H = 8
HD = D // H
NE = 8
HID = 256
EPS = 1e-5
RING = 4
FRONT = 15
LAST_LAG = 8
CH = 256
XW = 132
BR = 6
OG = 4
CR = 4
JUNK_ROW = float(1 << 20)
ROW_BIAS, ROW_MAX, ROW_END = 4 * HD, 4 * HD + 2, 4 * HD + 4
ROWS, PROJ, TURNED, S1, S2, PV = 0, 1, 2, 3, 5, 7
HBANKS, YBANKS = (3, 4, 5), (6, 7, 1)


class Image:

    def __init__(self, slot, it, lag, count):
        c = slot - lag
        self.ring = c % RING
        self.turn = it + c // RING
        self.ring2, self.turn2 = c % 2, RING // 2 * it + c // 2
        self.n = RING * it + c
        self.live = not isinstance(self.n, int) or 0 <= self.n < count


def wait(eng, sem, value):
    if not isinstance(value, int) or value > 0:
        eng.wait_ge(sem, value)


def freed(eng, *users):
    for img, sem, value in users:
        if img.live:
            wait(eng, sem, value)
            return


def vit_block(nc, x, wtok, wqkv, wo, gw1, gw2, wexp, be2, cols, rows, edges, attr, ebw, consts, tri,
              tokens, out):
    NB = x.shape[0]
    NK = x.shape[2]
    NT = NB * N
    TILES = 2 * NB
    REGION = NT + CH
    NCH = (2 * NT + NE * (CH - 1)) // CH
    TURNS = (NB - 1 - FRONT) // RING
    EJ = edges.shape[2]
    assert (NB - 1 - FRONT) % RING == 0 and TILES % (CR * OG) == 0

    with ExitStack() as ctx:
        def sb(name, shape, dt=F32):
            return ctx.enter_context(nc.sbuf_tensor(name, shape, dt))

        def sem(name):
            return ctx.enter_context(nc.semaphore(name))

        ps = ctx.enter_context(nc.psum_tensor("ps", [P, 8, 512], F32))

        xsort = nc.dram_tensor("xsort", (NE * REGION + CH, XW), F32, kind="Internal").ap()
        ysort = nc.dram_tensor("ysort", (2 * NT, D), F32, kind="Internal").ap()

        wtok_s = sb("wtok_s", [P, NK, D])
        wqkv_s = sb("wqkv_s", [P, 3, D])
        wo_s = sb("wo_s", [P, D])
        gw1_s = sb("gw1_s", [P, D])
        gw2_s = sb("gw2_s", [P, NE])
        cols_s = sb("cols_s", [P, 4])
        vb_s = sb("vb_s", [HALF, 2, D])
        gb2_s = sb("gb2_s", [HALF, 2, NE])
        ob_s = sb("ob_s", [HALF, 2, D])
        power = sb("power", [HALF, 2])
        ebw_s = sb("ebw_s", [HALF, 4, H])
        ident = sb("ident", [P, P])
        expert_no = sb("expert_no", [HALF, NE])
        region_row = sb("region_row", [HALF, NE])
        lower = sb("lower", [HALF, 2, HALF], BF16)

        WW = 2 * HID + 2
        room1 = sb("room1", [P, BR * WW])
        edge_i = room1[:, 0:2 * EJ].bitcast(I32).rearrange("p (a j) -> p a j", a=2)
        edge_f = room1[:, 2 * EJ:4 * EJ].rearrange("p (a j) -> p a j", a=2)
        edge_ok = room1[:, 4 * EJ:8 * EJ].rearrange("p (a j) -> p a j", a=4)
        edge_key = room1[:, 8 * EJ:9 * EJ]
        tok_no = room1[:, 9 * EJ:9 * EJ + N + 1]
        edge_last = room1[:, 10 * EJ + N:10 * EJ + 2 * N]
        halves = room1[:, 10 * EJ + 2 * N:10 * EJ + 2 * N + 5 * N // 2].bitcast(BF16)
        tok_no16 = halves[:, 0:N]
        edge_hit = halves[:, N:3 * N].rearrange("p (a n) -> p a n", a=2)
        edge_last16 = halves[:, 3 * N:5 * N].rearrange("p (a n) -> p a n", a=2)
        last = sb("last", [HALF, 3, 2])
        last_i = sb("last_i", [HALF, 2], U32)
        attr_s = sb("attr_s", [HALF, 2, 4])
        eb = sb("eb", [HALF, 2, H])
        bias_part = sb("bias_part", [H, 2, N], F32R)

        tokens_s = sb("tokens_s", [HALF, 4 * RING], U32)

        patches = sb("patches", [P, 2, NK, N])
        hcols = sb("hcols", [P, N])
        h_all = sb("h_all", [HALF, TILES, D])
        stats = sb("stats", [HALF, 2, 6])
        mv = sb("mv", [HALF, 2, 2])
        var = sb("var", [HALF, 2])
        rstd = sb("rstd", [HALF, 2])
        shift = sb("shift", [HALF, 2])
        xn = sb("xn", [HALF, 2, D])
        sizes = [2 * N, RING * 2 * H * 2 * HD, 4 * 2 * N, 2 * N]
        o = [sum(sizes[:i]) for i in range(5)]
        room2 = sb("room2", [P, max(o[4], 2 * CR * OG * D)])
        xncols = room2[:, o[0]:o[1]].rearrange("p (r n) -> p r n", r=2)
        vaug = room2[0:HALF, o[1]:o[2]].rearrange("p (r c h f) -> p r c h f", r=RING, c=2, h=H)
        probs = room2[0:HALF, o[2]:o[3]].rearrange("p (r c n) -> p r c n", r=4, c=2)
        sums = room2[:, o[3]:o[4]].rearrange("p (g n) -> p g n", g=2)
        parts = sb("parts", [P, 2, 2, 2, N], F32R)
        sides = sb("sides", [P, RING, H, 2, N], F32R)
        qside, kside = sides[:, :, :, 0], sides[:, :, :, 1]
        rowmax = sb("rowmax", [HALF, RING, 2, H])
        negmax = sb("negmax", [H, RING, 2, N], F32R)
        rden = sb("rden", [HALF, 2, H])
        att = sb("att", [HALF, 2, H, HD])
        att_cols = sb("att_cols", [P, N])
        stats2 = sb("stats2", [HALF, 2, 6])
        mv2 = sb("mv2", [HALF, 2, 2])
        var2 = sb("var2", [HALF, 2])
        rstd2 = sb("rstd2", [HALF, 2])
        shift2 = sb("shift2", [HALF, 2])
        room3 = sb("room3", [P, max(RING * 4, BR * 2) * XW])
        xs = room3[0:HALF, 0:RING * 4 * XW].rearrange("p (r c k w) -> p r c k w", r=RING, c=2, k=2)
        xs_cols = sb("xs_cols", [P, N])
        gate_h = sb("gate_h", [P, N])
        logits = sb("logits", [HALF, RING, 2, NE])
        top = sb("top", [HALF, RING, 2, NE])
        top_i = sb("top_i", [HALF, 2, NE], U32)
        top_f = sb("top_f", [HALF, 2, 2])
        first_hot = sb("first_hot", [HALF, 2, NE])
        hot = sb("hot", [HALF, 2, NE], BF16)
        base = sb("base", [HALF, RING, 2, NE])
        place = sb("place", [HALF, 2, NE])
        place_one = sb("place_one", [HALF, 4, NE])
        pos = sb("pos", [HALF, 4])
        pos_i = sb("pos_i", [HALF, RING, 4], U32)
        logits_all = sb("logits_all", [HALF, TILES, NE])
        top_all = sb("top_all", [HALF, TILES, 2])
        plan = sb("plan", [1, 6, NE])
        chunk_row = sb("chunk_row", [1, NCH])
        plan_c = sb("plan_c", [1, 4, NCH])
        passed = sb("passed", [1, NCH, NE])
        plan_i = sb("plan_i", [1, 2, NCH], I32)
        fill_i = sb("fill_i", [1, NE], I32)
        count_i = sb("count_i", [1, NE], I32)
        filler = sb("filler", [P, 2, XW])
        xg = room3[:, 0:BR * 2 * XW].rearrange("p (r s w) -> p r s w", r=BR, s=2)
        dest = sb("dest", [P, BR, 2], U32)
        wring = room1[:].rearrange("p (r w) -> p r w", r=BR)
        b2ring = room2[:, 0:BR * D].rearrange("p (r d) -> p r d", r=BR)
        xg_cols = room2[:, BR * D:BR * D + 3 * CH].rearrange("p (r n) -> p r n", r=3)
        hid = room2[:, BR * D + 3 * CH:BR * D + 9 * CH].rearrange("p (r j n) -> p r j n", r=3, j=2)
        ys = patches[:].rearrange("p r k n -> p (r k n)")[:, 0:BR * 2 * D].rearrange(
            "p (r s d) -> p r s d", r=BR, s=2)
        wt = sb("wt", [HALF, TILES, 2])
        psum2 = sb("psum2", [HALF, 3, TILES])
        yin = room2[0:HALF, 0:2 * CR * OG * D].rearrange("p (r k j d) -> p r k j d", r=CR, k=2, j=OG)
        res = room1[0:HALF, 0:CR * OG * D].rearrange("p (r j d) -> p r j d", r=CR, j=OG)

        c_embed, c_qkv, c_edge, c_misc = sem("c_embed"), sem("c_qkv"), sem("c_edge"), sem("c_misc")
        x_loaded = [sem(f"x_loaded{r}") for r in range(2)]
        sides_in = [sem(f"sides_in{r}") for r in range(RING)]
        max_in = [sem(f"max_in{r}") for r in range(RING)]
        rows_sent = [sem(f"rows_sent{r}") for r in range(RING)]
        memsets, gone_on = sem("memsets"), sem("gone_on")
        edge_step, edge_max, attr_in = sem("edge_step"), sem("edge_max"), sem("attr_in")
        edge_T, bias_T, bias_done = sem("edge_T"), sem("bias_T"), sem("bias_done")
        bias_in = [sem(f"bias_in{r}") for r in range(RING)]
        embed_done, hrows_done, xncols_done = sem("embed_done"), sem("hrows_done"), sem("xncols_done")
        qk_done, v_done, s1_done, s2_done, pv_done = (sem(x) for x in ("qk_done", "v_done", "s1_done", "s2_done", "pv_done"))
        max_T, sums_T, att_T, o_done, xs_T, gate1_done, gate2_done, rank_done = (
            sem(x) for x in ("max_T", "sums_T", "att_T", "o_done", "xs_T", "gate1_done", "gate2_done", "rank_done"))
        hcols_ready, h_ready, xncols_ready, high_ready, probs_ready = (
            sem(x) for x in ("hcols_ready", "h_ready", "xncols_ready", "high_ready", "probs_ready"))
        max_high, sums_ready, att_cols_ready, xs_cols_ready, gate_h_ready = (
            sem(x) for x in ("max_high", "sums_ready", "att_cols_ready", "xs_cols_ready", "gate_h_ready"))
        max_ready, max_low, low_ready, v_ready, rden_ready, att_ready = (
            sem(x) for x in ("max_ready", "max_low", "low_ready", "v_ready", "rden_ready", "att_ready"))
        stats_ready, mv_ready, rstd_ready, xn_ready = (sem(x) for x in ("stats_ready", "mv_ready", "rstd_ready", "xn_ready"))
        h2_ready, stats2_ready, mv2_ready, rstd2_ready, xs_ready = (
            sem(x) for x in ("h2_ready", "stats2_ready", "mv2_ready", "rstd2_ready", "xs_ready"))
        logits_ready, top_ready, top_i_ready, top_f_ready, first_ready, hot_ready = (
            sem(x) for x in ("logits_ready", "top_ready", "top_i_ready", "top_f_ready", "first_ready", "hot_ready"))
        place_ready, base_mid, base_ready, pos_f_ready, pos_ready = (
            sem(x) for x in ("place_ready", "base_mid", "base_ready", "pos_f_ready", "pos_ready"))
        var_ready, var2_ready, ob_added = sem("var_ready"), sem("var2_ready"), sem("ob_added")
        shift_ready, shift2_ready = sem("shift_ready"), sem("shift2_ready")
        xs2_ready, dest_in, dest_ready, kept = sem("xs2_ready"), sem("dest_in"), sem("dest_ready"), sem("kept")
        ends_ready = sem("ends_ready")
        plan_step, plan_ready, filled = sem("plan_step"), sem("plan_ready"), sem("filled")
        xg_loaded = [sem(f"xg_loaded{r}") for r in range(BR)]
        w_loaded = [sem(f"w_loaded{r}") for r in range(BR)]
        y_sent = [sem(f"y_sent{r}") for r in range(BR)]
        dest_kept = sem("dest_kept")
        xg_T, xg_ready, hid_done, hid_ready, y_done, y_ready = (
            sem(x) for x in ("xg_T", "xg_ready", "hid_done", "hid_ready", "y_done", "y_ready"))
        wt_step, wt_exp = sem("wt_step"), sem("wt_exp")
        yin_loaded = [sem(f"yin_loaded{r}") for r in range(CR)]
        out_stored = [sem(f"out_stored{r}") for r in range(CR)]
        yin_scaled, res_mid, res_ready = sem("yin_scaled"), sem("res_mid"), sem("res_ready")

        block = ctx.enter_context(nc.Block())

        def apart(eng, it):
            if not isinstance(it, int):
                eng.sem_inc(gone_on, 1)

        def slots(eng, slot):
            for t in range(FRONT):
                slot(t, 0)
            if TURNS == 1:
                for u in range(RING):
                    slot(FRONT + u, 0)
            else:
                with eng.Fori(0, TURNS) as it:
                    for u in range(RING):
                        slot(FRONT + u, it)
            for t in range(NB - 1, NB + LAST_LAG):
                slot(t, 0)

        def chunks(eng, ahead, one):
            turns = (NCH - BR - ahead) // BR
            for c in range(BR):
                one(c, 0)
            with eng.Fori(0, turns) as it:
                for u in range(BR):
                    one(BR + u, it)
            for c in range(BR + turns * BR, NCH):
                one(c, 0)

        def fill_behind(eng, experts):
            eng.wait_ge(ends_ready, 1)
            for e in experts:
                row = eng.value_load(fill_i[0:1, e:e + 1], min_val=0, max_val=NE * REGION - CH)
                eng.dma_start(xsort[bass.ds(row, CH), :].rearrange("(p s) w -> p s w", s=2), filler[:]).then_inc(
                    filled, 16)

        def tile_rows(n):
            return h_all[:, bass.ds(2 * n, 2), :]

        @block.sync
        def _(sp):
            sp.dma_start(wtok_s[:], wtok).then_inc(c_embed, 16)
            sp.dma_start(cols_s[:], cols).then_inc(c_embed, 16)
            sp.dma_start(patches[:, 0], x[0]).then_inc(x_loaded[0], 16)
            sp.dma_start(ident[:], consts[:, 0:P]).then_inc(c_embed, 16)
            sp.dma_start(wqkv_s[:], wqkv).then_inc(c_qkv, 16)
            sp.dma_start(vb_s[:], rows[0:1, 0:2 * D].to_broadcast([HALF, 2 * D]).rearrange(
                "p (c d) -> p c d", c=2)).then_inc(c_qkv, 16)
            sp.dma_start(wo_s[:], wo).then_inc(c_misc, 16)
            sp.dma_start(gw1_s[:], gw1).then_inc(c_misc, 16)
            sp.dma_start(gw2_s[:], gw2).then_inc(c_misc, 16)
            sp.dma_start(gb2_s[:], rows[0:1, 2 * D:2 * D + 2 * NE].to_broadcast([HALF, 2 * NE]).rearrange(
                "p (c e) -> p c e", c=2)).then_inc(c_misc, 16)
            sp.dma_start(ob_s[:], rows[0:1, 2 * D + 2 * NE:].to_broadcast([HALF, 2 * D]).rearrange(
                "p (c d) -> p c d", c=2)).then_inc(c_misc, 16)
            sp.dma_start(expert_no[:], consts[0:HALF, P:P + NE]).then_inc(c_misc, 16)
            sp.dma_start(region_row[:], consts[0:HALF, P + NE:P + 2 * NE]).then_inc(c_misc, 16)
            sp.dma_start(lower[:], tri).then_inc(c_misc, 16)
            sp.dma_start(chunk_row[:], consts[0:1, P + 2 * NE + N + 1:P + 2 * NE + N + 1 + NCH]).then_inc(c_misc, 16)
            sp.dma_start(tokens_s[:], tokens).then_inc(dest_in, 16)
            sp.wait_ge(memsets, 5)
            sp.dma_start(xsort[NE * REGION:NE * REGION + CH, :].rearrange("(p s) w -> p s w", s=2),
                         filler[:]).then_inc(filled, 16)

            def slot(t, it):
                a, b, c, d = (Image(t, it, lag, NB) for lag in (-1, 1, 3, 0))
                if a.live:
                    wait(sp, embed_done, a.n - 1)
                    apart(sp, it)
                    sp.dma_start(patches[:, a.ring2], x[bass.ds(a.n, 1)].rearrange("o p k n -> p (o k) n")).then_inc(
                        x_loaded[a.ring2], 16)
                if c.live:
                    sp.wait_ge(max_low, c.n + 1)
                    wait(sp, s2_done, H * (c.n - 3))
                    apart(sp, it)
                    for j in range(2):
                        sp.dma_start(qside[ROW_MAX + j:ROW_MAX + j + 1, c.ring].bitcast(F32),
                                     negmax[:, c.ring, j].bitcast(F32).rearrange("p (o n) -> p o n", o=1)).then_inc(
                                         max_in[c.ring], 16)
                if b.live:
                    wait(sp, s2_done, H * (b.n - 3))
                    apart(sp, it)
                    of_image = parts[:, b.ring2].bitcast(F32).rearrange("p a j n -> p (a j) n")
                    for j, pair in enumerate((of_image[:, 0:4:2], of_image[:, 0:4:3], of_image[:, 1:3],
                                              of_image[:, 1:4:2])):
                        if j < 2:
                            sp.wait_ge(high_ready if j == 0 else low_ready, 2 * (b.n + 1))
                            apart(sp, it)
                        sp.dma_start(sides[HD * j:HD * (j + 1), b.ring].bitcast(F32).rearrange("d h a n -> d (h a) n"),
                                     pair).then_inc(sides_in[b.ring], 16)

            slots(sp, slot)

            fill_behind(sp, range(0, NE, 2))
            sp.wait_ge(plan_ready, 1)
            sp.wait_ge(filled, 16 * (NE + 1))
            for r in range(RING):
                sp.wait_ge(rows_sent[r], 64 * len(range(r, NB, RING)))

            def load(c0, it):
                c, ring = BR * it + c0, c0 % BR
                row = sp.value_load(plan_i[0:1, 0, bass.ds(c, 1)], min_val=0, max_val=NE * REGION)
                wait(sp, y_ready, c - BR + 1)
                sp.dma_start(xg[:, ring], xsort[bass.ds(row, CH), :].rearrange("(p s) w -> p s w", s=2)).then_inc(
                    xg_loaded[ring], 16)

            chunks(sp, 0, load)

            for r in range(BR):
                sp.wait_ge(y_sent[r], 32 * len(range(r, NCH, BR)))
            ytiles = ysort.rearrange("(k t p) d -> k p t d", k=2, p=HALF)

            def group(g, r, turn):
                wait(sp, res_ready, g - CR + 1)
                for k in range(2):
                    sp.dma_start(yin[:, r, k], ytiles[k][:, bass.ds(OG * g, OG), :]).then_inc(yin_loaded[r], 16)

            for r in range(CR):
                group(r, r, 0)
            with sp.Fori(1, TILES // OG // CR) as it:
                for r in range(CR):
                    group(CR * it + r, r, it)

        @block.gpsimd
        def _(pool):
            for r in range(RING // 2):
                nc.gpsimd.memset(sides[4 * HD:P, 2 * r:2 * r + 2].bitcast(F32), 1.0).then_inc(memsets, 1)
            pool.wait_ge(memsets, 2)
            nc.gpsimd.memset(xs[:, :, :, :, D:XW], 0.0).then_inc(memsets, 1)
            nc.gpsimd.memset(filler[:, :, 0:D], 0.0).then_inc(memsets, 1)
            nc.gpsimd.memset(filler[:, :, D:XW].bitcast(U32), int(JUNK_ROW)).then_inc(memsets, 1)
            nc.gpsimd.memset(vaug[:, :, :, :, HD:2 * HD], 1.0).then_inc(memsets, 1)
            pool.wait_ge(dest_in, 16)
            pool.wait_ge(memsets, 3)
            nc.gpsimd.tensor_copy(xs[:, :, :, :, D].bitcast(U32).rearrange("p r c k -> p (r c k)"),
                                  tokens_s[:]).then_inc(dest_ready, 1)
            pool.wait_ge(dest_ready, 1)

            nc.gpsimd.memset(power[:], -0.5).then_inc(memsets, 1)
            pool.wait_ge(memsets, 7)
            pool.wait_ge(c_misc, 144)

            def edge_attributes():
                pool.wait_ge(edge_max, 4)
                for c in range(2):
                    pool.indirect_dma_start(attr_s[:, c, :], None, attr, bass.IndirectOffsetOnAxis(
                        ap=last_i[:, c:c + 1], axis=0)).then_inc(attr_in, 16)

            def rsqrt(out_, shift_, mv_, var_, ready, n, it):
                nc.gpsimd.tensor_scalar(shift_, mv_[:, :, 0], -1.0, None, ALU.mult).then_inc(ready[0], 1)
                nc.gpsimd.tensor_scalar(var_, mv_[:, :, 1], EPS, None, ALU.add).then_inc(ready[0], 1)
                pool.wait_ge(ready[0], 2 * (n + 1))
                apart(pool, it)
                nc.gpsimd.tensor_tensor(out_, var_, power[:], ALU.pow).then_inc(ready[1], 1)
                pool.wait_ge(ready[1], n + 1)
                apart(pool, it)
                nc.gpsimd.tensor_tensor(shift_, shift_, out_, ALU.mult).then_inc(ready[2], 1)

            def slot(t, it):
                i0, i1, i6, i7, i8 = (Image(t, it, lag, NB) for lag in (0, 1, 6, 7, 8))
                if t == 2:
                    edge_attributes()
                if i6.live:
                    pool.wait_ge(mv2_ready, 2 * (i6.n + 1))
                    wait(pool, xs_ready, 2 * i6.n)
                    apart(pool, it)
                    rsqrt(rstd2[:], shift2[:], mv2, var2[:], (var2_ready, rstd2_ready, shift2_ready), i6.n, it)
                if i8.live:
                    pool.wait_ge(pos_ready, i8.n + 1)
                    pool.wait_ge(xs2_ready, 2 * i8.n + 2)
                    apart(pool, it)
                    for c in range(2):
                        for k in range(2):
                            j = 2 * c + k
                            pool.indirect_dma_start(
                                xsort, bass.IndirectOffsetOnAxis(ap=pos_i[:, i8.ring, j:j + 1], axis=0),
                                xs[:, i8.ring, c, k, :], None).then_inc(rows_sent[i8.ring], 16)
                if i1.live:
                    pool.wait_ge(xn_ready, 2 * (i1.n + 1))
                    apart(pool, it)
                    nc.gpsimd.tensor_tensor(tile_rows(i1.n), tile_rows(i1.n), ob_s[:], ALU.add).then_inc(ob_added, 1)
                if i6.live:
                    pool.wait_ge(xs_ready, 2 * (i6.n + 1))
                    wait(pool, rows_sent[i6.ring], 64 * i6.turn)
                    apart(pool, it)
                    nc.gpsimd.tensor_copy(xs[:, i6.ring, :, 1, 0:D], xs[:, i6.ring, :, 0, 0:D]).then_inc(xs2_ready, 1)
                    step = 0.0 if isinstance(i6.n, int) and i6.n < RING else float(RING * N)
                    dest = xs[:, i6.ring, :, :, D].bitcast(U32)
                    nc.gpsimd.tensor_scalar(dest, dest, step, None, ALU.add).then_inc(xs2_ready, 1)
                if i7.live:
                    pool.wait_ge(top_ready, 2 * (i7.n + 1))
                    apart(pool, it)
                    nc.gpsimd.tensor_copy(logits_all[:, bass.ds(2 * i7.n, 2), :], logits[:, i7.ring]).then_inc(kept, 1)
                    nc.gpsimd.tensor_copy(top_all[:, bass.ds(2 * i7.n, 2), :], top[:, i7.ring, :, 0:2]).then_inc(
                        kept, 1)
                if i0.live:
                    pool.wait_ge(mv_ready, 2 * (i0.n + 1))
                    wait(pool, xn_ready, 2 * i0.n)
                    apart(pool, it)
                    rsqrt(rstd[:], shift[:], mv, var[:], (var_ready, rstd_ready, shift_ready), i0.n, it)

            slots(pool, slot)

            def send(c0, it):
                c, ring = BR * it + c0, c0 % BR
                pool.wait_ge(y_ready, c + 1)
                pool.wait_ge(dest_kept, c + 1)
                apart(pool, it)
                for s in range(2):
                    pool.indirect_dma_start(
                        ysort, bass.IndirectOffsetOnAxis(ap=dest[:, ring, s:s + 1], axis=0),
                        ys[:, ring, s, :], None, bounds_check=2 * NT - 1, oob_is_err=False).then_inc(y_sent[ring], 16)

            chunks(pool, 0, send)

        @block.scalar
        def _(act):
            act.dma_start(edge_i, edges).then_inc(c_edge, 16)
            act.dma_start(tok_no, consts[:, P + 2 * NE:P + 2 * NE + N + 1]).then_inc(c_edge, 16)
            act.dma_start(ebw_s[:], ebw[0:1, :].to_broadcast([HALF, 4 * H]).rearrange(
                "p (j h) -> p j h", j=4)).then_inc(c_edge, 16)
            act.wait_ge(c_embed, 48)

            def bias_rows():
                act.wait_ge(bias_T, 1)
                nc.scalar.activation(bias_part[:, 0], ps[0:H, TURNED, 0:N], ACT.Copy).then_inc(bias_done, 1)
                act.wait_ge(bias_done, 2)
                act.wait_ge(memsets, 6)
                send_bias(0)
                send_bias(1)

            def send_bias(r):
                for j in range(2):
                    act.dma_start(kside[ROW_BIAS + j:ROW_BIAS + j + 1, r].bitcast(F32),
                                  bias_part[:, j].bitcast(F32).rearrange("p (o n) -> p o n", o=1)
                                  ).then_inc(bias_in[r], 16)

            def normed(img, it, out_, rstd_, shift_, sems):
                act.wait_ge(sems[0], img.n + 1)
                apart(act, it)
                for c in range(2):
                    nc.scalar.activation(out_(c), h_all[:, bass.ds(2 * img.n + c, 1), :].rearrange("p o d -> p (o d)"),
                                         ACT.Identity, bias=shift_[:, c:c + 1], scale=rstd_[:, c:c + 1]).then_inc(
                                             sems[1], 1)

            def slot(t, it):
                i0, i1, i2, i3, i4, i5, i6 = (Image(t, it, lag, NB) for lag in range(7))
                if t in (3, 4):
                    send_bias(t - 1)
                for s in range(H):
                    if s == 0 and i5.live:
                        act.wait_ge(pv_done, H * (i5.n + 1))
                        wait(act, sums_T, i5.n)
                        nc.scalar.activation(sums[:], ps[:, PV, 0:2 * N].rearrange("p (g n) -> p g n", g=2),
                                             ACT.Copy).then_inc(sums_ready, 1)
                    if s == 2 and i1.live:
                        act.wait_ge(xncols_done, i1.n + 1)
                        wait(act, v_done, i1.n - 1)
                        nc.scalar.activation(xncols[:, i1.ring2], ps[:, TURNED, 0:N], ACT.Copy).then_inc(
                            xncols_ready, 1)
                    if s == 2 and i0.live:
                        act.wait_ge(embed_done, i0.n + 1)
                        wait(act, hrows_done, i0.n)
                        nc.scalar.activation(hcols[:], ps[:, ROWS, 0:N], ACT.Identity, bias=cols_s[:, 0:1]).then_inc(
                            hcols_ready, 1)
                    if s == 2 and t == 2:
                        bias_rows()
                    if s == 3 and i6.live:
                        act.wait_ge(xs_T, i6.n + 1)
                        wait(act, gate1_done, i6.n)
                        nc.scalar.activation(xs_cols[:], ps[:, TURNED, 0:N], ACT.Copy).then_inc(xs_cols_ready, 1)
                    if s == 3 and i3.live:
                        act.wait_ge(max_T, i3.n + 1)
                        wait(act, max_in[i3.ring], 32 * i3.turn)
                        nc.scalar.activation(negmax[:, i3.ring, 0], ps[0:H, ROWS, 0:N], ACT.Copy,
                                             scale=-1.0).then_inc(max_high, 1)
                    if s == 4 and i5.live:
                        act.wait_ge(att_T, i5.n + 1)
                        wait(act, o_done, i5.n)
                        nc.scalar.activation(att_cols[:], ps[:, TURNED, 0:N], ACT.Copy).then_inc(att_cols_ready, 1)
                    if s == 4 and i1.live:
                        act.wait_ge(qk_done, i1.n + 1)
                        if i3.live:
                            act.wait_ge(sides_in[i3.ring], 64 * (i3.turn + 1))
                        for a in range(2):
                            nc.scalar.activation(parts[:, i1.ring2, a, 0], ps[:, PROJ, a * N:(a + 1) * N],
                                                 ACT.Identity, bias=cols_s[:, 1 + a:2 + a]).then_inc(high_ready, 1)
                    if s == 5 and i0.live:
                        act.wait_ge(hrows_done, i0.n + 1)
                        apart(act, it)
                        nc.scalar.activation(tile_rows(i0.n), ps[0:HALF, ROWS, 0:2 * D].rearrange(
                            "p (c d) -> p c d", c=2), ACT.Copy).then_inc(h_ready, 1)
                    if s == 7 and i6.live:
                        act.wait_ge(gate1_done, i6.n + 1)
                        wait(act, gate2_done, i6.n)
                        nc.scalar.activation(gate_h[:], ps[:, ROWS, 0:N], ACT.Relu, bias=cols_s[:, 3:4]).then_inc(
                            gate_h_ready, 1)
                    if s == 1 and i6.live:
                        wait(act, rows_sent[i6.ring], 64 * i6.turn)
                        normed(i6, it, lambda c: xs[:, i6.ring, c, 0, 0:D], rstd2, shift2, (shift2_ready, xs_ready))
                    img, h = (i3, 0) if s == 7 else (i4, s + 1)
                    if img.live:
                        act.wait_ge(s2_done, H * img.n + h + 1)
                        wait(act, pv_done, H * img.n + h - 3)
                        nc.scalar.activation(probs[:, h % 4], ps[0:HALF, S2 + h % 2, 0:2 * N], ACT.Exp,
                                             scale=float(HD) ** -0.5).then_inc(probs_ready, 1)
                    if s == 0 and i1.live:
                        wait(act, xncols_done, i1.n)
                        normed(i1, it, lambda c: xn[:, c], rstd, shift, (shift_ready, xn_ready))

            slots(act, slot)

            AHEAD = 4

            def load(c0, it):
                c, ring = BR * it + c0, c0 % BR
                e = act.value_load(plan_i[0:1, 1, bass.ds(c, 1)], min_val=0, max_val=NE - 1)
                wait(act, y_ready, c - BR + 1)
                act.dma_start(wring[:, ring], wexp[bass.ds(e, 1)].rearrange("o p w -> p (o w)")).then_inc(
                    w_loaded[ring], 16)
                act.dma_start(b2ring[:, ring], be2[bass.ds(e, 1), :].to_broadcast([P, D])).then_inc(
                    w_loaded[ring], 16)

            def gelu(c0, it):
                c, r3, ring = BR * it + c0, c0 % 3, c0 % BR
                act.wait_ge(hid_done, c + 1)
                wait(act, y_done, c - 2)
                for j in range(2):
                    nc.scalar.activation(hid[:, r3, j], ps[:, HBANKS[r3], j * CH:(j + 1) * CH], ACT.Gelu,
                                         bias=wring[:, ring, 2 * HID + j:2 * HID + j + 1]).then_inc(hid_ready, 1)
                if not isinstance(it, int) or c0 + AHEAD < NCH:
                    load(c0 + AHEAD, it)

            fill_behind(act, range(1, NE, 2))
            act.wait_ge(plan_ready, 1)
            act.wait_ge(o_done, NB)
            load(0, 0)
            load(1, 0)
            load(2, 0)
            load(3, 0)
            chunks(act, AHEAD, gelu)

            act.wait_ge(wt_step, 2)
            nc.scalar.activation(logits_all[:], logits_all[:], ACT.Exp).then_inc(wt_exp, 1)
            nc.scalar.activation(psum2[:, 0], psum2[:, 0], ACT.Exp).then_inc(wt_exp, 1)
            act.wait_ge(wt_step, 6)
            nc.scalar.activation(psum2[:, 1], psum2[:, 1], ACT.Exp).then_inc(wt_exp, 1)

            otiles = out.rearrange("b (c p) d -> p (b c) d", p=HALF)

            GROUPS = TILES // OG

            def scale(g, r, turn):
                act.wait_ge(yin_loaded[r], 32 * (turn + 1))
                for j in range(OG):
                    nc.scalar.activation(yin[:, r, 1, j], yin[:, r, 1, j], ACT.Copy, scale=wt[:, bass.ds(
                        OG * g + j, 1), 1:2].rearrange("p o k -> p (o k)")).then_inc(yin_scaled, 1)

            def store(g, r):
                act.wait_ge(res_ready, g + 1)
                act.dma_start(otiles[:, bass.ds(OG * g, OG), :], res[:, r]).then_inc(out_stored[r], 16)

            act.wait_ge(wt_step, 9)
            scale(0, 0, 0)
            with act.Fori(0, GROUPS // CR - 1) as it:
                for u in range(CR):
                    scale(CR * it + 1 + u, (1 + u) % CR, it + (1 + u) // CR)
                    store(CR * it + u, u)
            for u in range(CR):
                if u < CR - 1:
                    scale(GROUPS - CR + 1 + u, 1 + u, GROUPS // CR - 1)
                store(GROUPS - CR + u, u)
            for r in range(CR):
                act.wait_ge(out_stored[r], 16 * (GROUPS // CR))

        @block.vector
        def _(dve):
            v = nc.vector
            dve.wait_ge(c_edge, 48)
            v.tensor_copy(edge_f, edge_i).then_inc(edge_step, 1)
            v.tensor_copy(tok_no16, tok_no[:, 0:N]).then_inc(edge_step, 1)
            v.memset(edge_last16, 0.0).then_inc(edge_step, 1)
            dve.wait_ge(edge_step, 3)
            for j in range(2):
                v.tensor_scalar(edge_ok[:, j], edge_f[:, j], 0.0, None, ALU.is_ge).then_inc(edge_step, 1)
            dve.wait_ge(edge_step, 5)
            for j in range(2):
                v.scalar_tensor_tensor(edge_ok[:, 2 + j], edge_f[:, j], float(N), edge_ok[:, j],
                                       ALU.is_lt, ALU.mult).then_inc(edge_step, 1)
            dve.wait_ge(edge_step, 7)
            v.tensor_tensor(edge_ok[:, 0], edge_ok[:, 2], edge_ok[:, 3], ALU.mult).then_inc(edge_step, 1)
            dve.wait_ge(edge_step, 8)
            v.tensor_tensor(edge_key, edge_ok[:, 0], tok_no[:, 1:EJ + 1], ALU.mult).then_inc(edge_step, 1)
            dve.wait_ge(edge_step, 9)

            def edge_hits(first, end):
                for j in range(first, end, 2):
                    before = 9 + 2 * j
                    for a in range(2):
                        if j:
                            dve.wait_ge(edge_step, before - 1 + a)
                        v.tensor_scalar(edge_hit[:, a], tok_no16, edge_f[:, 1, j + a:j + a + 1],
                                        edge_key[:, j + a:j + a + 1], ALU.is_equal, ALU.mult).then_inc(edge_step, 1)
                    for a in range(2):
                        dve.wait_ge(edge_step, before + 1 + a)
                        v.tensor_tensor(edge_last16[:, a], edge_last16[:, a], edge_hit[:, a],
                                        ALU.max).then_inc(edge_step, 1)

            def edge_end():
                es = 9 + 2 * EJ
                dve.wait_ge(edge_step, es)
                v.tensor_tensor(edge_hit[:, 0], edge_last16[:, 0], edge_last16[:, 1], ALU.max).then_inc(edge_step, 1)
                dve.wait_ge(edge_step, es + 1)
                v.tensor_scalar(edge_last, edge_hit[:, 0], 0.0, tok_no[:, N:N + 1], ALU.is_gt, ALU.mult).then_inc(
                    edge_step, 1)
                dve.wait_ge(edge_step, es + 2)
                v.tensor_tensor(edge_last, edge_last, edge_hit[:, 0], ALU.add).then_inc(edge_T, 1)

            edge_hits(0, EJ // 4)
            dve.wait_ge(c_misc, 144)
            v.tensor_copy(base[:, 0, 0], region_row[:]).then_inc(base_ready, 1)

            def norm_stats(img, it, ready, s_):
                apart(dve, it)
                for c in range(2):
                    v.bn_stats(s_[:, c], h_all[:, bass.ds(2 * img.n + c, 1), :].rearrange("p o d -> p (o d)")).then_inc(
                        ready, 1)

            def norm_aggr(img, it, sems, s_, m_):
                dve.wait_ge(sems[0], 2 * (img.n + 1))
                apart(dve, it)
                for c in range(2):
                    v.bn_aggr(m_[:, c], s_[:, c]).then_inc(sems[1], 1)

            def column_bias():
                dve.wait_ge(edge_T, 2)
                v.tensor_reduce(last[:, 0], ps[0:HALF, TURNED, 0:2 * P].rearrange("p (c e) -> p c e", c=2),
                                AX_X, ALU.max).then_inc(edge_max, 1)
                dve.wait_ge(edge_max, 1)
                v.tensor_scalar(last[:, 1], last[:, 0], 1.0, 4.0, ALU.is_ge, ALU.mult).then_inc(edge_max, 1)
                v.tensor_scalar(last[:, 2], last[:, 0], -1.0, 0.0, ALU.add, ALU.max).then_inc(edge_max, 1)
                dve.wait_ge(edge_max, 3)
                v.tensor_copy(last_i[:], last[:, 2]).then_inc(edge_max, 1)
                dve.wait_ge(attr_in, 32)
                for c in range(2):
                    for j in range(3):
                        v.scalar_tensor_tensor(eb[:, c], ebw_s[:, j], attr_s[:, c, j:j + 1],
                                               ebw_s[:, 3] if j == 0 else eb[:, c], ALU.mult, ALU.add).then_inc(
                                                   edge_max, 1)
                        dve.wait_ge(edge_max, 5 + 4 * c + j)
                    v.tensor_scalar(eb[:, c], eb[:, c], last[:, 1, c:c + 1], None, ALU.mult).then_inc(edge_max, 1)
                dve.wait_ge(bias_done, 1)
                v.tensor_tensor(bias_part[:, 1], ps[0:H, TURNED, 0:N], bias_part[:, 0].bitcast(F32),
                                ALU.subtract).then_inc(bias_done, 1)

            def slot(t, it):
                i0, i1, i2, i3, i4, i5, i6, i7 = (Image(t, it, lag, NB) for lag in range(8))
                if t == 1:
                    edge_hits(EJ // 4, EJ // 2)
                if t == 2:
                    edge_hits(EJ // 2, EJ)
                    edge_end()
                    column_bias()
                for s in range(H):
                    if s == 1 and i7.live:
                        dve.wait_ge(gate2_done, i7.n + 1)
                        wait(dve, kept, 2 * (i7.n - 3))
                        v.tensor_tensor(logits[:, i7.ring], ps[0:HALF, S1, 2 * N:2 * N + 2 * NE].rearrange(
                            "p (c e) -> p c e", c=2), gb2_s[:], ALU.add).then_inc(logits_ready, 1)
                    if s == 2 and i5.live:
                        dve.wait_ge(sums_T, i5.n + 1)
                        four = ps[0:HALF, PROJ, :].rearrange("p (c h f) -> p c h f", c=2, h=H)
                        v.reciprocal(rden[:], four[:, :, :, HD]).then_inc(rden_ready, 1)
                    if s == 2 and i7.live:
                        dve.wait_ge(logits_ready, i7.n + 1)
                        apart(dve, it)
                        for c in range(2):
                            v.max(top[:, i7.ring, c], logits[:, i7.ring, c]).then_inc(top_ready, 1)
                    if s == 2 and i5.live:
                        dve.wait_ge(rden_ready, i5.n + 1)
                        wait(dve, att_T, i5.n)
                        for c in range(2):
                            v.tensor_tensor(att[:, c], four[:, c, :, 0:HD],
                                            rden[:, c].rearrange("p (h o) -> p h o", o=1).to_broadcast([HALF, H, HD]),
                                            ALU.mult).then_inc(att_ready, 1)
                    if s == 2 and i7.live:
                        dve.wait_ge(top_ready, 2 * (i7.n + 1))
                        apart(dve, it)
                        for c in range(2):
                            v.max_index(top_i[:, c], top[:, i7.ring, c], logits[:, i7.ring, c]).then_inc(top_i_ready, 1)
                    if s == 3 and i7.live:
                        dve.wait_ge(top_f_ready, i7.n + 1)
                        wait(dve, rank_done, i7.n)
                        for c in range(2):
                            v.tensor_scalar(first_hot[:, c], expert_no[:], top_f[:, c, 0:1], None,
                                            ALU.is_equal).then_inc(first_ready, 1)
                        for c in range(2):
                            dve.wait_ge(first_ready, 2 * i7.n + 1 + c)
                            v.scalar_tensor_tensor(hot[:, c], expert_no[:], top_f[:, c, 1:2], first_hot[:, c],
                                                   ALU.is_equal, ALU.add).then_inc(hot_ready, 1)
                    if s == 4 and i3.live:
                        dve.wait_ge(max_high, i3.n + 1)
                        v.scalar_tensor_tensor(negmax[:, i3.ring, 1], ps[0:H, ROWS, 0:N], -1.0,
                                               negmax[:, i3.ring, 0].bitcast(F32), ALU.mult, ALU.subtract).then_inc(
                                                   max_low, 1)
                    if s == 5 and i7.live:
                        n, r = i7.n, i7.ring
                        ranks = ps[0:HALF, S1, 2 * N:2 * N + 4 * NE].rearrange("p (a e) -> p a e", a=4)
                        dve.wait_ge(rank_done, n + 1)
                        dve.wait_ge(base_ready, n + 1)
                        v.tensor_tensor(place[:, 0], ranks[:, 0], base[:, r, 0], ALU.add).then_inc(place_ready, 1)
                        v.tensor_tensor(base[:, r, 1], ranks[:, 2], base[:, r, 0], ALU.add).then_inc(base_mid, 1)
                    if s == 5 and i1.live:
                        dve.wait_ge(high_ready, 2 * (i1.n + 1))
                        for a in range(2):
                            v.scalar_tensor_tensor(parts[:, i1.ring2, a, 1], ps[:, PROJ, a * N:(a + 1) * N],
                                                   cols_s[:, 1 + a:2 + a], parts[:, i1.ring2, a, 0].bitcast(F32),
                                                   ALU.add, ALU.subtract).then_inc(low_ready, 1)
                    if s == 5 and i7.live:
                        dve.wait_ge(base_mid, i7.n + 1)
                        v.tensor_tensor(place[:, 1], ranks[:, 1], base[:, r, 1], ALU.add).then_inc(place_ready, 1)
                        v.tensor_tensor(base[:, (r + 1) % RING, 0], ranks[:, 3], base[:, r, 1],
                                        ALU.add).then_inc(base_ready, 1)
                    if s == 6 and i5.live:
                        dve.wait_ge(o_done, i5.n + 1)
                        dve.wait_ge(ob_added, i5.n + 1)
                        v.tensor_tensor(tile_rows(i5.n), ps[0:HALF, TURNED, 0:2 * D].rearrange(
                            "p (c d) -> p c d", c=2), tile_rows(i5.n), ALU.add).then_inc(h2_ready, 1)
                    if s == 6 and i0.live:
                        dve.wait_ge(h_ready, i0.n + 1)
                        norm_stats(i0, it, stats_ready, stats)
                    if s == 7 and i5.live:
                        dve.wait_ge(h2_ready, i5.n + 1)
                        norm_stats(i5, it, stats2_ready, stats2)
                    if s == 7 and i7.live:
                        n, r = i7.n, i7.ring
                        for c in range(2):
                            dve.wait_ge(place_ready, 2 * n + 1 + c)
                            for k in range(2):
                                j = 2 * c + k
                                v.scalar_tensor_tensor(place_one[:, j], expert_no[:], top_f[:, c, k:k + 1], place[:, c],
                                                       ALU.is_equal, ALU.mult, accum_out=pos[:, j:j + 1]).then_inc(
                                                           pos_f_ready, 1)
                    if s == 7 and i5.live:
                        wait(dve, shift2_ready, i5.n)
                        norm_aggr(i5, it, (stats2_ready, mv2_ready), stats2, mv2)
                    img, h = (i2, s - 2) if s >= 2 else (i3, s + 6)
                    if img.live:
                        dve.wait_ge(s1_done, H * img.n + h + 1)
                        v.tensor_reduce(rowmax[:, img.ring, :, h],
                                        ps[0:HALF, S1 + s % 2, 0:2 * N].rearrange("p (c n) -> p c n", c=2),
                                        AX_X, ALU.max).then_inc(max_ready, 1)
                    if s == 0 and i3.live:
                        dve.wait_ge(v_done, i3.n + 1)
                        wait(dve, pv_done, H * (i3.n - 3))
                        v.tensor_tensor(vaug[:, i3.ring, :, :, 0:HD], ps[0:HALF, PROJ, 0:2 * D].rearrange(
                            "p (c h d) -> p c h d", c=2, h=H), vb_s[:].rearrange("p c (h d) -> p c h d", h=H),
                            ALU.add).then_inc(v_ready, 1)
                    if s == 2 and i7.live:
                        dve.wait_ge(top_i_ready, 2 * (i7.n + 1))
                        v.tensor_copy(top_f[:], top_i[:, :, 0:2]).then_inc(top_f_ready, 1)
                    if s == 6 and i0.live:
                        wait(dve, shift_ready, i0.n)
                        norm_aggr(i0, it, (stats_ready, mv_ready), stats, mv)
                    if s == 7 and i7.live:
                        dve.wait_ge(pos_f_ready, 4 * (i7.n + 1))
                        wait(dve, rows_sent[i7.ring], 64 * i7.turn)
                        v.tensor_copy(pos_i[:, i7.ring], pos[:]).then_inc(pos_ready, 1)

            slots(dve, slot)

            steps = [0]

            def step(ins):
                steps[0] += 1
                ins.then_inc(plan_step, 1)
                dve.wait_ge(plan_step, steps[0])

            fin = base[0:1, NB % RING, 0]
            dve.wait_ge(base_ready, NB + 1)
            v.tensor_copy(fill_i[:], fin).then_inc(ends_ready, 1)
            count, rounded, ends, ones = (plan[:, i] for i in range(4))
            step(v.tensor_tensor(count, fin, region_row[0:1], ALU.subtract))
            step(v.tensor_scalar(count, count, float(CH - 1), None, ALU.add))
            step(v.tensor_copy(count_i[:], count))
            step(v.tensor_scalar(count_i[:], count_i[:], 8, 8, ALU.logical_shift_right, ALU.logical_shift_left))
            step(v.tensor_copy(rounded, count_i[:]))
            step(v.memset(ones, 1.0))
            step(v.tensor_tensor_scan(ends, ones, rounded, 0.0, ALU.mult, ALU.add))
            expert, start, row, live_ = (plan_c[:, i] for i in range(4))
            every = lambda x_: x_.rearrange("p (o e) -> p o e", o=1).to_broadcast([1, NCH, NE])
            step(v.tensor_tensor(passed[:], chunk_row[:].rearrange("p (c o) -> p c o", o=1).to_broadcast(
                [1, NCH, NE]), every(ends), ALU.is_ge))
            step(v.tensor_reduce(expert, passed[:], AX_X, ALU.add))
            step(v.tensor_tensor(passed[:], passed[:], every(rounded), ALU.mult))
            step(v.tensor_reduce(start, passed[:], AX_X, ALU.add))
            step(v.tensor_scalar(live_, expert, float(NE), None, ALU.is_lt))
            step(v.tensor_tensor(row, chunk_row[:], start, ALU.subtract))
            step(v.tensor_tensor(row, row, live_, ALU.mult))
            step(v.scalar_tensor_tensor(row, expert, float(REGION), row, ALU.mult, ALU.add))
            step(v.tensor_scalar(expert, expert, float(NE - 1), None, ALU.min))
            step(v.tensor_copy(plan_i[:, 0], row))
            v.tensor_copy(plan_i[:, 1], expert).then_inc(plan_ready, 1)

            def gate_differences():
                dve.wait_ge(kept, 2 * NB)
                best = top_all[:, :, 0:1]
                v.tensor_tensor(logits_all[:], logits_all[:], best.to_broadcast([HALF, TILES, NE]),
                                ALU.subtract).then_inc(wt_step, 1)
                v.tensor_tensor(psum2[:, 0], top_all[:, :, 1], top_all[:, :, 0], ALU.subtract).then_inc(wt_step, 1)

            def gate_weights():
                dve.wait_ge(wt_exp, 2)
                v.tensor_reduce(psum2[:, 2], logits_all[:], AX_X, ALU.add).then_inc(wt_step, 1)
                dve.wait_ge(wt_step, 3)
                v.reciprocal(psum2[:, 1], psum2[:, 2]).then_inc(wt_step, 1)
                dve.wait_ge(wt_step, 4)
                v.tensor_tensor(psum2[:, 0], psum2[:, 0], psum2[:, 1], ALU.mult).then_inc(wt_step, 1)
                dve.wait_ge(wt_step, 5)
                v.tensor_tensor(psum2[:, 1], psum2[:, 0], psum2[:, 1], ALU.subtract).then_inc(wt_step, 1)
                dve.wait_ge(wt_exp, 3)
                v.tensor_scalar(psum2[:, 2], psum2[:, 1], 1.0, None, ALU.add).then_inc(wt_step, 1)
                dve.wait_ge(wt_step, 7)
                v.reciprocal(wt[:, :, 0], psum2[:, 2]).then_inc(wt_step, 1)
                dve.wait_ge(wt_step, 8)
                v.tensor_tensor(wt[:, :, 1], psum2[:, 1], wt[:, :, 0], ALU.mult).then_inc(wt_step, 1)

            def turned(c0, it):
                c, ring, turn = BR * it + c0, c0 % BR, it + c0 // BR
                dve.wait_ge(xg_T, c + 1)
                wait(dve, hid_done, c - 2)
                v.tensor_copy(xg_cols[:, c0 % 3], ps[:, ROWS, 0:CH]).then_inc(xg_ready, 1)
                wait(dve, y_sent[ring], 32 * turn)
                v.tensor_copy(dest[:, ring], xg[:, ring, :, D].bitcast(U32)).then_inc(dest_kept, 1)

            def biased(c0, it):
                c, r3, ring = BR * it + c0, c0 % 3, c0 % BR
                dve.wait_ge(y_done, c + 1)
                b2 = b2ring[:, ring:ring + 1, :].to_broadcast([P, 2, D])
                v.tensor_tensor(ys[:, ring], ps[:, YBANKS[r3], 0:2 * D].rearrange("p (s d) -> p s d", s=2), b2,
                                ALU.add).then_inc(y_ready, 1)

            def both(c0, it):
                if not isinstance(it, int) or c0 + 2 < NCH:
                    turned(c0 + 2, it)
                biased(c0, it)
                if isinstance(it, int) and c0 == 0:
                    gate_differences()

            turned(0, 0)
            turned(1, 0)
            chunks(dve, 2, both)
            gate_weights()

            def group(g, r, turn):
                dve.wait_ge(yin_loaded[r], 32 * (turn + 1))
                wait(dve, out_stored[r], 16 * turn)
                for j in range(OG):
                    i = OG * g + j
                    v.scalar_tensor_tensor(res[:, r, j], yin[:, r, 0, j],
                                           wt[:, bass.ds(i, 1), 0:1].rearrange("p o k -> p (o k)"),
                                           h_all[:, bass.ds(i, 1), :].rearrange("p o d -> p (o d)"),
                                           ALU.mult, ALU.add).then_inc(res_mid, 1)
                dve.wait_ge(res_mid, OG * (g + 1))
                dve.wait_ge(yin_scaled, OG * (g + 1))
                v.tensor_tensor(res[:, r], res[:, r], yin[:, r, 1], ALU.add).then_inc(res_ready, 1)

            dve.wait_ge(wt_step, 9)
            for r in range(CR):
                group(r, r, 0)
            with dve.Fori(1, TILES // OG // CR) as it:
                for r in range(CR):
                    group(CR * it + r, r, it)

        @block.tensor
        def _(pe):
            mm, tr = nc.tensor.matmul, nc.tensor.transpose

            def edge_turn():
                pe.wait_ge(xncols_ready, 2)
                pe.wait_ge(edge_T, 1)
                for c in range(2):
                    last_ = tr(ps[0:HALF, TURNED, c * P:(c + 1) * P], edge_last[:, c * HALF:(c + 1) * HALF], ident[:])
                last_.then_inc(edge_T, 1)
                pe.wait_ge(edge_max, 12)
                for c in range(2):
                    last_ = tr(ps[0:H, TURNED, c * HALF:(c + 1) * HALF], eb[:, c], ident[0:HALF, 0:HALF])
                last_.then_inc(bias_T, 1)
                pe.wait_ge(bias_done, 2)

            def embed(img, part):
                if part == 0:
                    pe.wait_ge(x_loaded[img.ring2], 16 * (img.turn2 + 1))
                for k in range(part * NK // 3, (part + 1) * NK // 3):
                    last_ = mm(ps[:, ROWS, 0:N], wtok_s[:, k], patches[:, img.ring2, k], start=(k == 0),
                               stop=(k == NK - 1))
                if part == 2:
                    last_.then_inc(embed_done, 1)

            def slot(t, it):
                ahead, i0, i1, i2, i3, i4, i5, i6, i7, i8 = (Image(t, it, lag, NB) for lag in range(-1, 9))

                def row_scores(s):
                    img, h = (i2, s - 2) if s >= 2 else (i3, s + 6)
                    if img.live:
                        wait(pe, max_ready, H * img.n + h - 1)
                        if s == 2 and i7.live:
                            pe.wait_ge(logits_ready, i7.n + 1)
                        if s == 6 and i7.live:
                            pe.wait_ge(place_ready, 2 * (i7.n + 1))
                            pe.wait_ge(base_ready, i7.n + 2)
                    elif s in (0, 4) and i7.live:
                        pe.wait_ge(max_ready, H * NB)
                    if s == 0 and i7.live:
                        pe.wait_ge(gate_h_ready, i7.n + 1)
                        if not img.live:
                            freed(pe, (i8, base_ready, i8.n + 2))
                            freed(pe, (i8, place_ready, 2 * (i8.n + 1)))
                        for c in range(2):
                            last_ = mm(ps[0:HALF, S1, 2 * N + c * NE:2 * N + (c + 1) * NE],
                                       gate_h[:, c * HALF:(c + 1) * HALF], gw2_s[:], start=True, stop=True)
                        last_.then_inc(gate2_done, 1)
                    if s == 4 and i7.live:
                        pe.wait_ge(hot_ready, 2 * (i7.n + 1))
                        for a in range(2):
                            last_ = mm(ps[0:HALF, S1, 2 * N + 2 * NE * a:2 * N + 2 * NE * (a + 1)], lower[:, a],
                                       hot[:].rearrange("p c e -> p (c e)"), start=True, stop=True)
                        last_.then_inc(rank_done, 1)
                    if img.live:
                        if h == 0:
                            pe.wait_ge(sides_in[img.ring], 64 * (img.turn + 1))
                            if isinstance(img.n, int) and img.n < RING:
                                pe.wait_ge(bias_in[img.ring], 32)
                        for c in range(2):
                            last_ = mm(ps[0:HALF, S1 + s % 2, c * N:(c + 1) * N],
                                       qside[0:ROW_MAX, img.ring, h, c * HALF:(c + 1) * HALF],
                                       kside[0:ROW_MAX, img.ring, h, :], start=True, stop=True)
                        last_.then_inc(s1_done, 1)

                if t == 0:
                    pe.wait_ge(c_embed, 48)
                    embed(i0, 0)
                if t == 1:
                    pe.wait_ge(c_qkv, 32)
                if t == 5:
                    pe.wait_ge(c_misc, 144)
                for s in range(H):
                    if s == 1 and i5.live:
                        pe.wait_ge(sums_ready, i5.n + 1)
                        freed(pe, (i3, v_ready, i3.n + 1), (i6, att_ready, 2 * (i6.n + 1)))
                        for c in range(2):
                            for g in range(2):
                                last_ = tr(ps[0:HALF, PROJ, (2 * c + g) * P:(2 * c + g + 1) * P],
                                           sums[:, g, c * HALF:(c + 1) * HALF], ident[:])
                        last_.then_inc(sums_T, 1)
                    if s == 2 and t == 2:
                        edge_turn()
                    row_scores(s)
                    img, h = (i3, 0) if s == 7 else (i4, s + 1)
                    if img.live:
                        if h == 0:
                            pe.wait_ge(max_in[img.ring], 32 * (img.turn + 1))
                        wait(pe, probs_ready, H * img.n + h - 1)
                        for c in range(2):
                            last_ = mm(ps[0:HALF, S2 + h % 2, c * N:(c + 1) * N],
                                       kside[0:ROW_END, img.ring, h, c * HALF:(c + 1) * HALF],
                                       qside[0:ROW_END, img.ring, h, :], start=True, stop=True)
                        last_.then_inc(s2_done, 1)
                    if s == 1 and i1.live:
                        pe.wait_ge(xn_ready, 2 * (i1.n + 1))
                        freed(pe, (i6, h2_ready, i6.n + 1), (i2, xncols_ready, i2.n + 1))
                        for c in range(2):
                            last_ = tr(ps[:, TURNED, c * HALF:(c + 1) * HALF], xn[:, c], ident[0:HALF, 0:HALF])
                        last_.then_inc(xncols_done, 1)
                    if s in (0, 1) and i0.live:
                        embed(i0, s + 1)
                    if s == 3 and i1.live:
                        pe.wait_ge(xncols_ready, i1.n + 1)
                        freed(pe, (i5, att_ready, 2 * (i5.n + 1)), (i3, v_ready, i3.n + 1),
                              (i2, low_ready, 2 * (i2.n + 1)))
                        for a in range(2):
                            last_ = mm(ps[:, PROJ, a * N:(a + 1) * N], wqkv_s[:, a], xncols[:, i1.ring2], start=True,
                                       stop=True)
                        last_.then_inc(qk_done, 1)
                    if s == 5 and i5.live:
                        pe.wait_ge(att_cols_ready, i5.n + 1)
                        for c in range(2):
                            last_ = mm(ps[0:HALF, TURNED, c * D:(c + 1) * D], att_cols[:, c * HALF:(c + 1) * HALF],
                                       wo_s[:], start=True, stop=True)
                        last_.then_inc(o_done, 1)
                    if s == 6 and i6.live:
                        pe.wait_ge(xs_cols_ready, i6.n + 1)
                        freed(pe, (i0, h_ready, i0.n + 1), (i3, max_low, i3.n + 1), (i7, gate_h_ready, i7.n + 1))
                        mm(ps[:, ROWS, 0:N], gw1_s[:], xs_cols[:], start=True, stop=True).then_inc(gate1_done, 1)
                    if s == 6 and i2.live:
                        freed(pe, (i1, low_ready, 2 * (i1.n + 1)), (i5, att_ready, 2 * (i5.n + 1)))
                        for c in range(2):
                            last_ = mm(ps[0:HALF, PROJ, c * D:(c + 1) * D],
                                       xncols[:, i2.ring2, c * HALF:(c + 1) * HALF], wqkv_s[:, 2], start=True, stop=True)
                        last_.then_inc(v_done, 1)
                    if i4.live:
                        g, j = s // 4, s % 4
                        pe.wait_ge(probs_ready, H * i4.n + s + 1)
                        if s == 0:
                            pe.wait_ge(v_ready, i4.n + 1)
                            wait(pe, sums_ready, i4.n)
                        for c in range(2):
                            last_ = mm(ps[2 * HD * j:2 * HD * (j + 1), PV, g * N:(g + 1) * N], vaug[:, i4.ring, c, s],
                                       probs[:, s % 4, c], start=(c == 0), stop=(c == 1))
                        last_.then_inc(pv_done, 1)
                    if s == 7 and ahead.live:
                        freed(pe, (i6, gate_h_ready, i6.n + 1), (i0, h_ready, i0.n + 1))
                        embed(ahead, 0)
                    if s == 2 and i6.live:
                        pe.wait_ge(xs_ready, 2 * (i6.n + 1))
                        freed(pe, (i1, xncols_ready, i1.n + 1))
                        for c in range(2):
                            last_ = tr(ps[:, TURNED, c * HALF:(c + 1) * HALF], xs[:, i6.ring, c, 0, 0:D],
                                       ident[0:HALF, 0:HALF])
                        last_.then_inc(xs_T, 1)
                    if s == 2 and i3.live:
                        pe.wait_ge(max_ready, H * (i3.n + 1))
                        freed(pe, (i0, hcols_ready, i0.n + 1), (i7, gate_h_ready, i7.n + 1))
                        for c in range(2):
                            last_ = tr(ps[0:H, ROWS, c * HALF:(c + 1) * HALF], rowmax[:, i3.ring, c],
                                       ident[0:HALF, 0:HALF])
                        last_.then_inc(max_T, 1)
                    if s == 3 and i5.live:
                        pe.wait_ge(att_ready, 2 * (i5.n + 1))
                        freed(pe, (i6, xs_cols_ready, i6.n + 1), (i1, xncols_ready, i1.n + 1))
                        for c in range(2):
                            last_ = tr(ps[:, TURNED, c * HALF:(c + 1) * HALF], att[:, c].rearrange("p h d -> p (h d)"),
                                       ident[0:HALF, 0:HALF])
                        last_.then_inc(att_T, 1)
                    if s == 4 and i0.live:
                        pe.wait_ge(hcols_ready, i0.n + 1)
                        freed(pe, (i3, max_low, i3.n + 1))
                        for c in range(2):
                            last_ = tr(ps[0:HALF, ROWS, c * D:(c + 1) * D], hcols[:, c * HALF:(c + 1) * HALF], ident[:])
                        last_.then_inc(hrows_done, 1)

            slots(pe, slot)

            def turn_x(c0, it):
                c, ring, turn = BR * it + c0, c0 % BR, it + c0 // BR
                pe.wait_ge(xg_loaded[ring], 16 * (turn + 1))
                wait(pe, xg_ready, c)
                for s in range(2):
                    last_ = tr(ps[:, ROWS, s * P:(s + 1) * P], xg[:, ring, s, 0:D], ident[:])
                last_.then_inc(xg_T, 1)

            def hidden(c0, it):
                c, r3, ring, turn = BR * it + c0, c0 % 3, c0 % BR, it + c0 // BR
                pe.wait_ge(xg_ready, c + 1)
                pe.wait_ge(w_loaded[ring], 32 * (turn + 1))
                wait(pe, hid_ready, 2 * (c - 2))
                for j in range(2):
                    last_ = mm(ps[:, HBANKS[r3], j * CH:(j + 1) * CH], wring[:, ring, j * P:(j + 1) * P],
                               xg_cols[:, r3], start=True, stop=True)
                last_.then_inc(hid_done, 1)

            def outputs(c0, it):
                c, r3, ring = BR * it + c0, c0 % 3, c0 % BR
                pe.wait_ge(hid_ready, 2 * (c + 1))
                wait(pe, y_ready, c - 2)
                for s in range(2):
                    for j in range(2):
                        last_ = mm(ps[:, YBANKS[r3], s * D:(s + 1) * D], hid[:, r3, j, s * P:(s + 1) * P],
                                   wring[:, ring, HID + j * D:HID + (j + 1) * D], start=(j == 0), stop=(j == 1))
                last_.then_inc(y_done, 1)

            def all_three(c0, it):
                if not isinstance(it, int) or c0 + 2 < NCH:
                    turn_x(c0 + 2, it)
                if not isinstance(it, int) or c0 + 1 < NCH:
                    hidden(c0 + 1, it)
                outputs(c0, it)

            turn_x(0, 0)
            turn_x(1, 0)
            hidden(0, 0)
            chunks(pe, 2, all_three)


def kernel(**inputs):
    import numpy as np
    import concourse.bacc as bacc
    from concourse.bass_utils import run_bass_kernel_spmd as run

    a = {k: np.asarray(v) for k, v in inputs.items()}
    nb, ch, hh, ww = a["x"].shape
    hp, wp = hh // PATCH, ww // PATCH
    k = ch * PATCH * PATCH
    nk = k // P
    f32 = np.float32

    x = a["x"].reshape(nb, ch, hp, PATCH, wp, PATCH).transpose(0, 1, 3, 5, 2, 4).reshape(nb, nk, P, hp * wp)
    x = x.transpose(0, 2, 1, 3)
    wtok = a["L0_tok_w"].T.reshape(nk, P, D).transpose(1, 0, 2)
    by_feature = lambda w: np.moveaxis(w.reshape((H, HD) + w.shape[1:]), 0, 1).reshape(w.shape)
    wqkv = np.stack([by_feature(a["L0_attn_q_w"]).T, by_feature(a["L0_attn_k_w"]).T, a["L0_attn_v_w"].T], axis=1)
    gh = a["L0_ffn_gw1"].shape[1]
    gw1 = np.zeros((D, P), f32)
    gw1[:, 0:gh] = a["L0_ffn_gw1"]
    gw2 = np.zeros((P, NE), f32)
    gw2[0:gh] = a["L0_ffn_gw2"]
    gb1 = np.zeros(P, f32)
    gb1[0:gh] = a["L0_ffn_gb1"]
    wexp = np.concatenate(
        [a["L0_ffn_we1"], a["L0_ffn_we2"].reshape(NE, 2, P, D).transpose(0, 2, 1, 3).reshape(NE, P, 2 * D),
         a["L0_ffn_be1"].reshape(NE, 2, P).transpose(0, 2, 1)], axis=2)
    cols = np.stack([a["L0_tok_b"], by_feature(a["L0_attn_q_b"]), by_feature(a["L0_attn_k_b"]), gb1], axis=1)
    rows = np.concatenate([a["L0_attn_v_b"]] * 2 + [a["L0_ffn_gb2"]] * 2 + [a["L0_attn_o_b"]] * 2)[None]
    ne = a["L0_attn_edge_index"].shape[1]
    edges = a["L0_attn_edge_index"].reshape(2, P, ne // P).transpose(1, 0, 2)
    attr = np.zeros((ne, 4), f32)
    attr[:, 0:3] = a["L0_attn_edge_attr"]
    ebw = np.concatenate([a["L0_attn_eb_w"].T.reshape(-1), a["L0_attn_eb_b"]])[None]
    nt = nb * N
    region = nt + CH
    nch = (2 * nt + NE * (CH - 1)) // CH
    every = lambda r: np.broadcast_to(np.asarray(r, f32)[None], (P, len(r)))
    consts = np.concatenate(
        [np.eye(P, dtype=f32), every(range(NE)), every([e * region for e in range(NE)]), every(range(N)),
         (np.arange(P, dtype=f32) * (ne // P))[:, None], every([CH * c for c in range(nch)])], axis=1)
    import ml_dtypes
    earlier = np.triu(np.ones((HALF, HALF)), 1)
    tri = np.stack([earlier, np.ones((HALF, HALF))], axis=1).astype(ml_dtypes.bfloat16)
    tokens = np.array([[i * N + c * HALF + p + kk * nt for i in range(RING) for c in range(2) for kk in range(2)]
                       for p in range(HALF)], np.uint32)

    nc = bacc.Bacc("TRN2", target_bir_lowering=False, num_devices=1)
    arrays, args = {}, []
    for name, v in (("x", x), ("wtok", wtok), ("wqkv", wqkv), ("wo", a["L0_attn_o_w"].T), ("gw1", gw1), ("gw2", gw2),
                    ("wexp", wexp), ("be2", a["L0_ffn_be2"]), ("cols", cols), ("rows", rows), ("edges", edges),
                    ("attr", attr), ("ebw", ebw), ("consts", consts), ("tri", tri), ("tokens", tokens)):
        v = np.ascontiguousarray(v)
        arrays[name + "_in"] = v
        args.append(nc.dram_tensor(name + "_in", v.shape, mybir.dt.from_np(v.dtype), kind="ExternalInput").ap())
    out = nc.dram_tensor("h_out", (nb, N, D), F32, kind="ExternalOutput").ap()
    vit_block(nc, *args, out)
    r = run(nc, [arrays], core_ids=[0])
    return r.results[0]["h_out"]
```
